# Optimizing a Trainium2 kernel written in Bass

```python
import numpy as np
import jax
import jax.numpy as jnp

def _softmax(x, axis=-1):
    return jax.nn.softmax(x, axis=axis)

def _gelu(x):
    return jax.nn.gelu(x, approximate=True)

def _silu(x):
    return jax.nn.silu(x)

def _sigmoid(x):
    return jax.nn.sigmoid(x)

def _layernorm(x, axis=-1, eps=1e-05):
    m = jnp.mean(x, axis=axis, keepdims=True)
    v = jnp.var(x, axis=axis, keepdims=True)
    return (x - m) / jnp.sqrt(v + eps)

def _scatter_add(tgt, idx, src, axis=0):
    return tgt.at[idx].add(src)

def _segment_sum(src, seg, n):
    return jax.ops.segment_sum(src, seg, n)
kernel_name = 'mk_hybrid_d1_jaxref_r8_083d00'

def setup_inputs(seed: int=0):
    np.random.seed(seed)
    _w = jnp.asarray

    def _L0_attn_a_setup():
        import jax, jax.numpy as jnp
        import numpy as np
        B, S, E, H, ML = (4, 128, 128, 16, 256)
        HD = E // H

        def _layernorm(x, g, b, eps=1e-05):
            m = x.mean(-1, keepdims=True)
            v = ((x - m) ** 2).mean(-1, keepdims=True)
            return (x - m) * jax.lax.rsqrt(v + eps) * g + b

        def _causal_mask(size, rel_pos):
            flipped = jnp.flip(rel_pos[:, :size], -1)
            neg_inf = jnp.full((rel_pos.shape[0], size), -jnp.inf, rel_pos.dtype)
            padded = jnp.concatenate([flipped, neg_inf], axis=-1)
            idx = jnp.arange(size)[None, :] - jnp.arange(size)[:, None] + size - 1
            return padded[:, idx]
        key = jax.random.key(seed)
        ks = jax.random.split(key, 8)
        s = 0.02
        return {'x': jax.random.normal(ks[0], (B, S, E), dtype=jnp.float32), 'rel_pos': jax.random.normal(ks[1], (H, ML), dtype=jnp.float32), 'in_proj_w': jax.random.normal(ks[2], (3 * E, E), dtype=jnp.float32) * s, 'in_proj_b': jnp.zeros((3 * E,), jnp.float32), 'out_w': jax.random.normal(ks[3], (E, E), dtype=jnp.float32) * s, 'out_b': jnp.zeros((E,), jnp.float32), 'w1': jax.random.normal(ks[4], (4 * E, E), dtype=jnp.float32) * s, 'b1': jnp.zeros((4 * E,), jnp.float32), 'w2': jax.random.normal(ks[5], (E, 4 * E), dtype=jnp.float32) * s, 'b2': jnp.zeros((E,), jnp.float32), 'ln1_g': jnp.ones((E,), jnp.float32), 'ln1_b': jnp.zeros((E,), jnp.float32), 'ln2_g': jnp.ones((E,), jnp.float32), 'ln2_b': jnp.zeros((E,), jnp.float32)}
    _L0_attn_a_in = _L0_attn_a_setup()

    def _L0_attn_b_setup():
        import jax, jax.numpy as jnp
        import numpy as np
        B, T, D, H = (8, 512, 128, 128)
        LN_EPS = 1e-05

        def _log_g(a):
            return jnp.where(a >= 0, jnp.log(jax.nn.relu(a) + 0.5), -jax.nn.softplus(-a))

        def _reference_tuple_inner(x, Wz, bz, Wh, bh, gamma, beta):
            k = jnp.einsum('btd,dh->bth', x, Wz) + bz
            log_coeffs = -jax.nn.softplus(k)
            log_z = -jax.nn.softplus(-k)
            log_tilde_h = _log_g(jnp.einsum('btd,dh->bth', x, Wh) + bh)
            log_values = log_z + log_tilde_h
            a_star = jnp.cumsum(log_coeffs, axis=1)
            log_h = a_star + jax.lax.cumlogsumexp(log_values - a_star, axis=1)
            h = jnp.exp(log_h)
            mean = jnp.mean(h, axis=-1, keepdims=True)
            var = jnp.mean(jnp.square(h - mean), axis=-1, keepdims=True)
            out = (h - mean) * jax.lax.rsqrt(var + LN_EPS) * gamma + beta
            out = out + x
            hidden = h[:, -1]
            return (out, hidden)
        key = jax.random.key(seed)
        ks = jax.random.split(key, 3)
        x = jax.random.normal(ks[0], (B, T, D), dtype=jnp.float32)
        Wz = jax.random.normal(ks[1], (D, H), dtype=jnp.float32) / np.sqrt(D)
        Wh = jax.random.normal(ks[2], (D, H), dtype=jnp.float32) / np.sqrt(D)
        bz = jnp.zeros((H,), dtype=jnp.float32)
        bh = jnp.zeros((H,), dtype=jnp.float32)
        gamma = jnp.ones((H,), dtype=jnp.float32)
        beta = jnp.zeros((H,), dtype=jnp.float32)
        return {'x': x, 'Wz': Wz, 'bz': bz, 'Wh': Wh, 'bh': bh, 'gamma': gamma, 'beta': beta}
    _L0_attn_b_in = _L0_attn_b_setup()

    def _L0_ffn_setup():
        import jax, jax.numpy as jnp
        import numpy as np
        D_MODEL, D_FF, N_EXPERTS, TOP_K = (128, 256, 8, 2)
        B, S = (2, 256)
        key = jax.random.key(seed)
        ks = jax.random.split(key, 6)
        sd = 1.0 / np.sqrt(D_MODEL)
        sf = 1.0 / np.sqrt(D_FF)
        return {'x': jax.random.normal(ks[0], (B, S, D_MODEL), jnp.float32), 'router_w': jax.random.normal(ks[1], (N_EXPERTS, D_MODEL), jnp.float32) * sd, 'gate_w': jax.random.normal(ks[2], (N_EXPERTS, D_MODEL, D_FF), jnp.float32) * sd, 'gate_b': jnp.zeros((N_EXPERTS, D_FF), jnp.float32), 'up_w': jax.random.normal(ks[3], (N_EXPERTS, D_MODEL, D_FF), jnp.float32) * sd, 'up_b': jnp.zeros((N_EXPERTS, D_FF), jnp.float32), 'down_w': jax.random.normal(ks[4], (N_EXPERTS, D_FF, D_MODEL), jnp.float32) * sf, 'down_b': jnp.zeros((N_EXPERTS, D_MODEL), jnp.float32)}
    _L0_ffn_in = _L0_ffn_setup()
    _d = {'L0_attn_a_x': _L0_attn_a_in['x'], 'L0_attn_a_rel_pos': _L0_attn_a_in['rel_pos'], 'L0_attn_a_in_proj_w': _L0_attn_a_in['in_proj_w'], 'L0_attn_a_in_proj_b': _L0_attn_a_in['in_proj_b'], 'L0_attn_a_out_w': _L0_attn_a_in['out_w'], 'L0_attn_a_out_b': _L0_attn_a_in['out_b'], 'L0_attn_a_w1': _L0_attn_a_in['w1'], 'L0_attn_a_b1': _L0_attn_a_in['b1'], 'L0_attn_a_w2': _L0_attn_a_in['w2'], 'L0_attn_a_b2': _L0_attn_a_in['b2'], 'L0_attn_a_ln1_g': _L0_attn_a_in['ln1_g'], 'L0_attn_a_ln1_b': _L0_attn_a_in['ln1_b'], 'L0_attn_a_ln2_g': _L0_attn_a_in['ln2_g'], 'L0_attn_a_ln2_b': _L0_attn_a_in['ln2_b'], 'L0_attn_b_Wz': _L0_attn_b_in['Wz'], 'L0_attn_b_bz': _L0_attn_b_in['bz'], 'L0_attn_b_Wh': _L0_attn_b_in['Wh'], 'L0_attn_b_bh': _L0_attn_b_in['bh'], 'L0_attn_b_gamma': _L0_attn_b_in['gamma'], 'L0_attn_b_beta': _L0_attn_b_in['beta'], 'L0_ffn_router_w': _L0_ffn_in['router_w'], 'L0_ffn_gate_w': _L0_ffn_in['gate_w'], 'L0_ffn_gate_b': _L0_ffn_in['gate_b'], 'L0_ffn_up_w': _L0_ffn_in['up_w'], 'L0_ffn_up_b': _L0_ffn_in['up_b'], 'L0_ffn_down_w': _L0_ffn_in['down_w'], 'L0_ffn_down_b': _L0_ffn_in['down_b']}
    _x0 = _d['L0_attn_a_x']
    _d['L0_attn_a_x'] = jax.random.normal(jax.random.fold_in(jax.random.key(seed), 1), (32, 256, 128), dtype=_x0.dtype)
    del _x0
    return _d

def reference(L0_attn_a_x, L0_attn_a_rel_pos, L0_attn_a_in_proj_w, L0_attn_a_in_proj_b, L0_attn_a_out_w, L0_attn_a_out_b, L0_attn_a_w1, L0_attn_a_b1, L0_attn_a_w2, L0_attn_a_b2, L0_attn_a_ln1_g, L0_attn_a_ln1_b, L0_attn_a_ln2_g, L0_attn_a_ln2_b, L0_attn_b_Wz, L0_attn_b_bz, L0_attn_b_Wh, L0_attn_b_bh, L0_attn_b_gamma, L0_attn_b_beta, L0_ffn_router_w, L0_ffn_gate_w, L0_ffn_gate_b, L0_ffn_up_w, L0_ffn_up_b, L0_ffn_down_w, L0_ffn_down_b):

    def _L0_attn_a_ref(x, rel_pos, in_proj_w, in_proj_b, out_w, out_b, w1, b1, w2, b2, ln1_g, ln1_b, ln2_g, ln2_b):
        import jax, jax.numpy as jnp
        import numpy as np
        B, S, E, H, ML = (4, 128, 128, 16, 256)
        HD = E // H

        def _layernorm(x, g, b, eps=1e-05):
            m = x.mean(-1, keepdims=True)
            v = ((x - m) ** 2).mean(-1, keepdims=True)
            return (x - m) * jax.lax.rsqrt(v + eps) * g + b

        def _causal_mask(size, rel_pos):
            flipped = jnp.flip(rel_pos[:, :size], -1)
            neg_inf = jnp.full((rel_pos.shape[0], size), -jnp.inf, rel_pos.dtype)
            padded = jnp.concatenate([flipped, neg_inf], axis=-1)
            idx = jnp.arange(size)[None, :] - jnp.arange(size)[:, None] + size - 1
            return padded[:, idx]
        b, s, e = x.shape
        xn = _layernorm(x, ln1_g, ln1_b)
        qkv = xn @ in_proj_w.T + in_proj_b
        q, k, v = jnp.split(qkv, 3, axis=-1)
        q = q.reshape(b, s, H, HD).transpose(0, 2, 1, 3)
        k = k.reshape(b, s, H, HD).transpose(0, 2, 1, 3)
        v = v.reshape(b, s, H, HD).transpose(0, 2, 1, 3)
        mask = _causal_mask(s, rel_pos)
        scores = jnp.einsum('bhqd,bhkd->bhqk', q, k) / np.sqrt(HD) + mask[None]
        attn = jax.nn.softmax(scores, axis=-1)
        o = jnp.einsum('bhqk,bhkd->bhqd', attn, v)
        o = o.transpose(0, 2, 1, 3).reshape(b, s, e)
        att_out = o @ out_w.T + out_b
        x = x + att_out
        xm = _layernorm(x, ln2_g, ln2_b)
        mlp = jax.nn.relu(xm @ w1.T + b1) @ w2.T + b2
        return x + mlp

    def _L0_attn_b_ref(x, Wz, bz, Wh, bh, gamma, beta):
        import jax, jax.numpy as jnp
        import numpy as np
        B, T, D, H = (8, 512, 128, 128)
        LN_EPS = 1e-05

        def _log_g(a):
            return jnp.where(a >= 0, jnp.log(jax.nn.relu(a) + 0.5), -jax.nn.softplus(-a))

        def _reference_tuple_inner(x, Wz, bz, Wh, bh, gamma, beta):
            k = jnp.einsum('btd,dh->bth', x, Wz) + bz
            log_coeffs = -jax.nn.softplus(k)
            log_z = -jax.nn.softplus(-k)
            log_tilde_h = _log_g(jnp.einsum('btd,dh->bth', x, Wh) + bh)
            log_values = log_z + log_tilde_h
            a_star = jnp.cumsum(log_coeffs, axis=1)
            log_h = a_star + jax.lax.cumlogsumexp(log_values - a_star, axis=1)
            h = jnp.exp(log_h)
            mean = jnp.mean(h, axis=-1, keepdims=True)
            var = jnp.mean(jnp.square(h - mean), axis=-1, keepdims=True)
            out = (h - mean) * jax.lax.rsqrt(var + LN_EPS) * gamma + beta
            out = out + x
            hidden = h[:, -1]
            return (out, hidden)
        return _reference_tuple_inner(x, Wz, bz, Wh, bh, gamma, beta)[0]

    def _L0_ffn_ref(x, router_w, gate_w, gate_b, up_w, up_b, down_w, down_b):
        import jax, jax.numpy as jnp
        import numpy as np
        D_MODEL, D_FF, N_EXPERTS, TOP_K = (128, 256, 8, 2)
        B, S = (2, 256)
        b, s, d = x.shape
        xf = x.reshape(b * s, d)
        n = xf.shape[0]
        router_logits = xf @ router_w.T
        probs = jax.nn.softmax(router_logits, axis=-1)
        topv, topi = jax.lax.top_k(probs, TOP_K)
        mask = jnp.zeros_like(probs).at[jnp.arange(n)[:, None], topi].set(1.0)
        probs = probs * mask
        probs = probs / (probs.sum(axis=-1, keepdims=True) + 1e-09)
        g = jnp.einsum('nd,edf->nef', xf, gate_w) + gate_b
        u = jnp.einsum('nd,edf->nef', xf, up_w) + up_b
        h = jax.nn.silu(g) * u
        expert_out = jnp.einsum('nef,efd->ned', h, down_w) + down_b
        y = jnp.einsum('ne,ned->nd', probs, expert_out)
        return y.reshape(b, s, d)
    x = L0_attn_a_x
    x = x + _L0_attn_a_ref(_layernorm(x, axis=-1), L0_attn_a_rel_pos, L0_attn_a_in_proj_w, L0_attn_a_in_proj_b, L0_attn_a_out_w, L0_attn_a_out_b, L0_attn_a_w1, L0_attn_a_b1, L0_attn_a_w2, L0_attn_a_b2, L0_attn_a_ln1_g, L0_attn_a_ln1_b, L0_attn_a_ln2_g, L0_attn_a_ln2_b)
    x = x + _L0_ffn_ref(_layernorm(x, axis=-1), L0_ffn_router_w, L0_ffn_gate_w, L0_ffn_gate_b, L0_ffn_up_w, L0_ffn_up_b, L0_ffn_down_w, L0_ffn_down_b)
    x = x + _L0_attn_b_ref(_layernorm(x, axis=-1), L0_attn_b_Wz, L0_attn_b_bz, L0_attn_b_Wh, L0_attn_b_bh, L0_attn_b_gamma, L0_attn_b_beta)
    x = x + _L0_ffn_ref(_layernorm(x, axis=-1), L0_ffn_router_w, L0_ffn_gate_w, L0_ffn_gate_b, L0_ffn_up_w, L0_ffn_up_b, L0_ffn_down_w, L0_ffn_down_b)
    return x

_drawn_inputs = setup_inputs


def setup_inputs(seed=0):
    import zlib

    import numpy as np

    out = dict(_drawn_inputs(seed))
    spreads = {'L0_attn_a_in_proj_b': (0.0, 0.351),
     'L0_attn_a_out_b': (0.0, 0.1),
     'L0_attn_a_b1': (0.0, 0.1),
     'L0_attn_a_b2': (0.0, 0.1),
     'L0_attn_a_ln1_g': (1.0, 0.6),
     'L0_attn_a_ln1_b': (0.0, 0.67),
     'L0_attn_a_ln2_g': (1.0, 0.6),
     'L0_attn_a_ln2_b': (0.0, 0.574),
     'L0_attn_b_bz': (0.0, 0.438),
     'L0_attn_b_bh': (0.0, 0.1),
     'L0_attn_b_gamma': (1.0, 0.2),
     'L0_attn_b_beta': (0.0, 0.1),
     'L0_ffn_gate_b': (0.0, 0.1),
     'L0_ffn_up_b': (0.0, 0.1),
     'L0_ffn_down_b': (0.0, 0.1)}
    factors = {'L0_attn_a_rel_pos': 4.726, 'L0_attn_a_in_proj_w': 3.751}
    for name, (base, spread) in spreads.items():
        noise = np.random.default_rng([zlib.crc32(name.encode()), seed]).standard_normal(out[name].shape)
        drawn = base * np.exp(spread * noise) if base else spread * noise
        out[name] = jnp.asarray(drawn.astype(out[name].dtype))
    for name, factor in factors.items():
        out[name] = (out[name] * factor).astype(out[name].dtype)
    return out
```

```python
import concourse.bass as bass
from concourse import mybir
from contextlib import ExitStack

F32 = mybir.dt.float32
F32R = mybir.dt.float32r
BF16 = mybir.dt.bfloat16
F16 = mybir.dt.float16
I32 = mybir.dt.int32
ALU = mybir.AluOpType
ACT = mybir.ActivationFunctionType
AXX = mybir.AxisListType.X

P = 128
EPS = 1e-5
MASKED = -1.0e30


class Chain:

    def __init__(self, engine, semaphore):
        self.engine, self.semaphore, self.base, self.n = engine, semaphore, 0, 0

    def start(self, base):
        self.base, self.n = base, 0

    def mark(self, instruction):
        self.n += 1
        instruction.then_inc(self.semaphore, 1)
        return self.base + self.n

    def wait(self, value):
        self.engine.wait_ge(self.semaphore, value)

    def step(self, instruction):
        self.wait(self.mark(instruction))


def moments(nc, ch, stats, mom):
    ch.mark(nc.vector.tensor_tensor(mom[:, 0, :], stats[:, :, 1], stats[:, :, 4], ALU.add))
    ch.mark(nc.vector.tensor_tensor(mom[:, 1, :], stats[:, :, 1], stats[:, :, 4], ALU.subtract))
    ch.step(nc.vector.tensor_tensor(mom[:, 2, :], stats[:, :, 2], stats[:, :, 5], ALU.add))
    ch.mark(nc.vector.tensor_scalar(mom[:, 0, :], mom[:, 0, :], 0.5, None, ALU.mult))
    ch.step(nc.vector.tensor_tensor(mom[:, 1, :], mom[:, 1, :], mom[:, 1, :], ALU.mult))
    ch.step(nc.vector.scalar_tensor_tensor(mom[:, 3, :], mom[:, 2, :], 4.0 / P, mom[:, 1, :], ALU.mult, ALU.add))


class Shapes:
    def __init__(self, x, rel_pos, w1, gate_w):
        self.B, self.S, self.E = x.shape
        self.H, self.ML = rel_pos.shape
        self.HD = self.E // self.H
        self.FF = w1.shape[0]
        self.NE, _, self.EF = gate_w.shape
        self.QT = self.S // P
        self.TILES = self.B * self.QT
        self.N = self.B * self.S


def build(nc, ins, out):
    s = Shapes(ins["L0_attn_a_x"], ins["L0_attn_a_rel_pos"], ins["L0_attn_a_w1"], ins["L0_ffn_gate_w"])
    assert s.E == P and s.QT == 2 and s.H == 16 and s.HD == 8 and s.NE == 8
    with ExitStack() as kept:
        xres = kept.enter_context(nc.sbuf_tensor("xres", [P, s.TILES, s.E], F32))
        ident = kept.enter_context(nc.sbuf_tensor("ident", [P, P], F32))
        identb = kept.enter_context(nc.sbuf_tensor("identb", [P, P], BF16))
        with ExitStack() as mem:
            attention(nc, mem, s, ins, xres, ident, identb)
        with ExitStack() as mem:
            experts = expert_weights(nc, mem, s, ins, ident)
            mixture(nc, s, 'first_', xres, ident, experts)
            recurrence(nc, s, ins, xres, ident)
            mixture(nc, s, 'second_', xres, ident, experts)
        store(nc, s, out, xres)


def store(nc, s, out, xres):
    with ExitStack() as ctx:
        stored = ctx.enter_context(nc.semaphore("stored"))
        with nc.Block() as block:
            @block.sync
            def _(sp):
                sp.dma_start(out.rearrange("b (t p) e -> p (b t) e", p=P), xres[:]).then_inc(stored, 16)
                sp.wait_ge(stored, 16)


def attention(nc, ctx, s, ins, xres, ident, identb):
    H, HD, FF, B = s.H, s.HD, s.FF, s.B
    AUG = 64
    PAIRS = H // 2
    KROWS, XROWS = 6 * HD, 6 * HD + 2
    VW = 3 * (HD + 1)
    BK = 3 * P

    def sb(name, shape, dt=F32):
        return ctx.enter_context(nc.sbuf_tensor(name, shape, dt))

    def sem(name):
        return ctx.enter_context(nc.semaphore(name))

    wqkv = sb("wqkv", [P, 3 * s.E])
    bqkv = sb("bqkv", [P, 3 * s.E])
    wo = sb("wo", [P, s.E])
    outb = sb("outb", [P, s.E])
    w1 = sb("w1", [P, FF])
    b1 = sb("b1", [P, FF // P])
    w2 = sb("w2", [P, FF // P, s.E])
    b2 = sb("b2", [P, s.E])
    bias32 = sb("bias32", [P, H, BK])
    biasb = sb("biasb", [P, H, 2 * P], BF16)
    neghalf = sb("neghalf", [P, 4])
    unit = sb("unit", [P, 2, s.E])
    aug = sb("aug", [P, 2, 2, H, AUG], BF16)
    vaug = sb("vaug", [P, 2, H, 3, HD + 1], BF16)

    x_dram = ins["L0_attn_a_x"].rearrange("b (t p) e -> p (b t) e", p=P)

    with ExitStack() as c2:
        def sb2(name, shape, dt=F32):
            return c2.enter_context(nc.sbuf_tensor(name, shape, dt))

        def sem2(name):
            return c2.enter_context(nc.semaphore(name))

        wrow = sb2("wrow", [P, 8, s.E])
        w2row = sb2("w2row", [P, FF])
        gcol = sb2("gcol", [P, 4])
        b1ld = sb2("b1ld", [P, FF // P])
        inb = sb2("inb", [P, 3 * s.E])
        ones = sb2("ones", [P, P])
        lnb1 = sb2("lnb1", [P, P])
        anti = sb2("anti", [P, P])
        relpad = sb2("relpad", [H, 3 * P])
        hank = sb2("hank", [P, H, 2 * P])
        pw = [c2.enter_context(nc.psum_tensor(f"pw{i}", [P, 512], F32)) for i in range(4)]
        scratch = nc.dram_tensor("rel_padded", (H, 3 * P), F32, kind="Internal").ap()
        hankel = bass.AP(tensor=scratch.tensor, offset=0, ap=[[1, P], [3 * P, H], [1, 2 * P]])

        loaded = sem2("weights_loaded")
        rel_in, rel_out, rel_tab = sem2("rel_loaded"), sem2("rel_stored"), sem2("hankel_loaded")
        x_in = sem2("x_loaded")
        filled, full, taken = sem2("filled"), sem2("pw_full"), sem2("pw_taken")
        padded = sem2("rel_padded_set")
        vchain = sem2("vector_steps")
        gchain = sem2("gpsimd_steps")
        NLOADS = 14

        def col(name):
            return ins[name].rearrange("(p a) -> p a", a=1)

        def row(name):
            t = ins[name]
            return bass.AP(tensor=t.tensor, offset=t.offset, ap=[[0, P], [1, t.shape[0]]])

        with nc.Block() as block:
            @block.sync
            def _(sp):
                sp.wait_ge(padded, 1)
                sp.dma_start(relpad[:, P - 1:P - 1 + s.S], ins["L0_attn_a_rel_pos"][:, 0:s.S]).then_inc(rel_in, 16)
                sp.wait_ge(rel_in, 16)
                sp.dma_start(scratch, relpad[:]).then_inc(rel_out, 16)
                sp.wait_ge(rel_out, 16)
                sp.dma_start(hank[:], hankel).then_inc(rel_tab, 16)
                for q in range(4):
                    n = s.TILES // 4
                    sp.dma_start(xres[:, q * n:(q + 1) * n, :], x_dram[:, q * n:(q + 1) * n, :]).then_inc(x_in, 16)
                sp.wait_ge(x_in, 64)
                sp.wait_ge(rel_tab, 16)

            @block.scalar
            def _(act):
                loads = [
                    (wrow[:, 0:3, :], ins["L0_attn_a_in_proj_w"].rearrange("(c p) e -> p c e", p=P)),
                    (wrow[:, 3, :], ins["L0_attn_a_out_w"]),
                    (wrow[:, 4:8, :], ins["L0_attn_a_w1"].rearrange("(c p) e -> p c e", p=P)),
                    (w2row[:], ins["L0_attn_a_w2"]),
                    (gcol[:, 0:1], col("L0_attn_a_ln1_g")), (gcol[:, 1:2], col("L0_attn_a_ln1_b")),
                    (gcol[:, 2:3], col("L0_attn_a_ln2_g")), (gcol[:, 3:4], col("L0_attn_a_ln2_b")),
                    (inb[:], row("L0_attn_a_in_proj_b")), (outb[:], row("L0_attn_a_out_b")),
                    (b2[:], row("L0_attn_a_b2")),
                ] + [(b1ld[:, c:c + 1], ins["L0_attn_a_b1"][c * P:(c + 1) * P].rearrange("(p a) -> p a", a=1))
                     for c in range(FF // P)]
                for dst, src in loads:
                    act.dma_start(dst, src).then_inc(loaded, 16)
                act.wait_ge(loaded, 16 * len(loads))
                assert len(loads) == NLOADS + 1

            @block.gpsimd
            def _(pool):
                ch = Chain(pool, gchain)
                nc.gpsimd.memset(relpad[:], MASKED).then_inc(padded, 1)
                ch.step(nc.gpsimd.memset(ident[:], 0.0))
                ch.step(nc.gpsimd.affine_select(out=ident[:], in_=ident[:], compare_op=ALU.not_equal, fill=1.0,
                                                base=0, pattern=[[-1, P]], channel_multiplier=1))
                ch.step(nc.gpsimd.memset(anti[:], 0.0))
                nc.gpsimd.affine_select(out=anti[:], in_=anti[:], compare_op=ALU.not_equal, fill=1.0,
                                        base=-(P - 1), pattern=[[1, P]], channel_multiplier=1).then_inc(filled, 1)
                ch.step(nc.gpsimd.memset(aug[:], 0.0))
                for t in range(2):
                    ch.step(nc.gpsimd.memset(aug[:, 1, t, :, KROWS:XROWS], 1.0))
                ch.step(nc.gpsimd.memset(vaug[:], 0.0))
                for t in range(2):
                    ch.step(nc.gpsimd.memset(vaug[:, t, :, 0, HD:HD + 1], 1.0))
                ch.step(nc.gpsimd.memset(unit[:], 1.0))
                nc.gpsimd.memset(neghalf[:], -0.5).then_inc(filled, 1)

            @block.vector
            def _(dve):
                ch = Chain(dve, vchain)
                dve.wait_ge(filled, 1)
                ch.step(nc.vector.tensor_copy(identb[:], ident[:]))
                dve.wait_ge(loaded, 16 * (NLOADS + 1))
                ch.step(nc.vector.memset(ones[:], 1.0))
                nc.vector.tensor_scalar(lnb1[:], ones[:], gcol[:, 1:2], None, ALU.mult).then_inc(filled, 1)
                dve.wait_ge(full, 1)
                ch.step(nc.vector.tensor_copy(wqkv[:], pw[0][:, 0:3 * s.E]))
                nc.vector.tensor_copy(wo[:], pw[0][:, 3 * s.E:4 * s.E]).then_inc(taken, 1)
                dve.wait_ge(full, 2)
                ch.step(nc.vector.tensor_copy(w1[:], pw[1][:]))
                nc.vector.tensor_copy(w2[:].rearrange("p c e -> p (c e)"), pw[2][:]).then_inc(taken, 1)
                dve.wait_ge(full, 3)
                ch.step(nc.vector.tensor_tensor(bqkv[:], pw[3][:, 0:3 * s.E], inb[:], ALU.add))
                ch.step(nc.vector.tensor_scalar(bqkv[:, 0:s.E], bqkv[:, 0:s.E], HD ** -0.5, None, ALU.mult))
                ch.step(nc.vector.tensor_tensor(b1[:], pw[0][:, 0:FF // P], b1ld[:], ALU.add))
                ch.step(nc.vector.tensor_scalar(wqkv[:], wqkv[:], gcol[:, 0:1], None, ALU.mult))
                ch.step(nc.vector.tensor_scalar(wqkv[:, 0:s.E], wqkv[:, 0:s.E], HD ** -0.5, None, ALU.mult))
                ch.step(nc.vector.tensor_scalar(w1[:], w1[:], gcol[:, 2:3], None, ALU.mult))
                for j in range(PAIRS):
                    dve.wait_ge(full, 4 + j)
                    src = pw[1 + j % 2][:].rearrange("p (h q) -> p h q", h=2)
                    ch.step(nc.vector.tensor_copy(bias32[:, 2 * j:2 * j + 2, 0:2 * P], src))
                    ch.step(nc.vector.tensor_copy(biasb[:, 2 * j:2 * j + 2, :], src))
                    nc.vector.tensor_copy(bias32[:, 2 * j:2 * j + 2, 2 * P:BK], src[:, :, 0:P]).then_inc(taken, 1)

            @block.tensor
            def _(pe):
                pe.wait_ge(loaded, 16 * (NLOADS + 1))
                pe.wait_ge(filled, 3)
                for c in range(4):
                    last = nc.tensor.transpose(pw[0][:, c * P:(c + 1) * P], wrow[:, c, :], ident[:])
                last.then_inc(full, 1)
                for c in range(4):
                    nc.tensor.transpose(pw[1][:, c * P:(c + 1) * P], wrow[:, 4 + c, :], ident[:])
                for c in range(4):
                    last = nc.tensor.transpose(pw[2][:, c * P:(c + 1) * P], w2row[:, c * P:(c + 1) * P], ident[:])
                last.then_inc(full, 1)
                pe.wait_ge(taken, 2)
                nc.tensor.matmul(pw[3][:, 0:3 * s.E], lnb1[:], wqkv[:], start=True, stop=True)
                for c in range(FF // P):
                    last = nc.tensor.matmul(pw[0][:, c:c + 1], w1[:, c * P:(c + 1) * P], gcol[:, 3:4],
                                            start=True, stop=True)
                last.then_inc(full, 1)
                pe.wait_ge(rel_tab, 16)
                for j in range(PAIRS):
                    if j >= 2:
                        pe.wait_ge(taken, 2 + j - 1)
                    nc.tensor.matmul(pw[1 + j % 2][:], anti[:],
                                     hank[:, 2 * j:2 * j + 2, :].rearrange("p h q -> p (h q)"),
                                     start=True, stop=True).then_inc(full, 1)

    xn = sb("xn", [P, 2, s.E])
    xnT = sb("xnT", [P, 2 * P])
    xlb = sb("xlb", [P, 2, 2, s.E])
    qkv = sb("qkv", [P, 3, 2, s.E])
    rest = sb("rest", [P, 2, 2, s.E])
    vrest = sb("vrest", [P, 2, s.E])
    qT = sb("qT", [P, 2, PAIRS, 2 * P], BF16)
    kT = sb("kT", [P, 2, PAIRS, 2 * P], BF16)
    stats = sb("stats", [P, 2, 6])
    mv = sb("mv", [P, 4, 2])
    arg = sb("arg", [P, 2, 2])
    rs = sb("rs", [P, 2, 2])
    stats2 = sb("stats2", [P, 2, 6])
    mv2 = sb("mv2", [P, 4, 2])
    arg2 = sb("arg2", [P, 2])
    rs2 = sb("rs2", [P, 2])
    mx = sb("mx", [P, H, 3])
    mq = sb("mq", [P, 2, H])
    mrest = sb("mrest", [P, 2, H])
    ebuf = sb("ebuf", [P, 2, 2, BK])
    p32 = sb("p32", [P, 2, 2, BK])
    phi = sb("phi", [P, 4, 2, BK], F16)
    plo = sb("plo", [P, 4, 2, BK], F16)
    osum = sb("osum", [P, 2, H, HD + 1])
    rden = sb("rden", [P, 2, H, 1])
    onrm = sb("onrm", [P, 2, s.E])
    oT = sb("oT", [P, 2 * P])
    y1 = sb("y1", [P, 2, s.E])
    xb2 = sb("xb2", [P, 2, s.E])
    ysum = sb("ysum", [P, 2, s.E])
    xm = sb("xm", [P, 2, s.E])
    xmT = sb("xmT", [P, 2 * P])
    hT = sb("hT", [P, FF // P, 2 * P])

    ring = [ctx.enter_context(nc.psum_tensor(f"ring{i}", [P, 2, 512], F32)) for i in range(2)]
    bankT = ctx.enter_context(nc.psum_tensor("bankT", [P, 512], F32))
    bankW = ctx.enter_context(nc.psum_tensor("bankW", [P, 512], F32))
    bankO = [ctx.enter_context(nc.psum_tensor(f"bankO{t}", [P, 512], F32)) for t in range(2)]

    T_full, T_free, W_full, W_free = sem("T_full"), sem("T_free"), sem("W_full"), sem("W_free")
    ring_full, ring_free = sem("ring_full"), sem("ring_free")
    biased, exped, lowed, weighed = sem("scores_biased"), sem("exp_done"), sem("low_done"), sem("pv_done")
    O_free = sem("O_free")
    arg1_ready, rs1_ready, xn_ready, xlb_ready, xl_ready = (sem("arg1_ready"), sem("rs1_ready"), sem("xn_ready"),
                                                            sem("xlb_ready"), sem("xl_ready"))
    v_ready, vaug_ready = sem("v_ready"), sem("vaug_ready")
    aug_ready, max_ready = sem("aug_ready"), sem("max_ready")
    on_ready, y1_ready, arg2_ready, rs2_ready = sem("on_ready"), sem("y1_ready"), sem("arg2_ready"), sem("rs2_ready")
    xm_ready, ysum_ready, x_done = sem("xm_ready"), sem("ysum_ready"), sem("x_done")
    vchain, gchain = sem("attn_vector_steps"), sem("attn_gpsimd_steps")

    T_BODY, W_BODY = 7, 8

    def useT(stage, b, u=0, last=False):
        if stage == "prep":
            return u if isinstance(b, int) and b == 0 else 4 + T_BODY * (b - 1) + u
        if stage == "out":
            return (4 if last else 7) + T_BODY * b + u
        return 3 + T_BODY * b

    def useW(stage, b, u=0, last=False):
        if stage == "prep":
            return u if isinstance(b, int) and b == 0 else 5 + W_BODY * (b - 1) + u
        if stage == "out":
            return (5 if last else 9) + W_BODY * b + u
        return 4 + W_BODY * b

    LAST = B - 1
    V_LN1, V_QKV, V_B = 5, 5, 5

    def heads(t):
        return t.rearrange("p t (h d) -> p (t h) d", d=HD)

    def tiles(b):
        return xres[:, bass.ds(2 * b, 2), :]

    def tile(b, t):
        return xres[:, bass.ds(2 * b + t, 1), :].rearrange("p a e -> p (a e)")

    with nc.Block() as block:

        @block.tensor
        def _(pe):
            def takeT(use):
                pe.wait_ge(T_free, use)

            def takeW(use):
                pe.wait_ge(W_free, use)

            def norm_T(b):
                pe.wait_ge(xn_ready, b + 1)
                takeW(useW("prep", b, 0))
                for t in range(2):
                    last = nc.tensor.transpose(bankW[:, t * P:(t + 1) * P], xn[:, t, :], ident[:])
                last.then_inc(W_full, 1)

            def project(b):
                pe.wait_ge(W_free, useW("prep", b, 0) + 1)
                takeT(useT("prep", b, 0))
                nc.tensor.matmul(bankT[:, 0:3 * s.E], xnT[:, 0:P], wqkv[:], start=True, stop=True).then_inc(T_full, 1)
                takeW(useW("prep", b, 1))
                nc.tensor.matmul(bankW[:, 0:3 * s.E], xnT[:, P:2 * P], wqkv[:], start=True, stop=True).then_inc(W_full, 1)

            def aug_T(which, t):
                bank = bankT if t == 0 else bankW
                dst = bank[:].bitcast(BF16).rearrange("p (g q) -> p g q", g=PAIRS)
                for g in range(PAIRS):
                    last = nc.tensor.transpose(dst[:, g, :], aug[:, which, t, 2 * g:2 * g + 2, :].rearrange("p h a -> p (h a)"),
                                               identb[:])
                last.then_inc(T_full if t == 0 else W_full, 1)

            def qk_T(b, which):
                if which == 0:
                    pe.wait_ge(aug_ready, b + 1)
                takeT(useT("prep", b, 1 + which))
                aug_T(which, 0)
                takeW(useW("prep", b, 2 + which))
                aug_T(which, 1)

            def max_T(b):
                pe.wait_ge(max_ready, b + 1)
                takeT(useT("max", b))
                aug_T(0, 0)
                takeW(useW("max", b))
                aug_T(0, 1)

            def scores_for_max(b, p, j):
                r = ring[j % 2]
                use = 16 * b + j
                if j == 0:
                    pe.wait_ge(T_free, useT("prep", b, 2) + 1)
                    pe.wait_ge(W_free, useW("prep", b, 3) + 1)
                if not (isinstance(use, int) and use < 2):
                    pe.wait_ge(ring_free, use - 1)
                for hh in range(2):
                    h = 2 * j + hh
                    nc.tensor.matmul(r[:, hh, 0:P], biasb[:, h, P:2 * P], identb[:], start=True, stop=False,
                                     skip_group_check=True)
                    nc.tensor.matmul(r[:, hh, P:2 * P], biasb[:, h, 0:P], identb[:], start=False, stop=False,
                                     skip_group_check=True)
                    nc.tensor.matmul(r[:, hh, 2 * P:BK], biasb[:, h, 0:P], identb[:], start=False, stop=False,
                                     skip_group_check=True)
                for hh in range(2):
                    rows = slice(AUG * hh, AUG * hh + KROWS)
                    nc.tensor.matmul(r[:, hh, 0:2 * P], qT[rows, p, j, P:2 * P], kT[rows, p, j, :],
                                     start=False, stop=True, skip_group_check=True)
                for hh in range(2):
                    rows = slice(AUG * hh, AUG * hh + KROWS)
                    last = nc.tensor.matmul(r[:, hh, 2 * P:BK], qT[rows, p, j, 0:P], kT[rows, p, j, 0:P],
                                            start=False, stop=True, skip_group_check=True)
                last.then_inc(ring_full, 1)

            def scores(b, p, j):
                r = ring[j % 2]
                if j == 0:
                    pe.wait_ge(T_free, useT("max", b) + 1)
                    pe.wait_ge(W_free, useW("max", b) + 1)
                pe.wait_ge(ring_free, 16 * b + 8 + j - 1)
                for hh in range(2):
                    rows = slice(AUG * hh, AUG * hh + XROWS)
                    nc.tensor.matmul(r[:, hh, 0:2 * P], kT[rows, p, j, 0:P], qT[rows, p, j, :], start=True, stop=True)
                for hh in range(2):
                    rows = slice(AUG * hh, AUG * hh + XROWS)
                    last = nc.tensor.matmul(r[:, hh, 2 * P:BK], kT[rows, p, j, P:2 * P], qT[rows, p, j, P:2 * P],
                                            start=True, stop=True)
                last.then_inc(ring_full, 1)

            def weigh(b, j):
                if j == 0:
                    pe.wait_ge(vaug_ready, b + 1)
                    pe.wait_ge(O_free, b + 1)
                pe.wait_ge(lowed, 8 * b + j + 3)
                for hh in range(2):
                    h = 2 * j + hh
                    for t, blocks in ((0, ((0, 0),)), (1, ((P, 0), (2 * P, 1)))):
                        n = 2 * len(blocks)
                        i = 0
                        for part in (phi, plo):
                            for col, kt in blocks:
                                last = nc.tensor.matmul(bankO[t][:, h * VW:(h + 1) * VW], part[:, j % 4, hh, col:col + P],
                                                        vaug[:, kt, h, :, :].rearrange("p s d -> p (s d)"),
                                                        start=(i == 0), stop=(i == n - 1))
                                i += 1
                last.then_inc(weighed, 1)

            def out_T(b, last_b):
                pe.wait_ge(on_ready, b + 1)
                takeT(useT("out", b, 0, last_b))
                for t in range(2):
                    last = nc.tensor.transpose(bankT[:, t * P:(t + 1) * P], onrm[:, t, :], ident[:])
                last.then_inc(T_full, 1)

            def out_proj(b, last_b):
                pe.wait_ge(T_free, useT("out", b, 0, last_b) + 1)
                takeW(useW("out", b, 0, last_b))
                for t in range(2):
                    last = nc.tensor.matmul(bankW[:, t * P:(t + 1) * P], oT[:, t * P:(t + 1) * P], wo[:],
                                            start=True, stop=True)
                last.then_inc(W_full, 1)

            def mlp_T(b, last_b):
                pe.wait_ge(xm_ready, b + 1)
                takeT(useT("out", b, 1, last_b))
                for t in range(2):
                    last = nc.tensor.transpose(bankT[:, t * P:(t + 1) * P], xm[:, t, :], ident[:])
                last.then_inc(T_full, 1)

            def mlp_up(b, last_b):
                pe.wait_ge(T_free, useT("out", b, 1, last_b) + 1)
                takeW(useW("out", b, 1, last_b))
                for f in range(2):
                    last = nc.tensor.matmul(bankW[:, f * 2 * P:(f + 1) * 2 * P], w1[:, f * P:(f + 1) * P], xmT[:],
                                            start=True, stop=True)
                last.then_inc(W_full, 1)
                takeT(useT("out", b, 2, last_b))
                for f in range(2):
                    last = nc.tensor.matmul(bankT[:, f * 2 * P:(f + 1) * 2 * P], w1[:, (2 + f) * P:(3 + f) * P], xmT[:],
                                            start=True, stop=True)
                last.then_inc(T_full, 1)

            def mlp_down(b, last_b):
                pe.wait_ge(T_free, useT("out", b, 2, last_b) + 1)
                takeW(useW("out", b, 2, last_b))
                for t in range(2):
                    for f in range(FF // P):
                        last = nc.tensor.matmul(bankW[:, t * P:(t + 1) * P], hT[:, f, t * P:(t + 1) * P], w2[:, f, :],
                                                start=(f == 0), stop=(f == FF // P - 1))
                last.then_inc(W_full, 1)

            def body(b, p, more):
                for j in range(PAIRS):
                    scores(b, p, j)
                    if j >= 2:
                        weigh(b, j - 2)
                    if more:
                        if j == 1:
                            norm_T(b + 1)
                        if j == 2:
                            project(b + 1)
                        if j == 6:
                            qk_T(b + 1, 0)
                        if j == 7:
                            qk_T(b + 1, 1)
                weigh(b, PAIRS - 2)
                weigh(b, PAIRS - 1)
                for j in range(PAIRS):
                    if more:
                        scores_for_max(b + 1, 1 - p, j)
                    if j == 1:
                        out_T(b, not more)
                    if j == 2:
                        out_proj(b, not more)
                    if j == 5:
                        mlp_T(b, not more)
                    if j == 6:
                        mlp_up(b, not more)
                    if j == 7:
                        mlp_down(b, not more)
                if more:
                    max_T(b + 1)

            norm_T(0)
            project(0)
            qk_T(0, 0)
            qk_T(0, 1)
            for j in range(PAIRS):
                scores_for_max(0, 0, j)
            max_T(0)
            with pe.Fori(0, (B - 2) // 2) as it:
                for p in range(2):
                    body(it * 2 + p, p, True)
            body(B - 2, 0, True)
            body(B - 1, 1, False)

        @block.vector
        def _(dve):
            ch = Chain(dve, vchain)

            def norm_stats(b):
                for t in range(2):
                    last = ch.mark(nc.vector.bn_stats(stats[:, t, :], tile(b, t)))
                ch.wait(last)
                moments(nc, ch, stats, mv)
                nc.vector.tensor_scalar(arg[:, 0, :], mv[:, 3, :], 0.25, EPS, ALU.mult, ALU.add)
                nc.vector.tensor_scalar(arg[:, 1, :], mv[:, 3, :], 0.25 * (1.0 + EPS), EPS * EPS, ALU.mult, ALU.add).then_inc(arg1_ready, 1)

            def norm_apply(b, p, use_free):
                dve.wait_ge(rs1_ready, b + 1)
                if use_free is not None:
                    dve.wait_ge(W_full, use_free)
                for t in range(2):
                    last = nc.vector.tensor_scalar(xn[:, t, :], tile(b, t), mv[:, 0, t:t + 1], rs[:, 1, t:t + 1],
                                                   ALU.subtract, ALU.mult)
                last.then_inc(xn_ready, 1)
                for t in range(2):
                    last = nc.vector.tensor_scalar(xlb[:, p, t, :], tile(b, t), mv[:, 0, t:t + 1], rs[:, 0, t:t + 1],
                                                   ALU.subtract, ALU.mult)
                last.then_inc(xl_ready, 1)

            def take_qkv(b):
                if not (isinstance(b, int) and b == 0):
                    dve.wait_ge(vaug_ready, b)
                dve.wait_ge(T_full, useT("prep", b, 0) + 1)
                nc.vector.tensor_tensor(qkv[:, :, 0, :], bankT[:, 0:3 * s.E].rearrange("p (c e) -> p c e", c=3),
                                        bqkv[:].rearrange("p (c e) -> p c e", c=3), ALU.add).then_inc(T_free, 1)
                dve.wait_ge(W_full, useW("prep", b, 1) + 1)
                nc.vector.tensor_tensor(qkv[:, :, 1, :], bankW[:, 0:3 * s.E].rearrange("p (c e) -> p c e", c=3),
                                        bqkv[:].rearrange("p (c e) -> p c e", c=3), ALU.add).then_inc(W_free, 1)
                dve.wait_ge(W_free, useW("prep", b, 1) + 1)
                dve.wait_ge(T_free, useT("prep", b, 0) + 1)
                dve.sem_inc(v_ready, 1)

            def slot(which, i):
                return aug[:, which, :, :, i * HD:(i + 1) * HD].rearrange("p t h d -> p (t h) d")

            def split_qk(b):
                q, k = heads(qkv[:, 0, :, :]), heads(qkv[:, 1, :, :])
                for i in range(3):
                    ch.mark(nc.vector.tensor_copy(slot(0, i), q))
                for i in (0, 3, 5):
                    last = ch.mark(nc.vector.tensor_copy(slot(1, i), k))
                ch.wait(last)
                nc.vector.tensor_tensor(heads(rest[:, 0, :, :]), q, slot(0, 0), ALU.subtract)
                ch.step(nc.vector.tensor_tensor(heads(rest[:, 1, :, :]), k, slot(1, 0), ALU.subtract))
                for which, i in ((0, 3), (0, 4), (1, 1), (1, 4)):
                    last = ch.mark(nc.vector.tensor_copy(slot(which, i), heads(rest[:, which, :, :])))
                ch.wait(last)
                nc.vector.tensor_tensor(slot(0, 5), heads(rest[:, 0, :, :]), slot(0, 4), ALU.subtract)
                nc.vector.tensor_tensor(slot(1, 2), heads(rest[:, 1, :, :]), slot(1, 4), ALU.subtract).then_inc(aug_ready, 1)

            def take_T(which, b, p):
                dve.wait_ge(W_full, useW("prep", b, 2 + which) + 1)
                nc.vector.tensor_copy((qT, kT)[which][:, p, :, P:2 * P],
                                      bankW[:].bitcast(BF16).rearrange("p (g q) -> p g q", g=PAIRS)).then_inc(W_free, 1)

            def reduce_max(b, j):
                dve.wait_ge(ring_full, 16 * b + j + 1)
                if j == 0 and not (isinstance(b, int) and b == 0):
                    dve.wait_ge(max_ready, b)
                nc.vector.reduce_max(mx[:, 2 * j:2 * j + 2, :],
                                     ring[j % 2][:, :, 0:BK].rearrange("p h (k c) -> p h k c", k=3), AXX).then_inc(ring_free, 1)

            def take_max(b):
                dve.wait_ge(ring_free, 16 * b + 8)
                nc.vector.tensor_tensor(mq[:, 1, :], mx[:, :, 0], mx[:, :, 1], ALU.max)
                ch.step(nc.vector.tensor_copy(mq[:, 0, :], mx[:, :, 2]))
                part = aug[:, 0, :, :, KROWS:XROWS]
                ch.step(nc.vector.tensor_scalar(part[:, :, :, 0], mq[:], -1.0, None, ALU.mult))
                nc.vector.scalar_tensor_tensor(part[:, :, :, 1], mq[:], -1.0, part[:, :, :, 0],
                                               ALU.mult, ALU.subtract).then_inc(max_ready, 1)

            def take_max_T(b, p):
                dve.wait_ge(W_full, useW("max", b) + 1)
                nc.vector.tensor_copy(qT[:, p, :, P:2 * P],
                                      bankW[:].bitcast(BF16).rearrange("p (g q) -> p g q", g=PAIRS)).then_inc(W_free, 1)

            def add_mask(b, j):
                dve.wait_ge(ring_full, 16 * b + 8 + j + 1)
                use = 8 * b + j
                if j >= 2:
                    dve.wait_ge(exped, use - 1)
                nc.vector.tensor_tensor(ebuf[:, j % 2, :, :], ring[j % 2][:, :, 0:BK], bias32[:, 2 * j:2 * j + 2, :],
                                        ALU.add).then_inc(biased, 1)
                dve.wait_ge(biased, use + 1)
                dve.sem_inc(ring_free, 1)

            def normalise(b):
                dve.wait_ge(weighed, 8 * b + 8)
                for t in range(2):
                    last = nc.vector.reduce_sum(osum[:, t, :, :], bankO[t][:, 0:H * VW].rearrange(
                        "p (h s d) -> p h d s", h=H, s=3), AXX)
                last.then_inc(O_free, 1)
                dve.wait_ge(O_free, b + 2)
                ch.step(nc.vector.reciprocal(rden[:].rearrange("p t h a -> p (t h a)"),
                                             osum[:, :, :, HD].rearrange("p t h -> p (t h)")))
                nc.vector.tensor_tensor(heads(onrm[:]), osum[:, :, :, 0:HD].rearrange("p t h d -> p (t h) d"),
                                        rden[:].rearrange("p t h a -> p (t h) a").broadcast_to([P, 2 * H, HD]),
                                        ALU.mult).then_inc(on_ready, 1)

            def second_norm(b, p, last_b):
                dve.wait_ge(W_full, useW("out", b, 0, last_b) + 1)
                dve.wait_ge(xlb_ready, b + 1)
                ch.step(nc.vector.tensor_tensor(y1[:].rearrange("p t e -> p (t e)"), bankW[:, 0:2 * P],
                                                xlb[:, p, :, :].rearrange("p t e -> p (t e)"), ALU.add))
                dve.sem_inc(W_free, 1)
                dve.sem_inc(y1_ready, 1)
                for t in range(2):
                    last = ch.mark(nc.vector.bn_stats(stats2[:, t, :], y1[:, t, :]))
                ch.wait(last)
                moments(nc, ch, stats2, mv2)
                nc.vector.tensor_scalar(arg2[:], mv2[:, 3, :], 0.25, EPS, ALU.mult, ALU.add).then_inc(arg2_ready, 1)

            def second_apply(b):
                dve.wait_ge(rs2_ready, b + 1)
                for t in range(2):
                    last = nc.vector.tensor_scalar(xm[:, t, :], y1[:, t, :], mv2[:, 0, t:t + 1], rs2[:, t:t + 1],
                                                   ALU.subtract, ALU.mult)
                last.then_inc(xm_ready, 1)

            def finish(b, last_b):
                dve.wait_ge(W_full, useW("out", b, 2, last_b) + 1)
                dve.wait_ge(ysum_ready, b + 1)
                nc.vector.tensor_tensor(tiles(b).rearrange("p t e -> p (t e)"), bankW[:, 0:2 * P],
                                        ysum[:].rearrange("p t e -> p (t e)"), ALU.add).then_inc(x_done, 1)
                dve.wait_ge(x_done, b + 1)
                dve.sem_inc(W_free, 1)

            def body(b, p, more, more2):
                for j in range(PAIRS):
                    add_mask(b, j)
                    if more:
                        if j == 3:
                            take_qkv(b + 1)
                        if j == 4:
                            split_qk(b + 1)
                        if j == 7:
                            take_T(0, b + 1, 1 - p)
                if more:
                    take_T(1, b + 1, 1 - p)
                for j in range(PAIRS):
                    if more:
                        reduce_max(b + 1, j)
                    if j == 0:
                        normalise(b)
                    if j == 3:
                        second_norm(b, p, not more)
                    if j == 4 and more2:
                        norm_stats(b + 2)
                    if j == 5:
                        second_apply(b)
                    if j == 6 and more2:
                        norm_apply(b + 2, p, useW("prep", b + 1, 0) + 1)
                if more:
                    take_max(b + 1)
                finish(b, not more)
                if more:
                    take_max_T(b + 1, 1 - p)

            dve.sem_inc(O_free, 1)
            norm_stats(0)
            norm_apply(0, 0, None)
            take_qkv(0)
            split_qk(0)
            take_T(0, 0, 0)
            take_T(1, 0, 0)
            for j in range(PAIRS):
                reduce_max(0, j)
            norm_stats(1)
            norm_apply(1, 1, 1)
            take_max(0)
            take_max_T(0, 0)
            before = ch.base + ch.n
            with dve.Fori(0, (B - 2) // 2) as it:
                for p in range(2):
                    b = it * 2 + p
                    per = 31
                    ch.start(b * per + before)
                    body(b, p, True, True)
                    assert ch.n == per, ch.n
            ch.start((B - 2) * per + before)
            body(B - 2, 0, True, False)
            body(B - 1, 1, False, False)

        @block.scalar
        def _(act):
            def take_norm(b):
                act.wait_ge(W_full, useW("prep", b, 0) + 1)
                nc.scalar.copy(xnT[:], bankW[:, 0:2 * P]).then_inc(W_free, 1)

            def take_T(which, b, p):
                act.wait_ge(T_full, useT("prep", b, 1 + which) + 1)
                nc.scalar.copy((qT, kT)[which][:, p, :, 0:P],
                               bankT[:].bitcast(BF16).rearrange("p (g q) -> p g q", g=PAIRS)).then_inc(T_free, 1)

            def take_max(b, p):
                act.wait_ge(T_full, useT("max", b) + 1)
                nc.scalar.copy(qT[:, p, :, 0:P],
                               bankT[:].bitcast(BF16).rearrange("p (g q) -> p g q", g=PAIRS)).then_inc(T_free, 1)

            def exponentials(b, j):
                use = 8 * b + j
                act.wait_ge(biased, use + 1)
                act.wait_ge(lowed, use + 1)
                nc.scalar.activation(p32[:, j % 2, :, :], ebuf[:, j % 2, :, :], ACT.Exp)
                if j >= 4:
                    act.wait_ge(weighed, use - 3)
                nc.scalar.activation(phi[:, j % 4, :, :], ebuf[:, j % 2, :, :], ACT.Exp).then_inc(exped, 1)

            def body(b, p, more):
                last_b = not more
                for j in range(PAIRS):
                    exponentials(b, j)
                    if more:
                        if j == 1:
                            take_norm(b + 1)
                        if j == 6:
                            take_T(0, b + 1, 1 - p)
                        if j == 7:
                            take_T(1, b + 1, 1 - p)
                act.wait_ge(T_full, useT("out", b, 0, last_b) + 1)
                nc.scalar.copy(oT[:], bankT[:, 0:2 * P]).then_inc(T_free, 1)
                act.wait_ge(T_full, useT("out", b, 1, last_b) + 1)
                nc.scalar.copy(xmT[:], bankT[:, 0:2 * P]).then_inc(T_free, 1)
                act.wait_ge(W_full, useW("out", b, 1, last_b) + 1)
                for f in range(2):
                    last = nc.scalar.activation(hT[:, f, :], bankW[:, f * 2 * P:(f + 1) * 2 * P], ACT.Relu,
                                                bias=b1[:, f:f + 1])
                last.then_inc(W_free, 1)
                act.wait_ge(T_full, useT("out", b, 2, last_b) + 1)
                for f in range(2):
                    last = nc.scalar.activation(hT[:, 2 + f, :], bankT[:, f * 2 * P:(f + 1) * 2 * P], ACT.Relu,
                                                bias=b1[:, 2 + f:3 + f])
                last.then_inc(T_free, 1)
                if more:
                    take_max(b + 1, 1 - p)

            take_norm(0)
            take_T(0, 0, 0)
            take_T(1, 0, 0)
            take_max(0, 0)
            with act.Fori(0, (B - 2) // 2) as it:
                for p in range(2):
                    body(it * 2 + p, p, True)
            body(B - 2, 0, True)
            body(B - 1, 1, False)

        @block.gpsimd
        def _(pool):
            ch = Chain(pool, gchain)

            def low_part(b, j):
                use = 8 * b + j
                pool.wait_ge(exped, use + 1)
                if j >= 4:
                    pool.wait_ge(weighed, use - 3)
                nc.gpsimd.tensor_tensor(plo[:, j % 4, :, :], p32[:, j % 2, :, :], phi[:, j % 4, :, :],
                                        ALU.subtract).then_inc(lowed, 1)

            def split_v(b):
                pool.wait_ge(v_ready, b + 1)
                if not (isinstance(b, int) and b == 0):
                    pool.wait_ge(weighed, 8 * b)
                v = heads(qkv[:, 2, :, :])

                def part(i):
                    return vaug[:, :, :, i, 0:HD].rearrange("p t h d -> p (t h) d")

                ch.step(nc.gpsimd.tensor_tensor(part(0), v, heads(unit[:]), ALU.mult))
                ch.step(nc.gpsimd.tensor_tensor(heads(vrest[:]), v, part(0), ALU.subtract))
                ch.step(nc.gpsimd.tensor_tensor(part(1), heads(vrest[:]), heads(unit[:]), ALU.mult))
                nc.gpsimd.tensor_tensor(part(2), heads(vrest[:]), part(1), ALU.subtract).then_inc(vaug_ready, 1)

            def roots(b):
                pool.wait_ge(arg1_ready, b + 1)
                nc.gpsimd.tensor_tensor(rs[:].rearrange("p a t -> p (a t)"), arg[:].rearrange("p a t -> p (a t)"),
                                        neghalf[:], ALU.pow).then_inc(rs1_ready, 1)

            def normed(b, p):
                pool.wait_ge(xl_ready, b + 1)
                for t in range(2):
                    last = nc.gpsimd.tensor_tensor(xlb[:, p, t, :], xlb[:, p, t, :], outb[:], ALU.add)
                last.then_inc(xlb_ready, 1)

            def body(b, p, more, more2):
                for j in range(PAIRS):
                    low_part(b, j)
                for t in range(2):
                    last = ch.mark(nc.gpsimd.tensor_tensor(xb2[:, t, :], tile(b, t), b2[:], ALU.add))
                ch.wait(last)
                if more:
                    split_v(b + 1)
                pool.wait_ge(arg2_ready, b + 1)
                nc.gpsimd.tensor_tensor(rs2[:], arg2[:], neghalf[:, 0:2], ALU.pow).then_inc(rs2_ready, 1)
                pool.wait_ge(y1_ready, b + 1)
                nc.gpsimd.tensor_tensor(ysum[:].rearrange("p t e -> p (t e)"), y1[:].rearrange("p t e -> p (t e)"),
                                        xb2[:].rearrange("p t e -> p (t e)"), ALU.add).then_inc(ysum_ready, 1)
                if more2:
                    roots(b + 2)
                    normed(b + 2, p)

            pool.sem_inc(lowed, 2)
            roots(0)
            normed(0, 0)
            split_v(0)
            roots(1)
            normed(1, 1)
            before = ch.base + ch.n
            with pool.Fori(0, (B - 2) // 2) as it:
                for p in range(2):
                    b = it * 2 + p
                    per = 5
                    ch.start(b * per + before)
                    body(b, p, True, True)
                    assert ch.n == per, ch.n
            ch.start((B - 2) * per + before)
            body(B - 2, 0, True, False)
            body(B - 1, 1, False, False)


CH = 4


def expert_weights(nc, ctx, s, ins, ident):
    NE, EF, E = s.NE, s.EF, s.E
    NF = EF // P

    def sb(name, shape, dt=F32):
        return ctx.enter_context(nc.sbuf_tensor(name, shape, dt))

    w = {
        "gate": sb("gate_w", [P, NE, EF]), "up": sb("up_w", [P, NE, EF]),
        "down": sb("down_w", [P, NE, NF, E]), "downb": sb("down_b", [NE, E]),
        "gateb": sb("gate_b", [P, NE * NF]), "upb": sb("up_b", [P, NE * NF]),
        "router": sb("router", [P, NE]), "iota": sb("iota", [P, NE]),
    }
    with ExitStack() as c2:
        rrow = c2.enter_context(nc.sbuf_tensor("router_rows", [NE, E], F32))
        brow = c2.enter_context(nc.sbuf_tensor("bias_rows", [2 * NE * NF, P], F32))
        bank = c2.enter_context(nc.psum_tensor("setup_bank", [P, 512], F32))
        loaded = c2.enter_context(nc.semaphore("experts_loaded"))
        full = c2.enter_context(nc.semaphore("experts_bank_full"))
        taken = c2.enter_context(nc.semaphore("experts_taken"))
        with nc.Block() as block:
            @block.sync
            def _(sp):
                sp.dma_start(rrow[:], ins["L0_ffn_router_w"]).then_inc(loaded, 16)
                sp.dma_start(brow[0:NE * NF, :], ins["L0_ffn_gate_b"].rearrange("e (c p) -> (e c) p", p=P)).then_inc(loaded, 16)
                sp.dma_start(brow[NE * NF:2 * NE * NF, :], ins["L0_ffn_up_b"].rearrange("e (c p) -> (e c) p", p=P)).then_inc(loaded, 16)
                sp.dma_start(w["downb"][:], ins["L0_ffn_down_b"]).then_inc(loaded, 16)
                sp.dma_start(w["gate"][:], ins["L0_ffn_gate_w"].rearrange("e d f -> d e f")).then_inc(loaded, 16)
                sp.dma_start(w["up"][:], ins["L0_ffn_up_w"].rearrange("e d f -> d e f")).then_inc(loaded, 16)
                sp.dma_start(w["down"][:], ins["L0_ffn_down_w"].rearrange("e (c p) d -> p e c d", p=P)).then_inc(loaded, 16)
                sp.wait_ge(loaded, 16 * 7)

            @block.gpsimd
            def _(pool):
                for e in range(NE):
                    last = nc.gpsimd.memset(w["iota"][:, e:e + 1], float(e))
                last.then_inc(taken, 1)

            @block.tensor
            def _(pe):
                pe.wait_ge(loaded, 16 * 7)
                nc.tensor.transpose(bank[:, 0:NE], rrow[:], ident[0:NE, 0:NE])
                nc.tensor.transpose(bank[:, 64:64 + 2 * NE * NF], brow[:], ident[0:2 * NE * NF, 0:2 * NE * NF]).then_inc(full, 1)

            @block.vector
            def _(dve):
                dve.wait_ge(full, 1)
                nc.vector.tensor_copy(w["router"][:], bank[:, 0:NE])
                nc.vector.tensor_copy(w["gateb"][:], bank[:, 64:64 + NE * NF])
                nc.vector.tensor_copy(w["upb"][:], bank[:, 64 + NE * NF:64 + 2 * NE * NF]).then_inc(taken, 1)
    return w


def mixture(nc, s, tag, xres, ident, w):
    NE, NF, E, TILES = s.NE, s.EF // P, s.E, s.TILES
    CHUNKS = TILES // CH
    with ExitStack() as ctx:
        def sb(name, shape, dt=F32):
            return ctx.enter_context(nc.sbuf_tensor(tag + name, shape, dt))

        def sem(name):
            return ctx.enter_context(nc.semaphore(tag + name))

        xT = sb("xT", [P, TILES * P])
        logits = sb("logits", [P, TILES, NE])
        weight = sb("weight", [P, TILES, NE])
        route(nc, s, tag, xres, ident, w, xT, logits, weight)

        wT = sb("wT", [NE, CH * P])
        wch = sb("wch", [P, CH, NE])
        sg = sb("sg", [P, 2, CH * P])
        hid = sb("hid", [P, 2, NF, CH * P])
        bg = [ctx.enter_context(nc.psum_tensor(f"{tag}bg{i}", [P, 512], F32)) for i in range(2)]
        bu = [ctx.enter_context(nc.psum_tensor(f"{tag}bu{i}", [P, 512], F32)) for i in range(2)]
        by = [ctx.enter_context(nc.psum_tensor(f"{tag}by{i}", [P, 512], F32)) for i in range(2)]
        bw = ctx.enter_context(nc.psum_tensor(tag + "bw", [P, 512], F32))
        full_gu, gated, hid_done, y_full, y_taken = sem("gu_full"), sem("gated"), sem("hid_done"), sem("y_full"), sem("y_taken")
        w_full, w_taken, w_copied = sem("wT_full"), sem("wT_taken"), sem("w_copied")
        U = NE * NF
        with nc.Block() as block:
            @block.tensor
            def _(pe):
                with pe.Fori(0, CHUNKS) as c:
                    cols = bass.ds(c * CH * P, CH * P)
                    pe.wait_ge(w_copied, c + 1)
                    pe.wait_ge(w_taken, c + 1)
                    for t in range(CH):
                        last = nc.tensor.transpose(bw[0:NE, t * P:(t + 1) * P],
                                                   wch[:, t, :], ident[:])
                    last.then_inc(w_full, 1)

                    def down(e):
                        if e < 0:
                            pe.wait_ge(w_taken, c + 2)
                        else:
                            pe.wait_ge(hid_done, c * U + (e + 1) * NF + 1)
                        k = e + 1
                        pe.wait_ge(y_taken, c * (NE + 1) + max(k, 1))
                        for t in range(CH):
                            dst = by[k % 2][:, t * P:(t + 1) * P]
                            if e < 0:
                                last = nc.tensor.matmul(dst, wT[:, t * P:(t + 1) * P], w["downb"][:], start=True, stop=True)
                            else:
                                for f in range(NF):
                                    last = nc.tensor.matmul(dst, hid[:, e % 2, f, t * P:(t + 1) * P], w["down"][:, e, f, :],
                                                            start=(f == 0), stop=(f == NF - 1))
                        last.then_inc(y_full, 1)

                    down(-1)
                    for e in range(NE):
                        for f in range(NF):
                            i = e * NF + f
                            pe.wait_ge(hid_done, c * U + max(i, 1))
                            nc.tensor.matmul(bg[i % 2][:], w["gate"][:, e, f * P:(f + 1) * P], xT[:, cols], start=True, stop=True)
                            nc.tensor.matmul(bu[i % 2][:], w["up"][:, e, f * P:(f + 1) * P], xT[:, cols],
                                             start=True, stop=True).then_inc(full_gu, 1)
                        if e >= 1:
                            down(e - 1)
                    down(NE - 1)

            @block.scalar
            def _(act):
                act.sem_inc(w_taken, 1)
                with act.Fori(0, CHUNKS) as c:
                    act.wait_ge(w_full, c + 1)
                    nc.scalar.copy(wT[:], bw[0:NE, :]).then_inc(w_taken, 1)
                    for i in range(U):
                        act.wait_ge(full_gu, c * U + i + 1)
                        if i >= 2:
                            act.wait_ge(hid_done, c * U + i)
                        nc.scalar.activation(sg[:, i % 2, :], bg[i % 2][:], ACT.Silu, bias=w["gateb"][:, i:i + 1]).then_inc(gated, 1)

            @block.vector
            def _(dve):
                dve.sem_inc(y_taken, 1)
                dve.sem_inc(hid_done, 1)
                with dve.Fori(0, CHUNKS) as c:
                    def add(k):
                        dve.wait_ge(y_full, c * (NE + 1) + k + 1)
                        if k > 0:
                            dve.wait_ge(y_taken, c * (NE + 1) + k + 1)
                        for t in range(CH):
                            x = xres[:, bass.ds(c * CH + t, 1), :].rearrange("p a e -> p (a e)")
                            y = by[k % 2][:, t * P:(t + 1) * P]
                            if k == 0:
                                last = nc.vector.tensor_tensor(x, y, x, ALU.add)
                            else:
                                last = nc.vector.scalar_tensor_tensor(
                                    x, y, weight[:, bass.ds(c * CH + t, 1), k - 1:k].rearrange("p a e -> p (a e)"), x,
                                    ALU.mult, ALU.add)
                        last.then_inc(y_taken, 1)

                    dve.wait_ge(w_taken, c + 1)
                    nc.vector.tensor_copy(wch[:], weight[:, bass.ds(c * CH, CH), :]).then_inc(w_copied, 1)
                    add(0)
                    for i in range(U):
                        e, f = i // NF, i % NF
                        dve.wait_ge(gated, c * U + i + 1)
                        if f == 0 and e >= 2:
                            dve.wait_ge(y_full, c * (NE + 1) + e)
                        nc.vector.scalar_tensor_tensor(hid[:, e % 2, f, :], bu[i % 2][:], w["upb"][:, i:i + 1], sg[:, i % 2, :],
                                                       ALU.add, ALU.mult).then_inc(hid_done, 1)
                        if f == NF - 1 and e >= 1:
                            add(e)
                    add(NE)


def route(nc, s, tag, xres, ident, w, xT, logits, weight):
    NE, E, TILES = s.NE, s.E, s.TILES
    CHUNKS = TILES // CH
    with ExitStack() as ctx:
        def sb(name, shape, dt=F32):
            return ctx.enter_context(nc.sbuf_tensor(tag + name, shape, dt))

        def sem(name):
            return ctx.enter_context(nc.semaphore(tag + name))

        stats = sb("r_stats", [P, 2, CH, 6])
        mv = sb("r_mv", [P, 2, 4, CH])
        arg = sb("r_arg", [P, 2, CH])
        rs = sb("r_rs", [P, 2, CH])
        half = sb("r_half", [P, CH])
        xl = sb("r_xl", [P, 2, CH, E])
        xTc = sb("xTc", [P, 2, CH * P])
        prob = sb("prob", [P, TILES, NE])
        tmp = sb("r_tmp", [P, TILES, NE])
        tmp2 = sb("r_tmp2", [P, TILES, NE])
        hot = [sb(f"hot{k}", [P, TILES, NE]) for k in range(2)]
        top = [sb(f"top{k}", [P, TILES]) for k in range(2)]
        first = sb("first", [P, TILES])
        den = sb("den", [P, TILES])
        bx = [ctx.enter_context(nc.psum_tensor(f"{tag}bx{i}", [P, 512], F32)) for i in range(2)]
        bl = [ctx.enter_context(nc.psum_tensor(f"{tag}bl{i}", [P, 512], F32)) for i in range(2)]
        ready, rooted, normed, x_full, x_taken, l_full, l_taken = (
            sem("r_arg_ready"), sem("r_rooted"), sem("r_normed"), sem("r_xT_full"), sem("r_xT_taken"),
            sem("r_logits_full"), sem("r_logits_taken"))
        shifted, exped, chain = sem("r_shifted"), sem("r_exped"), sem("r_vector_steps")
        half_set = sem("r_half_set")

        with nc.Block() as block:
            @block.vector
            def _(dve):
                ch = Chain(dve, chain)
                nc.vector.memset(half[:], -0.5).then_inc(half_set, 1)
                PER = CH + 6

                def head(c, q):
                    for t in range(CH):
                        last = ch.mark(nc.vector.bn_stats(stats[:, q, t, :], xres[:, bass.ds(c * CH + t, 1), :].rearrange("p a e -> p (a e)")))
                    ch.wait(last)
                    if not (isinstance(c, int) and c < 2):
                        dve.wait_ge(normed, c - 1)
                    moments(nc, ch, stats[:, q], mv[:, q])
                    nc.vector.tensor_scalar(arg[:, q, :], mv[:, q, 3, :], 0.25, EPS, ALU.mult, ALU.add).then_inc(ready, 1)

                def tail(c, q):
                    dve.wait_ge(rooted, c + 1)
                    if not (isinstance(c, int) and c < 2):
                        dve.wait_ge(x_full, c - 1)
                    for t in range(CH):
                        last = nc.vector.tensor_scalar(xl[:, q, t, :], xres[:, bass.ds(c * CH + t, 1), :].rearrange("p a e -> p (a e)"),
                                                       mv[:, q, 0, t:t + 1], rs[:, q, t:t + 1], ALU.subtract, ALU.mult)
                    last.then_inc(normed, 1)

                def take(c, q):
                    dve.wait_ge(l_full, c + 1)
                    nc.vector.tensor_copy(logits[:, bass.ds(c * CH, CH), :].rearrange("p t e -> p (t e)"),
                                          bl[q][:, 0:CH * NE]).then_inc(l_taken, 1)

                def pair(c):
                    head(c + 1, 1)
                    tail(c, 0)
                    head(c + 2, 0)
                    tail(c + 1, 1)
                    take(c, 0)
                    take(c + 1, 1)

                head(0, 0)
                pair(0)
                with dve.Fori(1, CHUNKS // 2 - 1) as it:
                    ch.start(it * (2 * PER) + PER)
                    pair(it * 2)
                ch.start((CHUNKS // 2 - 1) * 2 * PER + PER)
                head(CHUNKS - 1, 1)
                tail(CHUNKS - 2, 0)
                tail(CHUNKS - 1, 1)
                take(CHUNKS - 2, 0)
                take(CHUNKS - 1, 1)
                dve.wait_ge(l_taken, CHUNKS)

                V = nc.vector

                def over(x):
                    return x[:].rearrange("p (t a) -> p t a", a=1).broadcast_to([P, TILES, NE])

                iota = w["iota"][:].rearrange("p (a e) -> p a e", a=1).broadcast_to([P, TILES, NE])
                ch.step(V.reduce_max(den[:], logits[:], AXX))
                V.tensor_tensor(logits[:], logits[:], over(den), ALU.subtract).then_inc(shifted, 1)
                dve.wait_ge(exped, 1)
                ch.step(V.reduce_sum(den[:], prob[:], AXX))
                ch.step(V.reciprocal(den[:], den[:]))
                ch.step(V.tensor_tensor(prob[:], prob[:], over(den), ALU.mult))
                left = prob
                for k in range(2):
                    ch.step(V.reduce_max(top[k][:], left[:], AXX))
                    ch.step(V.tensor_tensor(tmp[:], left[:], over(top[k]), ALU.is_equal))
                    ch.step(V.scalar_tensor_tensor(tmp[:], tmp[:], -float(NE), iota, ALU.mult, ALU.add))
                    ch.step(V.tensor_reduce(first[:], tmp[:], AXX, ALU.min))
                    ch.step(V.tensor_scalar(first[:], first[:], float(NE), None, ALU.add))
                    ch.step(V.tensor_tensor(hot[k][:], over(first), iota, ALU.is_equal))
                    if k == 0:
                        ch.step(V.scalar_tensor_tensor(tmp2[:], hot[0][:], -2.0, left[:], ALU.mult, ALU.add))
                        left = tmp2
                ch.step(V.scalar_tensor_tensor(den[:], top[0][:], 1e-9, top[1][:], ALU.add, ALU.add))
                ch.step(V.reciprocal(den[:], den[:]))
                for k in range(2):
                    ch.step(V.tensor_tensor(top[k][:], top[k][:], den[:], ALU.mult))
                    ch.step(V.tensor_tensor(hot[k][:], hot[k][:], over(top[k]), ALU.mult))
                ch.step(V.tensor_tensor(weight[:], hot[0][:], hot[1][:], ALU.add))

            @block.gpsimd
            def _(pool):
                pool.wait_ge(half_set, 1)

                def root(c, q):
                    pool.wait_ge(ready, c + 1)
                    nc.gpsimd.tensor_tensor(rs[:, q, :], arg[:, q, :], half[:], ALU.pow).then_inc(rooted, 1)

                with pool.Fori(0, CHUNKS // 2) as it:
                    root(it * 2, 0)
                    root(it * 2 + 1, 1)

            @block.tensor
            def _(pe):
                def chunk(c, q):
                    pe.wait_ge(normed, c + 1)
                    for t in range(CH):
                        last = nc.tensor.transpose(bx[q][:, t * P:(t + 1) * P], xl[:, q, t, :], ident[:])
                    last.then_inc(x_full, 1)
                    pe.wait_ge(x_taken, c + 1)
                    for t in range(CH):
                        last = nc.tensor.matmul(bl[q][:, t * NE:(t + 1) * NE],
                                                xTc[:, q, t * P:(t + 1) * P],
                                                w["router"][:], start=True, stop=True)
                    last.then_inc(l_full, 1)

                chunk(0, 0)
                chunk(1, 1)
                with pe.Fori(1, CHUNKS // 2) as it:
                    pe.wait_ge(l_taken, it * 2 - 1)
                    chunk(it * 2, 0)
                    pe.wait_ge(l_taken, it * 2)
                    chunk(it * 2 + 1, 1)


            @block.scalar
            def _(act):
                def chunk(c, q):
                    act.wait_ge(x_full, c + 1)
                    nc.scalar.copy(xTc[:, q, :], bx[q][:])
                    nc.scalar.copy(xT[:, bass.ds(c * CH * P, CH * P)], bx[q][:]).then_inc(x_taken, 1)

                chunk(0, 0)
                chunk(1, 1)
                with act.Fori(1, CHUNKS // 2) as it:
                    act.wait_ge(l_full, it * 2 - 1)
                    chunk(it * 2, 0)
                    act.wait_ge(l_full, it * 2)
                    chunk(it * 2 + 1, 1)
                act.wait_ge(shifted, 1)
                nc.scalar.activation(prob[:], logits[:], ACT.Exp).then_inc(exped, 1)


def recurrence(nc, s, ins, xres, ident):
    E, B, S = s.E, s.B, s.S
    with ExitStack() as ctx:
        def sb(name, shape, dt=F32):
            return ctx.enter_context(nc.sbuf_tensor(name, shape, dt))

        def sem(name):
            return ctx.enter_context(nc.semaphore(name))

        wz, wh = sb("wz", [P, E]), sb("wh", [P, E])
        cols = sb("z_cols", [P, 3])
        gamma, beta = sb("gamma", [P, 2, E]), sb("beta", [P, 2, E])
        half = sb("z_half", [P, 2])
        stats, mv = sb("z_stats", [P, 2, 2, 6]), sb("z_mv", [P, 2, 4, 2])
        arg, rs = sb("z_arg", [P, 2, 2]), sb("z_rs", [P, 2, 2])
        xl = sb("z_xl", [P, 2, 2, E])
        xT = sb("z_xT", [P, 2, 2 * P])
        keep, z, sg = sb("z_keep", [P, 2, S]), sb("z_gate", [P, 2, S]), sb("z_sig", [P, 2, S])
        relu, val, hs = sb("z_relu", [P, S]), sb("z_val", [P, S]), sb("z_h", [P, 2, S])
        stats2, mv2 = sb("z_stats2", [P, 2, 2, 6]), sb("z_mv2", [P, 2, 4, 2])
        arg2, rs2 = sb("z_arg2", [P, 2, 2]), sb("z_rs2", [P, 2, 2])
        nh, base = sb("z_nh", [P, 2, E]), sb("z_base", [P, 2, 2, E])
        bx = [ctx.enter_context(nc.psum_tensor(f"zx{i}", [P, 512], F32)) for i in range(2)]
        bk = [ctx.enter_context(nc.psum_tensor(f"zk{i}", [P, 512], F32)) for i in range(2)]
        bh = [ctx.enter_context(nc.psum_tensor(f"zh{i}", [P, 512], F32)) for i in range(2)]
        loaded, setup = sem("z_loaded"), sem("z_setup")
        ready, rooted, normed, x_full, x_taken, k_full = (sem("z_arg_ready"), sem("z_rooted"), sem("z_normed"),
                                                          sem("z_xT_full"), sem("z_xT_taken"), sem("z_k_full"))
        gates, scanned, h_full, ready2, rooted2, based, done = (sem("z_gates"), sem("z_scanned"), sem("z_h_full"),
                                                                sem("z_arg2_ready"), sem("z_rooted2"), sem("z_based"), sem("z_done"))
        chain, gchain = sem("z_vector_steps"), sem("z_gpsimd_steps")

        def col(name):
            return ins[name].rearrange("(p a) -> p a", a=1)

        def row(name):
            t = ins[name]
            return bass.AP(tensor=t.tensor, offset=t.offset, ap=[[0, P], [1, E]])

        with nc.Block() as block:
            @block.sync
            def _(sp):
                for dst, src in ((wz[:], ins["L0_attn_b_Wz"]), (wh[:], ins["L0_attn_b_Wh"]), (cols[:, 0:1], col("L0_attn_b_bz")),
                                 (cols[:, 1:2], col("L0_attn_b_bh")), (gamma[:, 0, :], row("L0_attn_b_gamma")),
                                 (gamma[:, 1, :], row("L0_attn_b_gamma")), (beta[:, 0, :], row("L0_attn_b_beta")),
                                 (beta[:, 1, :], row("L0_attn_b_beta"))):
                    sp.dma_start(dst, src).then_inc(loaded, 16)
                sp.wait_ge(loaded, 128)

            @block.vector
            def _(dve):
                dve.wait_ge(loaded, 128)
                nc.vector.tensor_scalar(cols[:, 2:3], cols[:, 0:1], -1.0, None, ALU.mult).then_inc(setup, 1)
                nc.vector.memset(half[:], -0.5).then_inc(setup, 1)

        def tile(b, t):
            return xres[:, bass.ds(2 * b + t, 1), :].rearrange("p a e -> p (a e)")

        def tiles(b):
            return xres[:, bass.ds(2 * b, 2), :].rearrange("p t e -> p (t e)")

        def flat(t):
            return t.rearrange("p t e -> p (t e)")

        with nc.Block() as block:
            @block.vector
            def _(dve):
                ch = Chain(dve, chain)

                def head(b, q):
                    for t in range(2):
                        last = ch.mark(nc.vector.bn_stats(stats[:, q, t, :], tile(b, t)))
                    ch.wait(last)
                    moments(nc, ch, stats[:, q], mv[:, q])
                    nc.vector.tensor_scalar(arg[:, q, :], mv[:, q, 3, :], 0.25, EPS, ALU.mult, ALU.add).then_inc(ready, 1)
                    dve.wait_ge(rooted, b + 1)
                    if not (isinstance(b, int) and b < 2):
                        dve.wait_ge(based, b - 1)
                    for t in range(2):
                        last = nc.vector.tensor_scalar(xl[:, q, t, :], tile(b, t), mv[:, q, 0, t:t + 1], rs[:, q, t:t + 1],
                                                       ALU.subtract, ALU.mult)
                    last.then_inc(normed, 1)

                def scan(b, q):
                    dve.wait_ge(gates, b + 1)
                    ch.step(nc.vector.tensor_scalar(relu[:], bk[q][:, S:2 * S], cols[:, 1:2], 0.0, ALU.add, ALU.max))
                    ch.step(nc.vector.scalar_tensor_tensor(relu[:], sg[:, q, :], 0.5, relu[:], ALU.min, ALU.add))
                    ch.step(nc.vector.tensor_tensor(val[:], z[:, q, :], relu[:], ALU.mult))
                    if not (isinstance(b, int) and b < 2):
                        dve.wait_ge(h_full, b - 1)
                    nc.vector.tensor_tensor_scan(hs[:, q, :], keep[:, q, :], val[:], 0.0, ALU.mult, ALU.add).then_inc(scanned, 1)

                def norm(b, q):
                    dve.wait_ge(h_full, b + 1)
                    for t in range(2):
                        last = ch.mark(nc.vector.bn_stats(stats2[:, q, t, :], bh[q][:, t * P:(t + 1) * P]))
                    ch.wait(last)
                    moments(nc, ch, stats2[:, q], mv2[:, q])
                    nc.vector.tensor_scalar(arg2[:, q, :], mv2[:, q, 3, :], 0.25, EPS, ALU.mult, ALU.add).then_inc(ready2, 1)

                def finish(b, q):
                    dve.wait_ge(rooted2, b + 1)
                    for t in range(2):
                        last = ch.mark(nc.vector.tensor_scalar(nh[:, t, :], bh[q][:, t * P:(t + 1) * P], mv2[:, q, 0, t:t + 1],
                                                               rs2[:, q, t:t + 1], ALU.subtract, ALU.mult))
                    ch.wait(last)
                    ch.step(nc.vector.tensor_tensor(nh[:], nh[:], gamma[:], ALU.mult))
                    dve.wait_ge(based, b + 1)
                    nc.vector.tensor_tensor(tiles(b), flat(nh[:]), flat(base[:, q, :, :]), ALU.add).then_inc(done, 1)

                HEAD, SCAN, NORM, FIN = 8, 3, 8, 3
                head(0, 0)
                head(1, 1)
                scan(0, 0)
                before = 2 * HEAD + SCAN

                def pair(b):
                    norm(b, 0)
                    scan(b + 1, 1)
                    head(b + 2, 0)
                    finish(b, 0)
                    norm(b + 1, 1)
                    scan(b + 2, 0)
                    head(b + 3, 1)
                    finish(b + 1, 1)

                pair(0)
                with dve.Fori(1, B // 2 - 1) as it:
                    ch.start(it * (2 * (HEAD + SCAN + NORM + FIN)) + before)
                    pair(it * 2)
                    assert ch.n == 2 * (HEAD + SCAN + NORM + FIN)
                ch.start((B // 2 - 1) * (2 * (HEAD + SCAN + NORM + FIN)) + before)
                norm(B - 2, 0)
                scan(B - 1, 1)
                finish(B - 2, 0)
                norm(B - 1, 1)
                finish(B - 1, 1)
                dve.wait_ge(done, B)

            @block.gpsimd
            def _(pool):
                ch = Chain(pool, gchain)

                def first(b, q):
                    pool.wait_ge(ready, b + 1)
                    nc.gpsimd.tensor_tensor(rs[:, q, :], arg[:, q, :], half[:], ALU.pow).then_inc(rooted, 1)

                def second(b, q):
                    pool.wait_ge(normed, b + 1)
                    if not (isinstance(b, int) and b < 2):
                        pool.wait_ge(done, b - 1)
                    ch.step(nc.gpsimd.tensor_tensor(flat(base[:, q, :, :]), flat(xl[:, q, :, :]), tiles(b), ALU.add))
                    pool.wait_ge(x_full, b + 1)
                    nc.gpsimd.tensor_tensor(base[:, q, :, :], base[:, q, :, :], beta[:], ALU.add).then_inc(based, 1)

                def third(b, q):
                    pool.wait_ge(ready2, b + 1)
                    nc.gpsimd.tensor_tensor(rs2[:, q, :], arg2[:, q, :], half[:], ALU.pow).then_inc(rooted2, 1)

                first(0, 0)
                first(1, 1)
                second(0, 0)
                second(1, 1)
                with pool.Fori(0, B // 2 - 1) as it:
                    ch.start(it * 2 + 2)
                    b = it * 2
                    third(b, 0)
                    first(b + 2, 0)
                    second(b + 2, 0)
                    third(b + 1, 1)
                    first(b + 3, 1)
                    second(b + 3, 1)
                third(B - 2, 0)
                third(B - 1, 1)

            @block.tensor
            def _(pe):
                def gates_of(b, q):
                    pe.wait_ge(normed, b + 1)
                    for t in range(2):
                        last = nc.tensor.transpose(bx[q][:, t * P:(t + 1) * P], xl[:, q, t, :], ident[:])
                    last.then_inc(x_full, 1)
                    pe.wait_ge(x_taken, b + 1)
                    if not (isinstance(b, int) and b < 2):
                        pe.wait_ge(scanned, b - 1)
                    nc.tensor.matmul(bk[q][:, 0:S], wz[:], xT[:, q, :], start=True, stop=True)
                    nc.tensor.matmul(bk[q][:, S:2 * S], wh[:], xT[:, q, :], start=True, stop=True).then_inc(k_full, 1)

                def back(b, q):
                    pe.wait_ge(scanned, b + 1)
                    if not (isinstance(b, int) and b < 2):
                        pe.wait_ge(done, b - 1)
                    for t in range(2):
                        last = nc.tensor.transpose(bh[q][:, t * P:(t + 1) * P], hs[:, q, t * P:(t + 1) * P], ident[:])
                    last.then_inc(h_full, 1)

                gates_of(0, 0)
                gates_of(1, 1)
                back(0, 0)
                back(1, 1)
                with pe.Fori(1, B // 2) as it:
                    b = it * 2
                    gates_of(b, 0)
                    back(b, 0)
                    gates_of(b + 1, 1)
                    back(b + 1, 1)

            @block.scalar
            def _(act):
                def chunk(b, q):
                    act.wait_ge(x_full, b + 1)
                    if not (isinstance(b, int) and b < 2):
                        act.wait_ge(scanned, b - 1)
                    nc.scalar.copy(xT[:, q, :], bx[q][:, 0:2 * P]).then_inc(x_taken, 1)
                    act.wait_ge(k_full, b + 1)
                    nc.scalar.activation(z[:, q, :], bk[q][:, 0:S], ACT.Sigmoid, bias=cols[:, 0:1])
                    nc.scalar.activation(keep[:, q, :], bk[q][:, 0:S], ACT.Sigmoid, bias=cols[:, 2:3], scale=-1.0)
                    nc.scalar.activation(sg[:, q, :], bk[q][:, S:2 * S], ACT.Sigmoid, bias=cols[:, 1:2]).then_inc(gates, 1)

                chunk(0, 0)
                chunk(1, 1)
                with act.Fori(1, B // 2) as it:
                    chunk(it * 2, 0)
                    chunk(it * 2 + 1, 1)


_INS = ["L0_attn_a_x", "L0_attn_a_rel_pos", "L0_attn_a_in_proj_w", "L0_attn_a_in_proj_b", "L0_attn_a_out_w",
        "L0_attn_a_out_b", "L0_attn_a_w1", "L0_attn_a_b1", "L0_attn_a_w2", "L0_attn_a_b2", "L0_attn_a_ln1_g",
        "L0_attn_a_ln1_b", "L0_attn_a_ln2_g", "L0_attn_a_ln2_b", "L0_attn_b_Wz", "L0_attn_b_bz", "L0_attn_b_Wh",
        "L0_attn_b_bh", "L0_attn_b_gamma", "L0_attn_b_beta", "L0_ffn_router_w", "L0_ffn_gate_w", "L0_ffn_gate_b",
        "L0_ffn_up_w", "L0_ffn_up_b", "L0_ffn_down_w", "L0_ffn_down_b"]


def kernel(**inputs):
    import numpy as _np
    import concourse.bacc as _bacc
    from concourse import mybir as _mybir
    from concourse.bass_utils import run_bass_kernel_spmd as _run

    nc = _bacc.Bacc("TRN2", target_bir_lowering=False, num_devices=1)
    arrays, args = {}, {}
    for name in _INS:
        a = _np.ascontiguousarray(inputs[name])
        arrays[f"in_{name}"] = a
        args[name] = nc.dram_tensor(f"in_{name}", a.shape, _mybir.dt.from_np(a.dtype), kind="ExternalInput").ap()
    shape = inputs["L0_attn_a_x"].shape
    out = nc.dram_tensor("out", shape, _mybir.dt.float32, kind="ExternalOutput").ap()
    build(nc, args, out)
    r = _run(nc, [arrays], core_ids=[0])
    return r.results[0]["out"]
```

```python
import concourse.bass as bass
from concourse import mybir
from contextlib import ExitStack, contextmanager

F32 = mybir.dt.float32
F32R = mybir.dt.float32r
BF16 = mybir.dt.bfloat16
F16 = mybir.dt.float16
I32 = mybir.dt.int32
ALU = mybir.AluOpType
ACT = mybir.ActivationFunctionType
AXX = mybir.AxisListType.X

P = 128
EPS = 1e-5
MASKED = -1.0e30


class Chain:

    def __init__(self, engine, semaphore):
        self.engine, self.semaphore, self.base, self.n = engine, semaphore, 0, 0

    def start(self, base):
        self.base, self.n = base, 0

    def mark(self, instruction):
        self.n += 1
        instruction.then_inc(self.semaphore, 1)
        return self.base + self.n

    def wait(self, value):
        self.engine.wait_ge(self.semaphore, value)

    def step(self, instruction):
        self.wait(self.mark(instruction))


def moments(nc, ch, stats, mom):
    ch.mark(nc.vector.tensor_tensor(mom[:, 0, :], stats[:, :, 1], stats[:, :, 4], ALU.add))
    ch.mark(nc.vector.tensor_tensor(mom[:, 1, :], stats[:, :, 1], stats[:, :, 4], ALU.subtract))
    ch.step(nc.vector.tensor_tensor(mom[:, 2, :], stats[:, :, 2], stats[:, :, 5], ALU.add))
    ch.mark(nc.vector.tensor_scalar(mom[:, 0, :], mom[:, 0, :], 0.5, None, ALU.mult))
    ch.step(nc.vector.tensor_tensor(mom[:, 1, :], mom[:, 1, :], mom[:, 1, :], ALU.mult))
    ch.step(nc.vector.scalar_tensor_tensor(mom[:, 3, :], mom[:, 2, :], 4.0 / P, mom[:, 1, :], ALU.mult, ALU.add))


@contextmanager
def phase(nc):
    made = []

    def sem(name):
        made.append(nc.alloc_semaphore(name=name))
        return made[-1]

    with ExitStack() as ctx:
        yield ctx, sem
    nc.all_engine_barrier()
    nc.clear_and_free_semaphores(made)
    nc.all_engine_barrier()


class Shapes:
    def __init__(self, x, rel_pos, w1, gate_w):
        self.B, self.S, self.E = x.shape
        self.H, self.ML = rel_pos.shape
        self.HD = self.E // self.H
        self.FF = w1.shape[0]
        self.NE, _, self.EF = gate_w.shape
        self.QT = self.S // P
        self.TILES = self.B * self.QT
        self.N = self.B * self.S
        self.BODY = 8
        self.SLOT_TILES = -(-(2 * self.TILES + self.NE - 1) // self.BODY) * self.BODY


def build(nc, ins, out):
    s = Shapes(ins["L0_attn_a_x"], ins["L0_attn_a_rel_pos"], ins["L0_attn_a_w1"], ins["L0_ffn_gate_w"])
    assert s.E == P and s.QT == 2 and s.H == 16 and s.HD == 8 and s.NE == 8
    with ExitStack() as kept:
        xres = kept.enter_context(nc.sbuf_tensor("xres", [P, s.TILES, s.E], F32))
        ident = kept.enter_context(nc.sbuf_tensor("ident", [P, P], F32))
        identb = kept.enter_context(nc.sbuf_tensor("identb", [P, P], BF16))
        with ExitStack() as mem:
            attention(nc, mem, s, ins, xres, ident, identb)
        with ExitStack() as mem:
            experts = expert_weights(nc, mem, s, ins, ident)
            normed_dram = nc.dram_tensor("normed_rows", (s.N, s.E), F32, kind="Internal").ap()
            slot_dram = nc.dram_tensor("slot_rows", (s.SLOT_TILES * P, s.E), F32, kind="Internal").ap()
            with ExitStack() as routes:
                share, slot = mixture(nc, routes, s, "first_", xres, ident, experts, normed_dram, slot_dram)
                recurrence(nc, s, ins, xres, ident, share, slot, slot_dram)
            with ExitStack() as routes:
                share, slot = mixture(nc, routes, s, "second_", xres, ident, experts, normed_dram, slot_dram)
                combine(nc, s, xres, share, slot, slot_dram)
        store(nc, s, out, xres)


def store(nc, s, out, xres):
    with ExitStack() as ctx:
        stored = ctx.enter_context(nc.semaphore("stored"))
        with nc.Block() as block:
            @block.sync
            def _(sp):
                sp.dma_start(out.rearrange("b (t p) e -> p (b t) e", p=P), xres[:]).then_inc(stored, 16)
                sp.wait_ge(stored, 16)


def attention(nc, ctx, s, ins, xres, ident, identb):
    H, HD, FF, B = s.H, s.HD, s.FF, s.B
    AUG = 64
    PAIRS = H // 2
    KROWS, XROWS = 6 * HD, 6 * HD + 2
    VW = 3 * (HD + 1)
    BK = 3 * P

    def sb(name, shape, dt=F32):
        return ctx.enter_context(nc.sbuf_tensor(name, shape, dt))

    def sem(name):
        return ctx.enter_context(nc.semaphore(name))

    wqkv = sb("wqkv", [P, 3 * s.E])
    bqkv = sb("bqkv", [P, 3 * s.E])
    wo = sb("wo", [P, s.E])
    outb = sb("outb", [P, s.E])
    w1 = sb("w1", [P, FF])
    b1 = sb("b1", [P, FF // P])
    w2 = sb("w2", [P, FF // P, s.E])
    b2 = sb("b2", [P, s.E])
    bias32 = sb("bias32", [P, H, BK])
    biasb = sb("biasb", [P, H, 2 * P], BF16)
    neghalf = sb("neghalf", [P, 4])
    unit = sb("unit", [P, 2, s.E])
    aug = sb("aug", [P, 2, 2, 2, H, AUG], BF16)
    vaug = sb("vaug", [P, 2, H, 3, HD + 1], BF16)

    x_dram = ins["L0_attn_a_x"].rearrange("b (t p) e -> p (b t) e", p=P)

    with ExitStack() as c2:
        def sb2(name, shape, dt=F32):
            return c2.enter_context(nc.sbuf_tensor(name, shape, dt))

        def sem2(name):
            return c2.enter_context(nc.semaphore(name))

        wrow = sb2("wrow", [P, 8, s.E])
        w2row = sb2("w2row", [P, FF])
        gcol = sb2("gcol", [P, 4])
        b1ld = sb2("b1ld", [P, FF // P])
        inb = sb2("inb", [P, 3 * s.E])
        ones = sb2("ones", [P, P])
        lnb1 = sb2("lnb1", [P, P])
        anti = sb2("anti", [P, P])
        relpad = sb2("relpad", [H, 3 * P])
        hank = sb2("hank", [P, H, 2 * P])
        pw = [c2.enter_context(nc.psum_tensor(f"pw{i}", [P, 512], F32)) for i in range(4)]
        scratch = nc.dram_tensor("rel_padded", (H, 3 * P), F32, kind="Internal").ap()
        hankel = bass.AP(tensor=scratch.tensor, offset=0, ap=[[1, P], [3 * P, H], [1, 2 * P]])

        loaded = sem2("weights_loaded")
        rel_in, rel_out, rel_tab = sem2("rel_loaded"), sem2("rel_stored"), sem2("hankel_loaded")
        x_in = sem2("x_loaded")
        filled, full, taken = sem2("filled"), sem2("pw_full"), sem2("pw_taken")
        padded = sem2("rel_padded_set")
        vchain = sem2("vector_steps")
        gchain = sem2("gpsimd_steps")
        NLOADS = 14

        def col(name):
            return ins[name].rearrange("(p a) -> p a", a=1)

        def row(name):
            t = ins[name]
            return bass.AP(tensor=t.tensor, offset=t.offset, ap=[[0, P], [1, t.shape[0]]])

        with nc.Block() as block:
            @block.sync
            def _(sp):
                sp.wait_ge(padded, 1)
                sp.dma_start(relpad[:, P - 1:P - 1 + s.S], ins["L0_attn_a_rel_pos"][:, 0:s.S]).then_inc(rel_in, 16)
                sp.wait_ge(rel_in, 16)
                sp.dma_start(scratch, relpad[:]).then_inc(rel_out, 16)
                sp.wait_ge(rel_out, 16)
                sp.dma_start(hank[:], hankel).then_inc(rel_tab, 16)
                for q in range(4):
                    n = s.TILES // 4
                    sp.dma_start(xres[:, q * n:(q + 1) * n, :], x_dram[:, q * n:(q + 1) * n, :]).then_inc(x_in, 16)
                sp.wait_ge(x_in, 64)
                sp.wait_ge(rel_tab, 16)

            @block.scalar
            def _(act):
                loads = [
                    (wrow[:, 0:3, :], ins["L0_attn_a_in_proj_w"].rearrange("(c p) e -> p c e", p=P)),
                    (wrow[:, 3, :], ins["L0_attn_a_out_w"]),
                    (wrow[:, 4:8, :], ins["L0_attn_a_w1"].rearrange("(c p) e -> p c e", p=P)),
                    (w2row[:], ins["L0_attn_a_w2"]),
                    (gcol[:, 0:1], col("L0_attn_a_ln1_g")), (gcol[:, 1:2], col("L0_attn_a_ln1_b")),
                    (gcol[:, 2:3], col("L0_attn_a_ln2_g")), (gcol[:, 3:4], col("L0_attn_a_ln2_b")),
                    (inb[:], row("L0_attn_a_in_proj_b")), (outb[:], row("L0_attn_a_out_b")),
                    (b2[:], row("L0_attn_a_b2")),
                ] + [(b1ld[:, c:c + 1], ins["L0_attn_a_b1"][c * P:(c + 1) * P].rearrange("(p a) -> p a", a=1))
                     for c in range(FF // P)]
                for dst, src in loads:
                    act.dma_start(dst, src).then_inc(loaded, 16)
                act.wait_ge(loaded, 16 * len(loads))
                assert len(loads) == NLOADS + 1

            @block.gpsimd
            def _(pool):
                ch = Chain(pool, gchain)
                nc.gpsimd.memset(relpad[:], MASKED).then_inc(padded, 1)
                ch.step(nc.gpsimd.memset(ident[:], 0.0))
                ch.step(nc.gpsimd.affine_select(out=ident[:], in_=ident[:], compare_op=ALU.not_equal, fill=1.0,
                                                base=0, pattern=[[-1, P]], channel_multiplier=1))
                ch.step(nc.gpsimd.memset(anti[:], 0.0))
                nc.gpsimd.affine_select(out=anti[:], in_=anti[:], compare_op=ALU.not_equal, fill=1.0,
                                        base=-(P - 1), pattern=[[1, P]], channel_multiplier=1).then_inc(filled, 1)
                ch.step(nc.gpsimd.memset(aug[:], 0.0))
                for q in range(2):
                    for t in range(2):
                        ch.step(nc.gpsimd.memset(aug[:, q, 1, t, :, KROWS:XROWS], 1.0))
                ch.step(nc.gpsimd.memset(vaug[:], 0.0))
                for t in range(2):
                    ch.step(nc.gpsimd.memset(vaug[:, t, :, 0, HD:HD + 1], 1.0))
                ch.step(nc.gpsimd.memset(unit[:], 1.0))
                nc.gpsimd.memset(neghalf[:], -0.5).then_inc(filled, 1)

            @block.vector
            def _(dve):
                ch = Chain(dve, vchain)
                dve.wait_ge(filled, 1)
                ch.step(nc.vector.tensor_copy(identb[:], ident[:]))
                dve.wait_ge(loaded, 16 * (NLOADS + 1))
                ch.step(nc.vector.memset(ones[:], 1.0))
                nc.vector.tensor_scalar(lnb1[:], ones[:], gcol[:, 1:2], None, ALU.mult).then_inc(filled, 1)
                dve.wait_ge(full, 1)
                ch.step(nc.vector.tensor_copy(wqkv[:], pw[0][:, 0:3 * s.E]))
                nc.vector.tensor_copy(wo[:], pw[0][:, 3 * s.E:4 * s.E]).then_inc(taken, 1)
                dve.wait_ge(full, 2)
                ch.step(nc.vector.tensor_copy(w1[:], pw[1][:]))
                nc.vector.tensor_copy(w2[:].rearrange("p c e -> p (c e)"), pw[2][:]).then_inc(taken, 1)
                dve.wait_ge(full, 3)
                ch.step(nc.vector.tensor_tensor(bqkv[:], pw[3][:, 0:3 * s.E], inb[:], ALU.add))
                ch.step(nc.vector.tensor_scalar(bqkv[:, 0:s.E], bqkv[:, 0:s.E], HD ** -0.5, None, ALU.mult))
                ch.step(nc.vector.tensor_tensor(b1[:], pw[0][:, 0:FF // P], b1ld[:], ALU.add))
                ch.step(nc.vector.tensor_scalar(wqkv[:], wqkv[:], gcol[:, 0:1], None, ALU.mult))
                ch.step(nc.vector.tensor_scalar(wqkv[:, 0:s.E], wqkv[:, 0:s.E], HD ** -0.5, None, ALU.mult))
                ch.step(nc.vector.tensor_scalar(w1[:], w1[:], gcol[:, 2:3], None, ALU.mult))
                for j in range(PAIRS):
                    dve.wait_ge(full, 4 + j)
                    src = pw[1 + j % 2][:].rearrange("p (h q) -> p h q", h=2)
                    ch.step(nc.vector.tensor_copy(bias32[:, 2 * j:2 * j + 2, 0:2 * P], src))
                    ch.step(nc.vector.tensor_copy(biasb[:, 2 * j:2 * j + 2, :], src))
                    nc.vector.tensor_copy(bias32[:, 2 * j:2 * j + 2, 2 * P:BK], src[:, :, 0:P]).then_inc(taken, 1)

            @block.tensor
            def _(pe):
                pe.wait_ge(loaded, 16 * (NLOADS + 1))
                pe.wait_ge(filled, 3)
                for c in range(4):
                    last = nc.tensor.transpose(pw[0][:, c * P:(c + 1) * P], wrow[:, c, :], ident[:])
                last.then_inc(full, 1)
                for c in range(4):
                    nc.tensor.transpose(pw[1][:, c * P:(c + 1) * P], wrow[:, 4 + c, :], ident[:])
                for c in range(4):
                    last = nc.tensor.transpose(pw[2][:, c * P:(c + 1) * P], w2row[:, c * P:(c + 1) * P], ident[:])
                last.then_inc(full, 1)
                pe.wait_ge(taken, 2)
                nc.tensor.matmul(pw[3][:, 0:3 * s.E], lnb1[:], wqkv[:], start=True, stop=True)
                for c in range(FF // P):
                    last = nc.tensor.matmul(pw[0][:, c:c + 1], w1[:, c * P:(c + 1) * P], gcol[:, 3:4],
                                            start=True, stop=True)
                last.then_inc(full, 1)
                pe.wait_ge(rel_tab, 16)
                for j in range(PAIRS):
                    if j >= 2:
                        pe.wait_ge(taken, 2 + j - 1)
                    nc.tensor.matmul(pw[1 + j % 2][:], anti[:],
                                     hank[:, 2 * j:2 * j + 2, :].rearrange("p h q -> p (h q)"),
                                     start=True, stop=True).then_inc(full, 1)

    xn = sb("xn", [P, 2, s.E])
    xnT = sb("xnT", [P, 2 * P])
    xlb = sb("xlb", [P, 2, 2, s.E])
    qkv = sb("qkv", [P, 2, 3, 2, s.E])
    rest = sb("rest", [P, 2, 2, s.E])
    vrest = sb("vrest", [P, 2, s.E])
    qT = sb("qT", [P, 2, PAIRS, 2 * P], BF16)
    kT = sb("kT", [P, 2, PAIRS, 2 * P], BF16)
    stats = sb("stats", [P, 2, 6])
    mv = sb("mv", [P, 2, 4, 2])
    arg = sb("arg", [P, 2, 2])
    rs = sb("rs", [P, 2, 2, 2])
    stats2 = sb("stats2", [P, 2, 6])
    mv2 = sb("mv2", [P, 4, 2])
    arg2 = sb("arg2", [P, 2])
    rs2 = sb("rs2", [P, 2])
    mx = sb("mx", [P, H, 3])
    mq = sb("mq", [P, 2, H])
    mrest = sb("mrest", [P, 2, H])
    ebuf = sb("ebuf", [P, 2, 2, BK])
    p32 = sb("p32", [P, 2, 2, BK])
    phi = sb("phi", [P, 4, 2, BK], F16)
    plo = sb("plo", [P, 4, 2, BK], F16)
    osum = sb("osum", [P, 2, H, HD + 1])
    rden = sb("rden", [P, 2, H, 1])
    onrm = sb("onrm", [P, 2, s.E])
    oT = sb("oT", [P, 2 * P])
    y1 = sb("y1", [P, 2, s.E])
    xb2 = sb("xb2", [P, 2, s.E])
    ysum = sb("ysum", [P, 2, s.E])
    xm = sb("xm", [P, 2, s.E])
    xmT = sb("xmT", [P, 2 * P])
    hT = sb("hT", [P, FF // P, 2 * P])

    score_banks = ctx.enter_context(nc.psum_tensor("score_banks", [P, 2, 512], F32))
    max_banks = ctx.enter_context(nc.psum_tensor("max_banks", [P, 2, 512], F32))
    bankT = ctx.enter_context(nc.psum_tensor("bankT", [P, 512], F32))
    bankW = ctx.enter_context(nc.psum_tensor("bankW", [P, 512], F32))
    bankO = [ctx.enter_context(nc.psum_tensor(f"bankO{t}", [P, 512], F32)) for t in range(2)]

    T_full, T_free, W_full, W_free = sem("T_full"), sem("T_free"), sem("W_full"), sem("W_free")
    scores_full, maxed_full, maxed_free = sem("scores_full"), sem("maxed_full"), sem("maxed_free")
    kT_full, kT_taken, maxT_full, maxT_taken = sem("kT_full"), sem("kT_taken"), sem("maxT_full"), sem("maxT_taken")
    biased, exped, lowed, weighed = sem("scores_biased"), sem("exp_done"), sem("low_done"), sem("pv_done")
    O_free = sem("O_free")
    arg1_ready, rs1_ready, xn_ready, xlb_ready, xl_ready = (sem("arg1_ready"), sem("rs1_ready"), sem("xn_ready"),
                                                            sem("xlb_ready"), sem("xl_ready"))
    v_ready, vaug_ready = sem("v_ready"), sem("vaug_ready")
    aug_ready, aug_copied, rest_ready, max_ready = sem("aug_ready"), sem("aug_copied"), sem("rest_ready"), sem("max_ready")
    on_ready, y1_ready, arg2_ready, rs2_ready = sem("on_ready"), sem("y1_ready"), sem("arg2_ready"), sem("rs2_ready")
    xm_ready, ysum_ready, x_done = sem("xm_ready"), sem("ysum_ready"), sem("x_done")
    vchain, gchain = sem("attn_vector_steps"), sem("attn_gpsimd_steps")

    def attends(b):
        return not isinstance(b, int) or 0 <= b < B

    def outputs(b):
        return not isinstance(b, int) or 1 <= b

    def maximises(b):
        return not isinstance(b, int) or -1 <= b <= B - 2

    def prepares(b):
        return not isinstance(b, int) or -2 <= b <= B - 3

    T_USES = ("oT", "project", "xmT", "up", "q")
    W_USES = ("att", "norm", "project", "up", "down", "q")

    def uses_of(order, b):
        has = {"oT": outputs, "att": outputs, "xmT": outputs, "up": outputs, "down": outputs}
        return [u for u in order if has.get(u, prepares)(b)]

    def use(order, name, b):
        if isinstance(b, int):
            return sum(len(uses_of(order, c)) for c in range(-2, b)) + uses_of(order, b).index(name)
        return sum(len(uses_of(order, c)) for c in range(-2, 1)) + len(order) * (b - 1) + order.index(name)

    def useT(name, b):
        return use(T_USES, name, b)

    def useW(name, b):
        return use(W_USES, name, b)

    def some(n):
        return not isinstance(n, int) or n > 0

    FIRST, SECOND, THIRD = ((0, 1, 2), (0, 3, 5)), ((3, 4), (1, 4)), (5, 2)

    def slot(q, which, i):
        return aug[:, q, which, :, :, i * HD:(i + 1) * HD].rearrange("p t h d -> p (t h) d")

    def heads(t):
        return t.rearrange("p t (h d) -> p (t h) d", d=HD)

    def tiles(b):
        return xres[:, bass.ds(2 * b, 2), :]

    def tile(b, t):
        return xres[:, bass.ds(2 * b + t, 1), :].rearrange("p a e -> p (a e)")

    with nc.Block() as block:

        @block.tensor
        def _(pe):
            def takeT(name, b):
                n = useT(name, b)
                if some(n):
                    pe.wait_ge(T_free, n)

            def takeW(name, b):
                n = useW(name, b)
                if some(n):
                    pe.wait_ge(W_free, n)

            def norm_T(b):
                pe.wait_ge(xn_ready, b + 3)
                takeW("norm", b)
                for t in range(2):
                    last = nc.tensor.transpose(bankW[:, t * P:(t + 1) * P], xn[:, t, :], ident[:])
                last.then_inc(W_full, 1)

            def project_0(b):
                pe.wait_ge(W_free, useW("norm", b) + 1)
                takeT("project", b)
                nc.tensor.matmul(bankT[:, 0:3 * s.E], xnT[:, 0:P], wqkv[:], start=True, stop=True).then_inc(T_full, 1)

            def project_1(b):
                takeW("project", b)
                nc.tensor.matmul(bankW[:, 0:3 * s.E], xnT[:, P:2 * P], wqkv[:], start=True, stop=True).then_inc(W_full, 1)

            def aug_T(bank, q, which, t):
                dst = bank.bitcast(BF16).rearrange("p (g q) -> p g q", g=PAIRS)
                for g in range(PAIRS):
                    last = nc.tensor.transpose(dst[:, g, :], aug[:, q, which, t, 2 * g:2 * g + 2, :].rearrange("p h a -> p (h a)"),
                                               identb[:])
                return last

            def q_T(b, p):
                pe.wait_ge(aug_ready, 2 * b + 5)
                pe.wait_ge(aug_copied, 2 * b + 5)
                takeT("q", b)
                aug_T(bankT[:], p, 0, 0).then_inc(T_full, 1)
                takeW("q", b)
                aug_T(bankW[:], p, 0, 1).then_inc(W_full, 1)

            def k_T(b, p):
                pe.wait_ge(aug_ready, 2 * b + 6)
                pe.wait_ge(aug_copied, 2 * b + 6)
                if maximises(b):
                    pe.wait_ge(maxed_free, 8 * b + 16)
                for t in range(2):
                    aug_T(max_banks[:, t, :], p, 1, t).then_inc(kT_full, 1)

            def max_T(b, p):
                pe.wait_ge(max_ready, b + 2)
                if attends(b):
                    pe.wait_ge(biased, 8 * b + 9)
                for t in range(2):
                    aug_T(score_banks[:, t, :], 1 - p, 0, t).then_inc(maxT_full, 1)

            def scores_for_max(b, q, j):
                r = max_banks
                if j == 0:
                    pe.wait_ge(T_free, useT("q", b - 2) + 1)
                    pe.wait_ge(W_free, useW("q", b - 2) + 1)
                    pe.wait_ge(kT_taken, 2 * b + 2)
                if some(8 * b + j):
                    pe.wait_ge(maxed_free, 8 * b + j)
                for hh in range(2):
                    h = 2 * j + hh
                    nc.tensor.matmul(r[:, hh, 0:P], biasb[:, h, P:2 * P], identb[:], start=True, stop=False,
                                     skip_group_check=True)
                    nc.tensor.matmul(r[:, hh, P:2 * P], biasb[:, h, 0:P], identb[:], start=False, stop=False,
                                     skip_group_check=True)
                    nc.tensor.matmul(r[:, hh, 2 * P:BK], biasb[:, h, 0:P], identb[:], start=False, stop=False,
                                     skip_group_check=True)
                for hh in range(2):
                    rows = slice(AUG * hh, AUG * hh + KROWS)
                    nc.tensor.matmul(r[:, hh, 0:2 * P], qT[rows, q, j, P:2 * P], kT[rows, q, j, :],
                                     start=False, stop=True, skip_group_check=True)
                for hh in range(2):
                    rows = slice(AUG * hh, AUG * hh + KROWS)
                    last = nc.tensor.matmul(r[:, hh, 2 * P:BK], qT[rows, q, j, 0:P], kT[rows, q, j, 0:P],
                                            start=False, stop=True, skip_group_check=True)
                last.then_inc(maxed_full, 1)

            def scores(b, p, j):
                r = score_banks
                if j == 0:
                    pe.wait_ge(maxT_taken, 2 * b + 2)
                pe.wait_ge(biased, 8 * b + j + 1)
                for hh in range(2):
                    rows = slice(AUG * hh, AUG * hh + XROWS)
                    nc.tensor.matmul(r[:, hh, 0:2 * P], kT[rows, p, j, 0:P], qT[rows, p, j, :], start=True, stop=True)
                for hh in range(2):
                    rows = slice(AUG * hh, AUG * hh + XROWS)
                    last = nc.tensor.matmul(r[:, hh, 2 * P:BK], kT[rows, p, j, P:2 * P], qT[rows, p, j, P:2 * P],
                                            start=True, stop=True)
                last.then_inc(scores_full, 1)

            def weigh(b, j):
                if j == 0:
                    pe.wait_ge(vaug_ready, b + 1)
                    pe.wait_ge(O_free, b + 1)
                pe.wait_ge(lowed, 8 * b + j + 3)
                for hh in range(2):
                    h = 2 * j + hh
                    for t, blocks in ((0, ((0, 0),)), (1, ((P, 0), (2 * P, 1)))):
                        n = 2 * len(blocks)
                        i = 0
                        for part in (phi, plo):
                            for col, kt in blocks:
                                last = nc.tensor.matmul(bankO[t][:, h * VW:(h + 1) * VW], part[:, j % 4, hh, col:col + P],
                                                        vaug[:, kt, h, :, :].rearrange("p s d -> p (s d)"),
                                                        start=(i == 0), stop=(i == n - 1))
                                i += 1
                last.then_inc(weighed, 1)

            def out_T(b):
                pe.wait_ge(on_ready, b)
                takeT("oT", b)
                for t in range(2):
                    last = nc.tensor.transpose(bankT[:, t * P:(t + 1) * P], onrm[:, t, :], ident[:])
                last.then_inc(T_full, 1)

            def out_proj(b):
                pe.wait_ge(T_free, useT("oT", b) + 1)
                takeW("att", b)
                for t in range(2):
                    last = nc.tensor.matmul(bankW[:, t * P:(t + 1) * P], oT[:, t * P:(t + 1) * P], wo[:],
                                            start=True, stop=True)
                last.then_inc(W_full, 1)

            def mlp_T(b):
                pe.wait_ge(xm_ready, b)
                takeT("xmT", b)
                for t in range(2):
                    last = nc.tensor.transpose(bankT[:, t * P:(t + 1) * P], xm[:, t, :], ident[:])
                last.then_inc(T_full, 1)

            def mlp_up_0(b):
                pe.wait_ge(T_free, useT("xmT", b) + 1)
                takeW("up", b)
                for f in range(2):
                    last = nc.tensor.matmul(bankW[:, f * 2 * P:(f + 1) * 2 * P], w1[:, f * P:(f + 1) * P], xmT[:],
                                            start=True, stop=True)
                last.then_inc(W_full, 1)

            def mlp_up_1(b):
                takeT("up", b)
                for f in range(2):
                    last = nc.tensor.matmul(bankT[:, f * 2 * P:(f + 1) * 2 * P], w1[:, (2 + f) * P:(3 + f) * P], xmT[:],
                                            start=True, stop=True)
                last.then_inc(T_full, 1)

            def mlp_down(b):
                pe.wait_ge(T_free, useT("up", b) + 1)
                takeW("down", b)
                for t in range(2):
                    for f in range(FF // P):
                        last = nc.tensor.matmul(bankW[:, t * P:(t + 1) * P], hT[:, f, t * P:(t + 1) * P], w2[:, f, :],
                                                start=(f == 0), stop=(f == FF // P - 1))
                last.then_inc(W_full, 1)

            def body(b, p):
                if attends(b):
                    scores(b, p, 0)
                if maximises(b):
                    scores_for_max(b + 1, 1 - p, 0)
                if attends(b):
                    scores(b, p, 1)
                if maximises(b):
                    scores_for_max(b + 1, 1 - p, 1)
                if outputs(b):
                    out_T(b)
                if attends(b):
                    scores(b, p, 2)
                if maximises(b):
                    scores_for_max(b + 1, 1 - p, 2)
                if attends(b):
                    weigh(b, 0)
                if outputs(b):
                    out_proj(b)
                if attends(b):
                    scores(b, p, 3)
                if maximises(b):
                    scores_for_max(b + 1, 1 - p, 3)
                if attends(b):
                    weigh(b, 1)
                    scores(b, p, 4)
                if prepares(b):
                    norm_T(b)
                if maximises(b):
                    scores_for_max(b + 1, 1 - p, 4)
                if attends(b):
                    weigh(b, 2)
                if prepares(b):
                    project_0(b)
                if attends(b):
                    scores(b, p, 5)
                if maximises(b):
                    scores_for_max(b + 1, 1 - p, 5)
                if attends(b):
                    weigh(b, 3)
                if prepares(b):
                    project_1(b)
                if outputs(b):
                    mlp_T(b)
                if attends(b):
                    scores(b, p, 6)
                if maximises(b):
                    scores_for_max(b + 1, 1 - p, 6)
                if attends(b):
                    weigh(b, 4)
                if outputs(b):
                    mlp_up_0(b)
                    mlp_up_1(b)
                if attends(b):
                    scores(b, p, 7)
                if maximises(b):
                    scores_for_max(b + 1, 1 - p, 7)
                if attends(b):
                    weigh(b, 5)
                if outputs(b):
                    mlp_down(b)
                if prepares(b):
                    q_T(b, p)
                    k_T(b, p)
                if attends(b):
                    weigh(b, 6)
                if maximises(b):
                    max_T(b, p)
                if attends(b):
                    weigh(b, 7)

            for b in (-2, -1, 0):
                body(b, b % 2)
            with pe.Fori(0, (B - 4) // 2) as it:
                body(it * 2 + 1, 1)
                body(it * 2 + 2, 0)
            for b in (B - 3, B - 2, B - 1, B):
                body(b, b % 2)

        @block.vector
        def _(dve):
            ch = Chain(dve, vchain)

            def norm_stats(b, p):
                for t in range(2):
                    last = ch.mark(nc.vector.bn_stats(stats[:, t, :], tile(b + 2, t)))
                ch.wait(last)
                moments(nc, ch, stats, mv[:, p])
                nc.vector.tensor_scalar(arg[:, 0, :], mv[:, p, 3, :], 0.25, EPS, ALU.mult, ALU.add)
                nc.vector.tensor_scalar(arg[:, 1, :], mv[:, p, 3, :], 0.25 * (1.0 + EPS), EPS * EPS, ALU.mult, ALU.add).then_inc(arg1_ready, 1)

            def norm_apply(b, p):
                dve.wait_ge(rs1_ready, b + 3)
                for t in range(2):
                    last = nc.vector.tensor_scalar(xn[:, t, :], tile(b + 2, t), mv[:, p, 0, t:t + 1], rs[:, p, 1, t:t + 1],
                                                   ALU.subtract, ALU.mult)
                last.then_inc(xn_ready, 1)

            def normed_input(b, p):
                for t in range(2):
                    last = nc.vector.tensor_scalar(xlb[:, p, t, :], tile(b, t), mv[:, p, 0, t:t + 1], rs[:, p, 0, t:t + 1],
                                                   ALU.subtract, ALU.mult)
                last.then_inc(xl_ready, 1)

            def take_qkv_0(b, p):
                if some(b + 1):
                    dve.wait_ge(vaug_ready, b + 1)
                dve.wait_ge(T_full, useT("project", b) + 1)
                nc.vector.tensor_tensor(qkv[:, p, :, 0, :], bankT[:, 0:3 * s.E].rearrange("p (c e) -> p c e", c=3),
                                        bqkv[:].rearrange("p (c e) -> p c e", c=3), ALU.add).then_inc(T_free, 1)

            def take_qkv_1(b, p):
                dve.wait_ge(W_full, useW("project", b) + 1)
                nc.vector.tensor_tensor(qkv[:, p, :, 1, :], bankW[:, 0:3 * s.E].rearrange("p (c e) -> p c e", c=3),
                                        bqkv[:].rearrange("p (c e) -> p c e", c=3), ALU.add).then_inc(W_free, 1)
                dve.wait_ge(W_free, useW("project", b) + 1)
                dve.wait_ge(T_free, useT("project", b) + 1)
                dve.sem_inc(v_ready, 1)

            def split(b, p, which):
                x, r = heads(qkv[:, p, which, :, :]), heads(rest[:, which, :, :])
                first, second, third = FIRST[which][0], SECOND[which][0], THIRD[which]
                if some(b + 2):
                    dve.wait_ge(aug_copied, 2 * b + 3 + which)
                ch.step(nc.vector.tensor_copy(slot(p, which, first), x))
                ch.step(nc.vector.tensor_tensor(r, x, slot(p, which, first), ALU.subtract))
                dve.sem_inc(rest_ready, 1)
                ch.step(nc.vector.tensor_copy(slot(p, which, second), r))
                nc.vector.tensor_tensor(slot(p, which, third), r, slot(p, which, second), ALU.subtract).then_inc(aug_ready, 1)

            def take_q(b, p):
                dve.wait_ge(W_full, useW("q", b) + 1)
                nc.vector.tensor_copy(qT[:, p, :, P:2 * P],
                                      bankW[:].bitcast(BF16).rearrange("p (g q) -> p g q", g=PAIRS)).then_inc(W_free, 1)

            def take_k(b, p):
                dve.wait_ge(kT_full, 2 * b + 6)
                nc.vector.tensor_copy(kT[:, p, :, P:2 * P],
                                      max_banks[:, 1, :].bitcast(BF16).rearrange("p (g q) -> p g q", g=PAIRS)).then_inc(kT_taken, 1)

            def reduce_max(b, j):
                dve.wait_ge(maxed_full, 8 * b + j + 1)
                if j == 0 and some(b):
                    dve.wait_ge(max_ready, b)
                nc.vector.reduce_max(mx[:, 2 * j:2 * j + 2, :],
                                     max_banks[:, :, 0:BK].rearrange("p h (k c) -> p h k c", k=3), AXX).then_inc(maxed_free, 1)

            def take_max(b, q):
                dve.wait_ge(maxed_free, 8 * b + 8)
                nc.vector.tensor_tensor(mq[:, 1, :], mx[:, :, 0], mx[:, :, 1], ALU.max)
                ch.step(nc.vector.tensor_copy(mq[:, 0, :], mx[:, :, 2]))
                part = aug[:, q, 0, :, :, KROWS:XROWS]
                ch.step(nc.vector.tensor_scalar(part[:, :, :, 0], mq[:], -1.0, None, ALU.mult))
                nc.vector.scalar_tensor_tensor(part[:, :, :, 1], mq[:], -1.0, part[:, :, :, 0],
                                               ALU.mult, ALU.subtract).then_inc(max_ready, 1)

            def take_max_T(b, p):
                dve.wait_ge(maxT_full, 2 * b + 4)
                nc.vector.tensor_copy(qT[:, 1 - p, :, P:2 * P],
                                      score_banks[:, 1, :].bitcast(BF16).rearrange("p (g q) -> p g q", g=PAIRS)).then_inc(maxT_taken, 1)

            def add_mask(b, j):
                dve.wait_ge(scores_full, 8 * b + j + 1)
                if j >= 2:
                    dve.wait_ge(exped, 8 * b + j - 1)
                nc.vector.tensor_tensor(ebuf[:, j % 2, :, :], score_banks[:, :, 0:BK], bias32[:, 2 * j:2 * j + 2, :],
                                        ALU.add).then_inc(biased, 1)

            def normalise(b):
                dve.wait_ge(weighed, 8 * b + 8)
                for t in range(2):
                    last = nc.vector.reduce_sum(osum[:, t, :, :], bankO[t][:, 0:H * VW].rearrange(
                        "p (h s d) -> p h d s", h=H, s=3), AXX)
                last.then_inc(O_free, 1)
                dve.wait_ge(O_free, b + 2)
                ch.step(nc.vector.reciprocal(rden[:].rearrange("p t h a -> p (t h a)"),
                                             osum[:, :, :, HD].rearrange("p t h -> p (t h)")))
                nc.vector.tensor_tensor(heads(onrm[:]), osum[:, :, :, 0:HD].rearrange("p t h d -> p (t h) d"),
                                        rden[:].rearrange("p t h a -> p (t h) a").broadcast_to([P, 2 * H, HD]),
                                        ALU.mult).then_inc(on_ready, 1)

            def second_norm(b, p):
                dve.wait_ge(W_full, useW("att", b) + 1)
                dve.wait_ge(xlb_ready, b)
                ch.step(nc.vector.tensor_tensor(y1[:].rearrange("p t e -> p (t e)"), bankW[:, 0:2 * P],
                                                xlb[:, 1 - p, :, :].rearrange("p t e -> p (t e)"), ALU.add))
                dve.sem_inc(W_free, 1)
                dve.sem_inc(y1_ready, 1)
                for t in range(2):
                    last = ch.mark(nc.vector.bn_stats(stats2[:, t, :], y1[:, t, :]))
                ch.wait(last)
                moments(nc, ch, stats2, mv2)
                nc.vector.tensor_scalar(arg2[:], mv2[:, 3, :], 0.25, EPS, ALU.mult, ALU.add).then_inc(arg2_ready, 1)

            def second_apply(b):
                dve.wait_ge(rs2_ready, b)
                for t in range(2):
                    last = nc.vector.tensor_scalar(xm[:, t, :], y1[:, t, :], mv2[:, 0, t:t + 1], rs2[:, t:t + 1],
                                                   ALU.subtract, ALU.mult)
                last.then_inc(xm_ready, 1)

            def finish(b):
                dve.wait_ge(W_full, useW("down", b) + 1)
                dve.wait_ge(ysum_ready, b)
                nc.vector.tensor_tensor(tiles(b - 1).rearrange("p t e -> p (t e)"), bankW[:, 0:2 * P],
                                        ysum[:].rearrange("p t e -> p (t e)"), ALU.add).then_inc(x_done, 1)
                dve.wait_ge(x_done, b)
                dve.sem_inc(W_free, 1)

            def body(b, p):
                for j in range(PAIRS):
                    if prepares(b) and j == 5:
                        take_qkv_0(b, p)
                    if attends(b):
                        add_mask(b, j)
                    if maximises(b):
                        reduce_max(b + 1, j)
                    if outputs(b):
                        if j == 0:
                            normalise(b - 1)
                        if j == 3:
                            second_norm(b, p)
                        if j == 4:
                            second_apply(b)
                    if prepares(b):
                        if j == 1:
                            norm_stats(b, p)
                        if j == 2:
                            norm_apply(b, p)
                        if j == 5:
                            take_qkv_1(b, p)
                        if j == 5:
                            split(b, p, 0)
                        if j == 6:
                            split(b, p, 1)
                if maximises(b):
                    take_max(b + 1, 1 - p)
                if outputs(b):
                    finish(b)
                if prepares(b):
                    take_q(b, p)
                if attends(b + 1):
                    normed_input(b + 1, 1 - p)
                if prepares(b):
                    take_k(b, p)
                if maximises(b):
                    take_max_T(b, p)

            dve.sem_inc(O_free, 1)
            dve.sem_inc(biased, 1)
            for b in (-2, -1, 0):
                body(b, b % 2)
            before = ch.base + ch.n
            with dve.Fori(0, (B - 4) // 2) as it:
                for u in range(2):
                    b = it * 2 + 1 + u
                    per = 26
                    ch.start((b - 1) * per + before)
                    body(b, 1 - u)
                    assert ch.n == per, ch.n
            ch.start((B - 4) * per + before)
            for b in (B - 3, B - 2, B - 1, B):
                body(b, b % 2)

        @block.scalar
        def _(act):
            def take_norm(b):
                act.wait_ge(W_full, useW("norm", b) + 1)
                nc.scalar.copy(xnT[:], bankW[:, 0:2 * P]).then_inc(W_free, 1)

            def take_q(b, p):
                act.wait_ge(T_full, useT("q", b) + 1)
                nc.scalar.copy(qT[:, p, :, 0:P],
                               bankT[:].bitcast(BF16).rearrange("p (g q) -> p g q", g=PAIRS)).then_inc(T_free, 1)

            def take_k(b, p):
                act.wait_ge(kT_full, 2 * b + 5)
                nc.scalar.copy(kT[:, p, :, 0:P],
                               max_banks[:, 0, :].bitcast(BF16).rearrange("p (g q) -> p g q", g=PAIRS)).then_inc(kT_taken, 1)

            def take_max_T(b, p):
                act.wait_ge(maxT_full, 2 * b + 3)
                nc.scalar.copy(qT[:, 1 - p, :, 0:P],
                               score_banks[:, 0, :].bitcast(BF16).rearrange("p (g q) -> p g q", g=PAIRS)).then_inc(maxT_taken, 1)

            def repeat_parts(b, p, which):
                act.wait_ge(v_ready, b + 3)
                for i in FIRST[which][1:]:
                    nc.scalar.copy(slot(p, which, i), heads(qkv[:, p, which, :, :]))
                act.wait_ge(rest_ready, 2 * b + 5 + which)
                nc.scalar.copy(slot(p, which, SECOND[which][1]), heads(rest[:, which, :, :])).then_inc(aug_copied, 1)

            def exponentials(b, j):
                use = 8 * b + j
                act.wait_ge(biased, use + 2)
                act.wait_ge(lowed, use + 1)
                nc.scalar.activation(p32[:, j % 2, :, :], ebuf[:, j % 2, :, :], ACT.Exp)
                if j >= 4:
                    act.wait_ge(weighed, use - 3)
                nc.scalar.activation(phi[:, j % 4, :, :], ebuf[:, j % 2, :, :], ACT.Exp).then_inc(exped, 1)

            def body(b, p):
                for j in range(PAIRS):
                    if attends(b):
                        exponentials(b, j)
                    if outputs(b):
                        if j == 1:
                            act.wait_ge(T_full, useT("oT", b) + 1)
                            nc.scalar.copy(oT[:], bankT[:, 0:2 * P]).then_inc(T_free, 1)
                        if j == 5:
                            act.wait_ge(T_full, useT("xmT", b) + 1)
                            nc.scalar.copy(xmT[:], bankT[:, 0:2 * P]).then_inc(T_free, 1)
                        if j == 6:
                            act.wait_ge(W_full, useW("up", b) + 1)
                            for f in range(2):
                                last = nc.scalar.activation(hT[:, f, :], bankW[:, f * 2 * P:(f + 1) * 2 * P], ACT.Relu,
                                                            bias=b1[:, f:f + 1])
                            last.then_inc(W_free, 1)
                            act.wait_ge(T_full, useT("up", b) + 1)
                            for f in range(2):
                                last = nc.scalar.activation(hT[:, 2 + f, :], bankT[:, f * 2 * P:(f + 1) * 2 * P], ACT.Relu,
                                                            bias=b1[:, 2 + f:3 + f])
                            last.then_inc(T_free, 1)
                    if prepares(b) and j == 3:
                        take_norm(b)
                    if prepares(b) and j == 5:
                        repeat_parts(b, p, 0)
                    if prepares(b) and j == 6:
                        repeat_parts(b, p, 1)
                if prepares(b):
                    take_q(b, p)
                    take_k(b, p)
                if maximises(b):
                    take_max_T(b, p)

            for b in (-2, -1, 0):
                body(b, b % 2)
            with act.Fori(0, (B - 4) // 2) as it:
                body(it * 2 + 1, 1)
                body(it * 2 + 2, 0)
            for b in (B - 3, B - 2, B - 1, B):
                body(b, b % 2)

        @block.gpsimd
        def _(pool):
            ch = Chain(pool, gchain)

            def low_part(b, j):
                use = 8 * b + j
                pool.wait_ge(exped, use + 1)
                if j >= 4:
                    pool.wait_ge(weighed, use - 3)
                nc.gpsimd.tensor_tensor(plo[:, j % 4, :, :], p32[:, j % 2, :, :], phi[:, j % 4, :, :],
                                        ALU.subtract).then_inc(lowed, 1)

            def split_v(b, p):
                pool.wait_ge(v_ready, b + 1)
                if some(b):
                    pool.wait_ge(weighed, 8 * b)
                v = heads(qkv[:, p, 2, :, :])

                def part(i):
                    return vaug[:, :, :, i, 0:HD].rearrange("p t h d -> p (t h) d")

                ch.step(nc.gpsimd.tensor_tensor(part(0), v, heads(unit[:]), ALU.mult))
                ch.step(nc.gpsimd.tensor_tensor(heads(vrest[:]), v, part(0), ALU.subtract))
                ch.step(nc.gpsimd.tensor_tensor(part(1), heads(vrest[:]), heads(unit[:]), ALU.mult))
                nc.gpsimd.tensor_tensor(part(2), heads(vrest[:]), part(1), ALU.subtract).then_inc(vaug_ready, 1)

            def roots(b, p):
                pool.wait_ge(arg1_ready, b + 3)
                nc.gpsimd.tensor_tensor(rs[:, p].rearrange("p a t -> p (a t)"), arg[:].rearrange("p a t -> p (a t)"),
                                        neghalf[:], ALU.pow).then_inc(rs1_ready, 1)

            def normed(b, p):
                pool.wait_ge(xl_ready, b + 1)
                for t in range(2):
                    last = nc.gpsimd.tensor_tensor(xlb[:, p, t, :], xlb[:, p, t, :], outb[:], ALU.add)
                last.then_inc(xlb_ready, 1)

            def second_root(b):
                pool.wait_ge(arg2_ready, b)
                nc.gpsimd.tensor_tensor(rs2[:], arg2[:], neghalf[:, 0:2], ALU.pow).then_inc(rs2_ready, 1)

            def biased_input(b):
                if some(b - 1):
                    pool.wait_ge(ysum_ready, b - 1)
                for t in range(2):
                    last = ch.mark(nc.gpsimd.tensor_tensor(xb2[:, t, :], tile(b - 1, t), b2[:], ALU.add))
                ch.wait(last)

            def residuals(b):
                pool.wait_ge(y1_ready, b)
                nc.gpsimd.tensor_tensor(ysum[:].rearrange("p t e -> p (t e)"), y1[:].rearrange("p t e -> p (t e)"),
                                        xb2[:].rearrange("p t e -> p (t e)"), ALU.add).then_inc(ysum_ready, 1)

            def body(b, p):
                if attends(b):
                    split_v(b, p)
                for j in range(PAIRS):
                    if prepares(b) and j == 2:
                        roots(b, p)
                    if outputs(b) and j == 4:
                        second_root(b)
                    if attends(b):
                        low_part(b, j)
                    if attends(b) and j == 2:
                        normed(b, p)
                    if outputs(b) and j == 3:
                        biased_input(b)
                    if outputs(b) and j == 5:
                        residuals(b)

            pool.sem_inc(lowed, 2)
            for b in (-2, -1, 0):
                body(b, b % 2)
            before = ch.base + ch.n
            with pool.Fori(0, (B - 4) // 2) as it:
                for u in range(2):
                    b = it * 2 + 1 + u
                    per = 5
                    ch.start((b - 1) * per + before)
                    body(b, 1 - u)
                    assert ch.n == per, ch.n
            ch.start((B - 4) * per + before)
            for b in (B - 3, B - 2, B - 1, B):
                body(b, b % 2)


CH = 4


def expert_weights(nc, ctx, s, ins, ident):
    NE, EF, E = s.NE, s.EF, s.E
    NF = EF // P

    def sb(name, shape, dt=F32):
        return ctx.enter_context(nc.sbuf_tensor(name, shape, dt))

    w = {
        "hi": sb("gate_up_hi", [P, NE, 2 * EF], F32R), "lo": sb("gate_up_lo", [P, NE, 2 * EF], F32R),
        "bias": sb("gate_up_bias", [P, NE, 2 * EF], BF16), "ones": sb("bias_rows_on", [P, P], BF16),
        "down": sb("down_w", [P, NE, NF, E]), "downb": sb("down_b", [P, NE, E]),
        "router": sb("router", [P, NE]), "iota": sb("iota", [P, NE]),
        "before": sb("before", [P, P]), "all": sb("all_ones", [P, P]),
        "slots": sb("iota_slots", [P, P], BF16), "ids": sb("token_ids", [P, s.TILES]),
        "tiles": sb("iota_tiles", [P, s.SLOT_TILES], BF16), "bits": sb("expert_bits", [1, s.BODY]), "tilesf": sb("iota_tiles_f", [P, s.SLOT_TILES]),
    }
    with ExitStack() as c2:
        def sb2(name, shape, dt=F32):
            return c2.enter_context(nc.sbuf_tensor(name, shape, dt))

        def sem2(name):
            return c2.enter_context(nc.semaphore(name))

        rrow = sb2("router_rows", [NE, E])
        raw = sb2("gate_up_raw", [P, NE, 2 * EF])
        braw = sb2("bias_raw", [NE, 2 * EF])
        brest = sb2("bias_rest", [NE, 2 * EF])
        bpart = sb2("bias_part", [NE, 3, 2 * EF], BF16)
        bank = c2.enter_context(nc.psum_tensor("setup_bank", [P, 512], F32))
        small, loaded, full, counted, set_, parts, placed, zeroed = (
            sem2("router_loaded"), sem2("experts_loaded"), sem2("experts_bank_full"), sem2("experts_iotas"),
            sem2("experts_set"), sem2("bias_parts_ready"), sem2("bias_placed"), sem2("bias_zeroed"))
        chain, gchain = sem2("experts_vector_steps"), sem2("experts_gpsimd_steps")
        downb = ins["L0_ffn_down_b"]
        with nc.Block() as block:
            @block.sync
            def _(sp):
                sp.dma_start(rrow[:], ins["L0_ffn_router_w"]).then_inc(small, 16)
                sp.dma_start(braw[:, 0:EF], ins["L0_ffn_gate_b"]).then_inc(small, 16)
                sp.dma_start(braw[:, EF:2 * EF], ins["L0_ffn_up_b"]).then_inc(small, 16)
                sp.dma_start(raw[:, :, 0:EF], ins["L0_ffn_gate_w"].rearrange("e d f -> d e f")).then_inc(loaded, 16)
                sp.dma_start(raw[:, :, EF:2 * EF], ins["L0_ffn_up_w"].rearrange("e d f -> d e f")).then_inc(loaded, 16)
                sp.dma_start(w["downb"][:], bass.AP(tensor=downb.tensor, offset=downb.offset,
                                                    ap=[[0, P], [E, NE], [1, E]])).then_inc(loaded, 16)
                sp.dma_start(w["down"][:], ins["L0_ffn_down_w"].rearrange("e (c p) d -> p e c d", p=P)).then_inc(loaded, 16)
                sp.wait_ge(small, 48)
                sp.wait_ge(loaded, 64)
                sp.wait_ge(parts, 1)
                sp.wait_ge(zeroed, 1)
                for j in range(3):
                    sp.dma_start(w["bias"][j:j + 1, :, :], bpart[:, j, :]).then_inc(placed, 16)
                sp.wait_ge(placed, 48)

            @block.gpsimd
            def _(pool):
                ch = Chain(pool, gchain)
                nc.gpsimd.iota(w["iota"][:], pattern=[[1, NE]], base=0, channel_multiplier=0,
                               allow_small_or_imprecise_dtypes=True)
                nc.gpsimd.iota(w["ids"][:], pattern=[[P, s.TILES]], base=-s.N // 2, channel_multiplier=1,
                               allow_small_or_imprecise_dtypes=True)
                nc.gpsimd.iota(w["slots"][:], pattern=[[1, P]], base=0, channel_multiplier=0,
                               allow_small_or_imprecise_dtypes=True)
                nc.gpsimd.iota(w["tiles"][:], pattern=[[1, s.SLOT_TILES]], base=0, channel_multiplier=0,
                               allow_small_or_imprecise_dtypes=True)
                nc.gpsimd.iota(w["tilesf"][:], pattern=[[1, s.SLOT_TILES]], base=0, channel_multiplier=0,
                               allow_small_or_imprecise_dtypes=True).then_inc(counted, 1)
                for u in range(s.BODY):
                    nc.gpsimd.memset(w["bits"][:, u:u + 1], float(NE ** u))
                ch.step(nc.gpsimd.memset(w["all"][:], 1.0))
                ch.step(nc.gpsimd.affine_select(out=w["before"][:], in_=w["all"][:], compare_op=ALU.is_gt, fill=0.0,
                                                base=0, pattern=[[1, P]], channel_multiplier=-1))
                ch.step(nc.gpsimd.affine_select(out=w["ones"][:], in_=w["all"][:], compare_op=ALU.is_gt, fill=0.0,
                                                base=3, pattern=[[0, P]], channel_multiplier=-1))

            @block.tensor
            def _(pe):
                pe.wait_ge(small, 48)
                nc.tensor.transpose(bank[:, 0:NE], rrow[:], ident[0:NE, 0:NE]).then_inc(full, 1)

            @block.vector
            def _(dve):
                ch = Chain(dve, chain)
                nc.vector.memset(w["bias"][:].rearrange("p e f -> p (e f)").bitcast(F32), 0.0).then_inc(zeroed, 1)
                dve.wait_ge(small, 48)
                ch.step(nc.vector.tensor_copy(bpart[:, 0, :], braw[:]))
                ch.step(nc.vector.tensor_tensor(brest[:], braw[:], bpart[:, 0, :], ALU.subtract))
                ch.step(nc.vector.tensor_copy(bpart[:, 1, :], brest[:]))
                nc.vector.tensor_tensor(bpart[:, 2, :], brest[:], bpart[:, 1, :], ALU.subtract).then_inc(parts, 1)
                dve.wait_ge(full, 1)
                nc.vector.tensor_copy(w["router"][:], bank[:, 0:NE])
                dve.wait_ge(loaded, 64)
                for e in range(NE):
                    ch.step(nc.vector.tensor_copy(w["hi"][:, e, :], raw[:, e, :]))
                    last = ch.mark(nc.vector.tensor_tensor(w["lo"][:, e, :], raw[:, e, :], w["hi"][:, e, :].bitcast(F32),
                                                           ALU.subtract))
                ch.wait(last)
    return w


def mixture(nc, kept, s, tag, xres, ident, w, normed_dram, slot_dram):
    share = kept.enter_context(nc.sbuf_tensor(tag + "share", [P, 2, s.TILES], F32))
    slot = kept.enter_context(nc.sbuf_tensor(tag + "slot", [P, 2, s.TILES], I32))
    with ExitStack() as ctx:
        def sb(name, shape, dt=F32):
            return ctx.enter_context(nc.sbuf_tensor(tag + name, shape, dt))

        token = sb("token", [P, s.SLOT_TILES], I32)
        expert = sb("expert", [1, s.SLOT_TILES // s.BODY], I32)
        route(nc, s, tag, xres, ident, w, share, slot, token, expert, normed_dram)
        run_experts(nc, s, tag, ident, w, token, expert, normed_dram, slot_dram)
    return share, slot


def run_experts(nc, s, tag, ident, w, token, expert, normed_dram, slot_dram):
    NE, EF, E, ST = s.NE, s.EF, s.E, s.SLOT_TILES
    NF = EF // P
    U = s.BODY
    G = 4
    assert ST % U == 0 and NE == 8
    with phase(nc) as (ctx, new_sem):
        def sb(name, shape, dt=F32):
            return ctx.enter_context(nc.sbuf_tensor(tag + name, shape, dt))

        def sem(name):
            return new_sem(tag + name)

        def pb(name):
            return [ctx.enter_context(nc.psum_tensor(f"{tag}{name}{i}", [P, 512], F32)) for i in range(2)]

        index = sb("index", [P, 2, G], I32)
        xg = sb("xg", [P, G, E])
        xhi, xlo = sb("xhi", [P, 2, P], F32R), sb("xlo", [P, 2, P], F32R)
        act_ = sb("silu", [P, 2, EF])
        hid = sb("hid", [P, 4, EF])
        hT = sb("hT", [P, 2, NF, P])
        yo = sb("yo", [P, 2, E])
        bx, bgu, bh, by = pb("bx"), pb("bgu"), pb("bh"), pb("by")
        arrived = [sem(f"rows_arrived{i}") for i in range(G)]
        stored = [sem(f"rows_stored{i}") for i in range(2)]
        xT_full, hi_done, lo_done, gu_full, silu_done, hid_done, hT_full, hT_done, y_full, y_done = (
            sem("xT_full"), sem("hi_done"), sem("lo_done"), sem("gu_full"), sem("silu_done"), sem("hid_done"),
            sem("hT_full"), sem("hT_done"), sem("y_full"), sem("y_done"))
        picked, turns = sem("index_picked"), sem("gather_turns")

        def experts_of(engine, body):
            word = engine.value_load(expert[0:1, bass.ds(body, 1)], min_val=0, max_val=NE ** U - 1)
            return [(word >> (3 * u)) & (NE - 1) for u in range(U)]

        with nc.Block() as block:
            @block.gpsimd
            def _(pool):
                def gather(i, u):
                    if u % G == 0:
                        if not isinstance(i, int):
                            pool.wait_ge(xT_full, i - G)
                        nc.gpsimd.tensor_copy(index[:, (u // G) % 2, :], token[:, bass.ds(i, G)]).then_inc(picked, 1)
                        if isinstance(i, int):
                            pool.wait_ge(picked, i // G + 1)
                        else:
                            pool.wait_ge(picked, pool_it[0] * (U // G) + u // G + 1)
                    if not isinstance(i, int) or i >= G:
                        pool.wait_ge(xT_full, i - G + 1)
                    pool.sem_inc(turns, 1)
                    pool.indirect_dma_start(
                        xg[:, u % G, :], None, normed_dram,
                        bass.IndirectOffsetOnAxis(ap=index[:, (u // G) % 2, u % G:u % G + 1], axis=0),
                    ).then_inc(arrived[u % G], 16)

                pool_it = [None]
                for u in range(U):
                    gather(u, u)
                with pool.Fori(1, ST // U) as it:
                    pool_it[0] = it
                    for u in range(U):
                        gather(it * U + u, u)

            @block.tensor
            def _(pe):
                def transpose_x(i, u, n):
                    pe.wait_ge(arrived[u % G], n)
                    if not isinstance(i, int) or i >= 2:
                        pe.wait_ge(lo_done, i - 1)
                    nc.tensor.transpose(bx[u % 2][:, 0:P], xg[:, u % G, :], ident[:]).then_inc(xT_full, 1)

                def gate_up(i, u, e):
                    if not isinstance(i, int) or i >= 2:
                        pe.wait_ge(hid_done, i - 1)
                    wh = w["hi"][:, bass.ds(e, 1), :].rearrange("p a f -> p (a f)")
                    wl = w["lo"][:, bass.ds(e, 1), :].rearrange("p a f -> p (a f)")
                    bias = w["bias"][:, bass.ds(e, 1), :].rearrange("p a f -> p (a f)")
                    dst = bgu[u % 2][:]
                    nc.tensor.matmul(dst, w["ones"][:], bias, start=True, stop=False)
                    pe.wait_ge(lo_done, i + 1)
                    nc.tensor.matmul(dst, xhi[:, u % 2, :], wh, start=False, stop=False)
                    nc.tensor.matmul(dst, xhi[:, u % 2, :], wl, start=False, stop=False)
                    nc.tensor.matmul(dst, xlo[:, u % 2, :], wh, start=False, stop=True).then_inc(gu_full, 1)

                def transpose_h(i, u):
                    pe.wait_ge(hid_done, i + 1)
                    if not isinstance(i, int) or i >= 2:
                        pe.wait_ge(hT_done, i - 1)
                    for f in range(NF):
                        last = nc.tensor.transpose(bh[u % 2][:, f * P:(f + 1) * P], hid[:, u % 4, f * P:(f + 1) * P], ident[:])
                    last.then_inc(hT_full, 1)

                def down(i, u, e):
                    pe.wait_ge(hT_done, i + 1)
                    if not isinstance(i, int) or i >= 2:
                        pe.wait_ge(y_done, i - 1)
                    for f in range(NF):
                        last = nc.tensor.matmul(by[u % 2][:, 0:E], hT[:, u % 2, f, :],
                                                w["down"][:, bass.ds(e, 1), f, :].rearrange("p a d -> p (a d)"),
                                                start=(f == 0), stop=(f == NF - 1))
                    last.then_inc(y_full, 1)

                def steps(i, u, n, e):
                    early = i if isinstance(i, int) else ST
                    if early >= 3:
                        transpose_h(i - 3, (u - 3) % U)
                    if n is not None:
                        transpose_x(i, u, n)
                    if early >= 4:
                        down(i - 4, (u - 4) % U, e[U + u - 4])
                    if early >= 1:
                        gate_up(i - 1, (u - 1) % U, e[U + u - 1])

                now = experts_of(pe, 0)
                for u in range(U):
                    steps(u, u, 16 * (u // G + 1), [None] * U + now)
                with pe.Fori(1, ST // U) as it:
                    both = experts_of(pe, it - 1) + experts_of(pe, it)
                    for u in range(U):
                        steps(it * U + u, u, it * (16 * U // G) + 16 * (u // G + 1), both)
                now = experts_of(pe, ST // U - 1)
                steps(ST, 0, None, now)
                for i in range(ST - 2, ST):
                    transpose_h(i, i % U)
                    down(i - 1, (i - 1) % U, now[i - 1 - ST])
                down(ST - 1, U - 1, now[-1])

            @block.scalar
            def _(act):
                def high(i, u):
                    act.wait_ge(xT_full, i + 1)
                    if not isinstance(i, int) or i >= 2:
                        act.wait_ge(gu_full, i - 1)
                    nc.scalar.copy(xhi[:, u % 2, :], bx[u % 2][:, 0:P]).then_inc(hi_done, 1)

                def silu(i, u):
                    act.wait_ge(gu_full, i + 1)
                    if not isinstance(i, int) or i >= 2:
                        act.wait_ge(hid_done, i - 1)
                    nc.scalar.activation(act_[:, u % 2, :], bgu[u % 2][:, 0:EF], ACT.Silu).then_inc(silu_done, 1)

                def take_h(i, u):
                    act.wait_ge(hT_full, i + 1)
                    if not isinstance(i, int) or i >= 2:
                        act.wait_ge(y_full, i - 1)
                    nc.scalar.copy(hT[:, u % 2, :, :], bh[u % 2][:, 0:EF].rearrange("p (f q) -> p f q", f=NF)).then_inc(hT_done, 1)

                def steps(i, u):
                    if not isinstance(i, int) or i >= 3:
                        take_h(i - 3, (u - 3) % U)
                    high(i, u)
                    if not isinstance(i, int) or i >= 1:
                        silu(i - 1, (u - 1) % U)

                for u in range(U):
                    steps(u, u)
                with act.Fori(1, ST // U) as it:
                    for u in range(U):
                        steps(it * U + u, u)
                take_h(ST - 3, U - 3)
                silu(ST - 1, U - 1)
                take_h(ST - 2, U - 2)
                take_h(ST - 1, U - 1)

            @block.vector
            def _(dve):
                def low(i, u):
                    dve.wait_ge(hi_done, i + 1)
                    if not isinstance(i, int) or i >= 2:
                        dve.wait_ge(gu_full, i - 1)
                    nc.vector.tensor_tensor(xlo[:, u % 2, :], bx[u % 2][:, 0:P], xhi[:, u % 2, :].bitcast(F32),
                                            ALU.subtract).then_inc(lo_done, 1)

                def hidden(i, u):
                    dve.wait_ge(silu_done, i + 1)
                    if not isinstance(i, int) or i >= 4:
                        dve.wait_ge(hT_full, i - 3)
                    nc.vector.tensor_tensor(hid[:, u % 4, :], bgu[u % 2][:, EF:2 * EF], act_[:, u % 2, :], ALU.mult).then_inc(hid_done, 1)

                def take_y(i, u, n, e):
                    dve.wait_ge(y_full, i + 1)
                    if n is not None:
                        dve.wait_ge(stored[u % 2], n)
                    nc.vector.tensor_tensor(yo[:, u % 2, :], by[u % 2][:, 0:E],
                                            w["downb"][:, bass.ds(e, 1), :].rearrange("p a d -> p (a d)"), ALU.add).then_inc(y_done, 1)

                def steps(i, u, it, e):
                    low(i, u)
                    if not isinstance(i, int) or i >= 4:
                        k = (i - 4) if isinstance(i, int) else u - 4
                        n = 16 * (k // 2)
                        take_y(i - 4, (u - 4) % U, (n or None) if isinstance(i, int) else it * (16 * U // 2) + n, e[U + u - 4])
                    if not isinstance(i, int) or i >= 1:
                        hidden(i - 1, (u - 1) % U)

                now = experts_of(dve, 0)
                for u in range(U):
                    steps(u, u, None, [None] * U + now)
                with dve.Fori(1, ST // U) as it:
                    both = experts_of(dve, it - 1) + experts_of(dve, it)
                    for u in range(U):
                        steps(it * U + u, u, it, both)
                now = experts_of(dve, ST // U - 1)
                for i in range(ST - 4, ST):
                    take_y(i, i % U, 16 * (i // 2), now[i - ST])
                    if i == ST - 4:
                        hidden(ST - 1, U - 1)

            @block.sync
            def _(sp):
                def store(i, u):
                    sp.wait_ge(y_done, i + 1)
                    sp.dma_start(slot_dram[bass.ds(i * P, P), :], yo[:, u % 2, :]).then_inc(stored[u % 2], 16)

                with sp.Fori(0, ST // U) as it:
                    for u in range(U):
                        store(it * U + u, u)
                for i in range(2):
                    sp.wait_ge(stored[i], 16 * ST // 2)


def combine(nc, s, xres, share, slot, slot_dram):
    E, TILES = s.E, s.TILES
    U = 4
    with phase(nc) as (ctx, new_sem):
        def sem(name):
            return new_sem(name)

        index = ctx.enter_context(nc.sbuf_tensor("c_index", [P, 2, 2, U], I32))
        row = ctx.enter_context(nc.sbuf_tensor("c_row", [P, 2 * U, E], F32))
        arrived = [sem(f"c_arrived{i}") for i in range(2 * U)]
        picked, turns, added, half = sem("c_picked"), sem("c_turns"), sem("c_added"), sem("c_half")
        with nc.Block() as block:
            @block.gpsimd
            def _(pool):
                def gather(it, q, first):
                    base = it * U if isinstance(it, int) else it * U
                    if not first:
                        pool.wait_ge(added, (it - 1) * U)
                    nc.gpsimd.tensor_copy(index[:, q, :, :], slot[:, :, bass.ds(it * U, U)]).then_inc(picked, 1)
                    pool.wait_ge(picked, it + 1)
                    for u in range(U):
                        for k in range(2):
                            r = (2 * u + k)
                            if not (isinstance(it, int) and it == 0):
                                pool.wait_ge(added, (it - 1) * U + u + 1)
                            pool.sem_inc(turns, 1)
                            pool.indirect_dma_start(row[:, r, :], None, slot_dram,
                                                    bass.IndirectOffsetOnAxis(ap=index[:, q, k, u:u + 1], axis=0)
                                                    ).then_inc(arrived[r], 16)

                gather(0, 0, True)
                gather(1, 1, True)
                with pool.Fori(1, TILES // U // 2) as it:
                    gather(it * 2, 0, False)
                    gather(it * 2 + 1, 1, False)

            @block.vector
            def _(dve):
                with dve.Fori(0, TILES // U) as it:
                    for u in range(U):
                        x = xres[:, bass.ds(it * U + u, 1), :].rearrange("p a e -> p (a e)")
                        for k in range(2):
                            dve.wait_ge(arrived[2 * u + k], it * 16 + 16)
                            if k == 1:
                                dve.wait_ge(half, it * U + u + 1)
                            nc.vector.scalar_tensor_tensor(
                                x, row[:, 2 * u + k, :], share[:, k, bass.ds(it * U + u, 1)], x, ALU.mult, ALU.add
                            ).then_inc(added if k == 1 else half, 1)
                dve.wait_ge(added, TILES)


def route(nc, s, tag, xres, ident, w, share, slot, token, expert, normed_dram):
    NE, E, TILES, ST = s.NE, s.E, s.TILES, s.SLOT_TILES
    CHUNKS = TILES // CH
    with phase(nc) as (ctx, new_sem):
        def sb(name, shape, dt=F32):
            return ctx.enter_context(nc.sbuf_tensor(tag + name, shape, dt))

        def sem(name):
            return new_sem(tag + name)

        def pb(name, n=1):
            return [ctx.enter_context(nc.psum_tensor(f"{tag}{name}{i}", [P, 512], F32)) for i in range(n)]

        stats = sb("r_stats", [P, 2, CH, 6])
        mv = sb("r_mv", [P, 2, 4, CH])
        arg = sb("r_arg", [P, 2, CH])
        rs = sb("r_rs", [P, 2, CH])
        half = sb("r_half", [P, CH])
        xl = sb("r_xl", [P, 2, CH, E])
        xT = sb("r_xT", [P, 2, CH * P])
        logits = sb("logits", [P, TILES, NE])
        prob = sb("prob", [P, TILES, NE])
        tmp = sb("r_tmp", [P, TILES, NE])
        tmp2 = sb("r_tmp2", [P, TILES, NE])
        hot = [sb(f"hot{k}", [P, TILES, NE]) for k in range(2)]
        top = [sb(f"top{k}", [P, TILES]) for k in range(2)]
        first = sb("first", [P, TILES])
        den = sb("den", [P, TILES])
        member = sb("member", [P, NE, TILES])
        seen = sb("seen", [P, NE, TILES])
        unit = sb("r_unit", [P, NE * TILES])
        count = sb("count", [P, NE])
        place = sb("place", [P, NE])
        ends = sb("ends", [P, NE])
        tiles_i = sb("tiles_i", [P, NE], I32)
        tiles_f = sb("tiles_f", [P, NE])
        slot_f = sb("slot_f", [P, 2, TILES])
        part_i = sb("part_i", [P, 2, 2, TILES], I32)
        part_f = sb("part_f", [P, 2, 2, TILES])
        ge = sb("ge", [1, ST, NE])
        ex_f = sb("ex_f", [1, ST])
        ex_w = sb("ex_w", [1, ST // s.BODY])
        in_tile = sb("in_tile", [P, 8, P], F32R)
        in_row = sb("in_row", [P, 8, 2 * P], F32R)
        bx, bl = pb("r_bx", 2), pb("r_bl", 2)
        bc, = pb("r_bc")
        bt, = pb("r_bt")
        ready, rooted, normed, x_full, x_taken, l_full, l_taken, half_set = (
            sem("r_arg_ready"), sem("r_rooted"), sem("r_normed"), sem("r_xT_full"), sem("r_xT_taken"),
            sem("r_logits_full"), sem("r_logits_taken"), sem("r_half_set"))
        shifted, exped, chain = sem("r_shifted"), sem("r_exped"), sem("r_vector_steps")
        row_out = [sem(f"r_rows_out{i}") for i in range(2)]
        counted, summed, hot_ready, hot_used, table_full = (sem("r_counted"), sem("r_summed"), sem("r_hot_ready"),
                                                            sem("r_hot_used"), sem("r_table_full"))
        assert 2 * P >= ST

        with nc.Block() as block:
            @block.vector
            def _(dve):
                ch = Chain(dve, chain)
                nc.vector.memset(half[:], -0.5).then_inc(half_set, 1)
                PER = CH + 6

                def head(c, q):
                    for t in range(CH):
                        last = ch.mark(nc.vector.bn_stats(stats[:, q, t, :], xres[:, bass.ds(c * CH + t, 1), :].rearrange("p a e -> p (a e)")))
                    ch.wait(last)
                    moments(nc, ch, stats[:, q], mv[:, q])
                    nc.vector.tensor_scalar(arg[:, q, :], mv[:, q, 3, :], 0.25, EPS, ALU.mult, ALU.add).then_inc(ready, 1)

                def tail(c, q, n):
                    dve.wait_ge(rooted, c + 1)
                    if n is not None:
                        dve.wait_ge(x_full, c - 1)
                        dve.wait_ge(row_out[q], n)
                    for t in range(CH):
                        last = nc.vector.tensor_scalar(xl[:, q, t, :], xres[:, bass.ds(c * CH + t, 1), :].rearrange("p a e -> p (a e)"),
                                                       mv[:, q, 0, t:t + 1], rs[:, q, t:t + 1], ALU.subtract, ALU.mult)
                    last.then_inc(normed, 1)

                def take(c, q):
                    dve.wait_ge(l_full, c + 1)
                    nc.vector.tensor_copy(logits[:, bass.ds(c * CH, CH), :].rearrange("p t e -> p (t e)"),
                                          bl[q][:, 0:CH * NE]).then_inc(l_taken, 1)

                def pair(c, n):
                    head(c + 1, 1)
                    tail(c, 0, n)
                    head(c + 2, 0)
                    tail(c + 1, 1, n)
                    if n is not None:
                        take(c - 2, 0)
                        take(c - 1, 1)

                head(0, 0)
                pair(0, None)
                with dve.Fori(1, CHUNKS // 2 - 1) as it:
                    ch.start(it * (2 * PER) + PER)
                    pair(it * 2, it * 16)
                ch.start((CHUNKS // 2 - 1) * 2 * PER + PER)
                head(CHUNKS - 1, 1)
                tail(CHUNKS - 2, 0, 16 * (CHUNKS // 2 - 1))
                tail(CHUNKS - 1, 1, 16 * (CHUNKS // 2 - 1))
                take(CHUNKS - 4, 0)
                take(CHUNKS - 3, 1)
                take(CHUNKS - 2, 0)
                take(CHUNKS - 1, 1)
                dve.wait_ge(l_taken, CHUNKS)

                V = nc.vector

                def over(x):
                    return x.rearrange("p (t a) -> p t a", a=1).broadcast_to([P, TILES, NE])

                iota = w["iota"][:].rearrange("p (a e) -> p a e", a=1).broadcast_to([P, TILES, NE])
                ch.step(V.reduce_max(den[:], logits[:], AXX))
                V.tensor_tensor(logits[:], logits[:], over(den[:]), ALU.subtract).then_inc(shifted, 1)
                dve.wait_ge(exped, 1)
                ch.step(V.reduce_sum(den[:], prob[:], AXX))
                ch.step(V.reciprocal(den[:], den[:]))
                ch.step(V.tensor_tensor(prob[:], prob[:], over(den[:]), ALU.mult))
                left = prob
                for k in range(2):
                    ch.step(V.reduce_max(top[k][:], left[:], AXX))
                    ch.step(V.tensor_tensor(tmp[:], left[:], over(top[k][:]), ALU.is_equal))
                    ch.step(V.scalar_tensor_tensor(tmp[:], tmp[:], -float(NE), iota, ALU.mult, ALU.add))
                    ch.step(V.tensor_reduce(first[:], tmp[:], AXX, ALU.min))
                    ch.step(V.tensor_scalar(first[:], first[:], float(NE), None, ALU.add))
                    ch.step(V.tensor_tensor(hot[k][:], over(first[:]), iota, ALU.is_equal))
                    if k == 0:
                        ch.step(V.scalar_tensor_tensor(tmp2[:], hot[0][:], -2.0, left[:], ALU.mult, ALU.add))
                        left = tmp2
                ch.step(V.scalar_tensor_tensor(den[:], top[0][:], 1e-9, top[1][:], ALU.add, ALU.add))
                ch.step(V.reciprocal(den[:], den[:]))
                for k in range(2):
                    ch.step(V.tensor_tensor(share[:, k, :], top[k][:], den[:], ALU.mult))

                ch.step(V.memset(unit[:], 1.0))
                ch.step(V.tensor_tensor(member[:].rearrange("p e t -> p t e"), hot[0][:], hot[1][:], ALU.add))
                ch.step(V.tensor_tensor_scan(seen[:].rearrange("p e t -> p (e t)"), unit[:],
                                             member[:].rearrange("p e t -> p (e t)"), 0.0, ALU.mult, ALU.add))
                ch.step(V.memset(ends[:], 0.0))
                ch.step(V.tensor_copy(ends[:, 1:NE], seen[:, 0:NE - 1, TILES - 1]))
                V.tensor_tensor(count[:], seen[:, :, TILES - 1], ends[:], ALU.subtract).then_inc(counted, 1)
                dve.wait_ge(summed, 1)
                ch.step(V.tensor_scalar(tiles_i[:], bc[:, NE:2 * NE], float(P - 1), None, ALU.add))
                ch.step(V.tensor_scalar(tiles_i[:], tiles_i[:], 7, None, ALU.arith_shift_right))
                ch.step(V.tensor_copy(tiles_f[:], tiles_i[:]))
                ch.step(V.tensor_tensor_scan(place[:], unit[:, 0:NE], tiles_f[:], 0.0, ALU.mult, ALU.add))
                ch.step(V.tensor_tensor(ge[:], w["tilesf"][0:1, :].rearrange("p (t a) -> p t a", a=1).broadcast_to([1, ST, NE]),
                                        place[0:1, :].rearrange("p (a e) -> p a e", a=1).broadcast_to([1, ST, NE]), ALU.is_ge))
                ch.step(V.reduce_sum(ex_f[:], ge[:], AXX))
                ch.step(V.tensor_scalar(ex_f[:], ex_f[:], float(NE - 1), None, ALU.min))
                ch.step(V.tensor_tensor(ex_f[:].rearrange("p (b u) -> p b u", u=s.BODY), ex_f[:].rearrange("p (b u) -> p b u", u=s.BODY),
                                        w["bits"][0:1, :].rearrange("p (a u) -> p a u", a=1).broadcast_to([1, ST // s.BODY, s.BODY]),
                                        ALU.mult))
                ch.step(V.reduce_sum(ex_w[:], ex_f[:].rearrange("p (b u) -> p b u", u=s.BODY), AXX))
                ch.step(V.tensor_copy(expert[:], ex_w[:]))
                ch.step(V.tensor_tensor(place[:], place[:], tiles_f[:], ALU.subtract))
                ch.step(V.scalar_tensor_tensor(place[:], place[:], float(P), ends[:], ALU.mult, ALU.subtract))
                ch.step(V.tensor_tensor(place[:], place[:], bc[:, 0:NE], ALU.add))
                ch.step(V.tensor_tensor(seen[:], seen[:], member[:], ALU.subtract))
                ch.step(V.tensor_tensor(seen[:], seen[:], place[:].rearrange("p (e a) -> p e a", a=1).broadcast_to([P, NE, TILES]),
                                        ALU.add))
                for k in range(2):
                    ch.step(V.tensor_tensor(tmp[:], seen[:].rearrange("p e t -> p t e"), hot[k][:], ALU.mult))
                    ch.step(V.reduce_sum(slot_f[:, k, :], tmp[:], AXX))
                ch.step(V.tensor_copy(slot[:], slot_f[:]))
                ch.step(V.tensor_scalar(part_i[:, 0], slot[:], 7, None, ALU.arith_shift_right))
                ch.step(V.tensor_scalar(part_i[:, 1], slot[:], P - 1, None, ALU.bitwise_and))
                ch.step(V.tensor_copy(part_f[:].rearrange("p a k t -> p (a k t)"), part_i[:].rearrange("p a k t -> p (a k t)")))
                for q in range(8):
                    last = ch.mark(V.memset(in_row[:, q, ST:2 * P].bitcast(F32), 0.0))
                ch.wait(last)
                dve.sem_inc(hot_used, 2)
                with dve.Fori(0, TILES // 4) as it:
                    for u in range(4):
                        for k in range(2):
                            n = 2 * u + k
                            if n % 4 == 0:
                                dve.wait_ge(hot_used, it * 2 + n // 4 + 1)
                            V.tensor_scalar(in_tile[:, n, :], w["slots"][:], part_f[:, 1, k, bass.ds(it * 4 + u, 1)], None,
                                            ALU.is_equal)
                            last = V.tensor_scalar(in_row[:, n, 0:ST], w["tiles"][:], part_f[:, 0, k, bass.ds(it * 4 + u, 1)],
                                                   w["ids"][:, bass.ds(it * 4 + u, 1)], ALU.is_equal, ALU.mult)
                        if u % 2 == 1:
                            last.then_inc(hot_ready, 1)
                dve.wait_ge(table_full, 1)
                ch.step(V.tensor_scalar(token[:], bt[:, 0:ST], float(s.N // 2), None, ALU.add))

            @block.gpsimd
            def _(pool):
                pool.wait_ge(half_set, 1)

                def root(c, q):
                    pool.wait_ge(ready, c + 1)
                    nc.gpsimd.tensor_tensor(rs[:, q, :], arg[:, q, :], half[:], ALU.pow).then_inc(rooted, 1)

                with pool.Fori(0, CHUNKS // 2) as it:
                    root(it * 2, 0)
                    root(it * 2 + 1, 1)

            @block.sync
            def _(sp):
                def store(c, q):
                    sp.wait_ge(normed, c + 1)
                    sp.dma_start(normed_dram.rearrange("(t p) e -> p t e", p=P)[:, bass.ds(c * CH, CH), :], xl[:, q, :, :]
                                 ).then_inc(row_out[q], 16)

                with sp.Fori(0, CHUNKS // 2) as it:
                    store(it * 2, 0)
                    store(it * 2 + 1, 1)
                for q in range(2):
                    sp.wait_ge(row_out[q], 8 * CHUNKS)

            @block.tensor
            def _(pe):
                def transposes(c, q):
                    pe.wait_ge(normed, c + 1)
                    if not isinstance(c, int) or c >= 2:
                        pe.wait_ge(x_taken, c - 1)
                    for t in range(CH):
                        last = nc.tensor.transpose(bx[q][:, t * P:(t + 1) * P], xl[:, q, t, :], ident[:])
                    last.then_inc(x_full, 1)

                def router(c, q):
                    pe.wait_ge(x_taken, c + 1)
                    if not isinstance(c, int) or c >= 2:
                        pe.wait_ge(l_taken, c - 1)
                    for t in range(CH):
                        last = nc.tensor.matmul(bl[q][:, t * NE:(t + 1) * NE], xT[:, q, t * P:(t + 1) * P],
                                                w["router"][:], start=True, stop=True)
                    last.then_inc(l_full, 1)

                transposes(0, 0)
                transposes(1, 1)
                router(0, 0)
                transposes(2, 0)
                router(1, 1)
                transposes(3, 1)
                with pe.Fori(2, CHUNKS // 2) as it:
                    router(it * 2 - 2, 0)
                    transposes(it * 2, 0)
                    router(it * 2 - 1, 1)
                    transposes(it * 2 + 1, 1)
                router(CHUNKS - 2, 0)
                router(CHUNKS - 1, 1)
                pe.wait_ge(counted, 1)
                nc.tensor.matmul(bc[:, 0:NE], w["before"][:], count[:], start=True, stop=True)
                nc.tensor.matmul(bc[:, NE:2 * NE], w["all"][:], count[:], start=True, stop=True).then_inc(summed, 1)

                def place_four(n, first, final):
                    for q in range(4):
                        last = nc.tensor.matmul(bt[:, 0:2 * P], in_tile[:, 4 * n + q, :], in_row[:, 4 * n + q, :],
                                                start=(first and q == 0), stop=(final and q == 3), skip_group_check=True)
                    return last

                pe.wait_ge(hot_ready, 1)
                place_four(0, True, False).then_inc(hot_used, 1)
                pe.wait_ge(hot_ready, 2)
                place_four(1, False, False).then_inc(hot_used, 1)
                with pe.Fori(1, TILES // 4 - 1) as it:
                    for n in range(2):
                        pe.wait_ge(hot_ready, it * 2 + n + 1)
                        place_four(n, False, False).then_inc(hot_used, 1)
                pe.wait_ge(hot_ready, TILES // 2 - 1)
                place_four(0, False, False).then_inc(hot_used, 1)
                pe.wait_ge(hot_ready, TILES // 2)
                place_four(1, False, True).then_inc(table_full, 1)

            @block.scalar
            def _(act):
                def chunk(c, q):
                    act.wait_ge(x_full, c + 1)
                    nc.scalar.copy(xT[:, q, :], bx[q][:]).then_inc(x_taken, 1)

                chunk(0, 0)
                chunk(1, 1)
                with act.Fori(1, CHUNKS // 2) as it:
                    act.wait_ge(l_full, it * 2 - 1)
                    chunk(it * 2, 0)
                    act.wait_ge(l_full, it * 2)
                    chunk(it * 2 + 1, 1)
                act.wait_ge(shifted, 1)
                nc.scalar.activation(prob[:], logits[:], ACT.Exp).then_inc(exped, 1)


def recurrence(nc, s, ins, xres, ident, share, slot, slot_dram):
    E, B, S = s.E, s.B, s.S
    with phase(nc) as (ctx, sem):
        def sb(name, shape, dt=F32):
            return ctx.enter_context(nc.sbuf_tensor(name, shape, dt))

        index = sb("z_index", [P, 2, 2, 2], I32)
        rows = sb("z_rows", [P, 2, 2, 2, E])
        arrived = [sem(f"z_arrived{i}") for i in range(8)]
        picked, turns, first_added, added, combined = (sem("z_picked"), sem("z_turns"), sem("z_first_added"),
                                                       sem("z_added"), sem("z_combined"))
        wz, wh = sb("wz", [P, E]), sb("wh", [P, E])
        cols = sb("z_cols", [P, 3])
        gamma, beta = sb("gamma", [P, 2, E]), sb("beta", [P, 2, E])
        half = sb("z_half", [P, 4])
        stats, mv = sb("z_stats", [P, 2, 4, 6]), sb("z_mv", [P, 2, 4, 4])
        arg, rs = sb("z_arg", [P, 2, 4]), sb("z_rs", [P, 2, 4])
        xl = sb("z_xl", [P, 2, 2, E])
        xT = sb("z_xT", [P, 2, 2 * P])
        keep, z, sg = sb("z_keep", [P, 2, S]), sb("z_gate", [P, 2, S]), sb("z_sig", [P, 2, S])
        relu, val, hs = sb("z_relu", [P, S]), sb("z_val", [P, S]), sb("z_h", [P, 2, S])
        nh = sb("z_nh", [P, 2, E])
        bx = [ctx.enter_context(nc.psum_tensor(f"zx{i}", [P, 512], F32)) for i in range(2)]
        bk = [ctx.enter_context(nc.psum_tensor(f"zk{i}", [P, 512], F32)) for i in range(2)]
        bh = [ctx.enter_context(nc.psum_tensor(f"zh{i}", [P, 512], F32)) for i in range(2)]
        loaded, setup = sem("z_loaded"), sem("z_setup")
        ready, rooted, normed, x_full, x_taken, k_full = (sem("z_arg_ready"), sem("z_rooted"), sem("z_normed"),
                                                          sem("z_xT_full"), sem("z_xT_taken"), sem("z_k_full"))
        gates, scanned, h_full, based, done = (sem("z_gates"), sem("z_scanned"), sem("z_h_full"), sem("z_based"),
                                               sem("z_done"))
        chain, gchain = sem("z_vector_steps"), sem("z_gpsimd_steps")

        def col(name):
            return ins[name].rearrange("(p a) -> p a", a=1)

        def row(name):
            t = ins[name]
            return bass.AP(tensor=t.tensor, offset=t.offset, ap=[[0, P], [1, E]])

        with nc.Block() as block:
            @block.sync
            def _(sp):
                for dst, src in ((wz[:], ins["L0_attn_b_Wz"]), (wh[:], ins["L0_attn_b_Wh"]), (cols[:, 0:1], col("L0_attn_b_bz")),
                                 (cols[:, 1:2], col("L0_attn_b_bh")), (gamma[:, 0, :], row("L0_attn_b_gamma")),
                                 (gamma[:, 1, :], row("L0_attn_b_gamma")), (beta[:, 0, :], row("L0_attn_b_beta")),
                                 (beta[:, 1, :], row("L0_attn_b_beta"))):
                    sp.dma_start(dst, src).then_inc(loaded, 16)
                sp.wait_ge(loaded, 128)

            @block.vector
            def _(dve):
                dve.wait_ge(loaded, 128)
                nc.vector.tensor_scalar(cols[:, 2:3], cols[:, 0:1], -1.0, None, ALU.mult).then_inc(setup, 1)
                nc.vector.memset(stats[:], 0.0).then_inc(setup, 1)
                nc.vector.memset(half[:], -0.5).then_inc(setup, 1)

        def tile(b, t):
            return xres[:, bass.ds(2 * b + t, 1), :].rearrange("p a e -> p (a e)")

        def tiles(b):
            return xres[:, bass.ds(2 * b, 2), :].rearrange("p t e -> p (t e)")

        def flat(t):
            return t.rearrange("p t e -> p (t e)")

        def enters(i):
            return not isinstance(i, int) or i < B

        def scans(i):
            return not isinstance(i, int) or 1 <= i <= B

        def ends(i):
            return not isinstance(i, int) or i >= 2

        with nc.Block() as block:
            @block.vector
            def _(dve):
                ch = Chain(dve, chain)

                def combine_rows(b, q):
                    for k in range(2):
                        for t in range(2):
                            dve.wait_ge(arrived[4 * q + 2 * t + k], (b - q) * 8 + 16)
                            if k == 1:
                                dve.wait_ge(first_added, b * 2 + t + 1)
                            nc.vector.scalar_tensor_tensor(
                                tile(b, t), rows[:, q, t, k, :], share[:, k, bass.ds(b * 2 + t, 1)], tile(b, t), ALU.mult, ALU.add
                            ).then_inc((first_added, added)[k], 1)
                    dve.wait_ge(added, b * 2 + 2)
                    dve.sem_inc(combined, 1)

                def statistics(i, q):
                    last = None
                    if ends(i):
                        dve.wait_ge(h_full, i - 1)
                        for t in range(2):
                            last = ch.mark(nc.vector.bn_stats(stats[:, q, 2 + t, :], bh[q][:, t * P:(t + 1) * P]))
                    if enters(i):
                        combine_rows(i, q)
                        for t in range(2):
                            last = ch.mark(nc.vector.bn_stats(stats[:, q, t, :], tile(i, t)))
                    ch.wait(last)
                    moments(nc, ch, stats[:, q], mv[:, q])
                    nc.vector.tensor_scalar(arg[:, q, :], mv[:, q, 3, :], 0.25, EPS, ALU.mult, ALU.add).then_inc(ready, 1)

                def normalise(i, q):
                    if not isinstance(i, int) or i >= 2:
                        dve.wait_ge(based, i - 1)
                    for t in range(2):
                        last = nc.vector.tensor_scalar(xl[:, q, t, :], tile(i, t), mv[:, q, 0, t:t + 1], rs[:, q, t:t + 1],
                                                       ALU.subtract, ALU.mult)
                    last.then_inc(normed, 1)

                def scan(b, q):
                    dve.wait_ge(gates, b + 1)
                    ch.step(nc.vector.tensor_scalar(relu[:], bk[q][:, S:2 * S], cols[:, 1:2], 0.0, ALU.add, ALU.max))
                    ch.step(nc.vector.scalar_tensor_tensor(relu[:], sg[:, q, :], 0.5, relu[:], ALU.min, ALU.add))
                    ch.step(nc.vector.tensor_tensor(val[:], z[:, q, :], relu[:], ALU.mult))
                    nc.vector.tensor_tensor_scan(hs[:, q, :], keep[:, q, :], val[:], 0.0, ALU.mult, ALU.add).then_inc(scanned, 1)

                def finish(b, q):
                    for t in range(2):
                        last = ch.mark(nc.vector.scalar_tensor_tensor(nh[:, t, :], bh[q][:, t * P:(t + 1) * P], mv[:, q, 0, 2 + t:3 + t],
                                                                      gamma[:, t, :], ALU.subtract, ALU.mult))
                    ch.wait(last)
                    dve.wait_ge(based, b + 1)
                    for t in range(2):
                        last = nc.vector.scalar_tensor_tensor(tile(b, t), nh[:, t, :], rs[:, q, 2 + t:3 + t], tile(b, t),
                                                              ALU.mult, ALU.add)
                    last.then_inc(done, 1)

                def step(i, q):
                    statistics(i, q)
                    if scans(i):
                        scan(i - 1, 1 - q)
                    dve.wait_ge(rooted, i + 1)
                    if enters(i):
                        normalise(i, q)
                    if ends(i):
                        finish(i - 2, q)

                step(0, 0)
                step(1, 1)
                before = ch.base + ch.n
                with dve.Fori(0, B // 2 - 1) as it:
                    for q in range(2):
                        i = it * 2 + 2 + q
                        per = 15
                        ch.start((i - 2) * per + before)
                        step(i, q)
                        assert ch.n == per, ch.n
                ch.start((B - 2) * per + before)
                step(B, 0)
                step(B + 1, 1)
                dve.wait_ge(done, B)

            @block.gpsimd
            def _(pool):
                ch = Chain(pool, gchain)

                def pick(b, q):
                    if not isinstance(b, int) or b >= 2:
                        pool.wait_ge(added, b * 2 - 2)
                    pool.sem_inc(turns, 1)
                    nc.gpsimd.tensor_copy(index[:, q, :, :], slot[:, :, bass.ds(b * 2, 2)]).then_inc(picked, 1)
                    pool.wait_ge(picked, b + 1)
                    pool.sem_inc(turns, 1)

                def gather(q, t, k):
                    pool.indirect_dma_start(rows[:, q, t, k, :], None, slot_dram,
                                            bass.IndirectOffsetOnAxis(ap=index[:, q, k, t:t + 1], axis=0)
                                            ).then_inc(arrived[4 * q + 2 * t + k], 16)

                def add_to_tiles(b, q):
                    pool.wait_ge(normed, b + 1)
                    pool.sem_inc(turns, 1)
                    ch.step(nc.gpsimd.tensor_tensor(tiles(b), flat(xl[:, q, :, :]), tiles(b), ALU.add))
                    pool.wait_ge(x_full, b + 1)
                    pool.sem_inc(turns, 1)
                    nc.gpsimd.tensor_tensor(tiles(b), tiles(b), flat(beta[:]), ALU.add).then_inc(based, 1)

                def step(i, q):
                    more = not isinstance(i, int) or i + 1 < B
                    if more:
                        pick(i + 1, 1 - q)
                        gather(1 - q, 0, 0)
                        gather(1 - q, 1, 0)
                        gather(1 - q, 0, 1)
                    pool.wait_ge(ready, i + 1)
                    nc.gpsimd.tensor_tensor(rs[:, q, :], arg[:, q, :], half[:], ALU.pow).then_inc(rooted, 1)
                    if more:
                        gather(1 - q, 1, 1)
                    if enters(i):
                        add_to_tiles(i, q)

                pick(0, 0)
                for t in range(2):
                    for k in range(2):
                        gather(0, t, k)
                step(0, 0)
                step(1, 1)
                before = ch.base + ch.n
                with pool.Fori(0, B // 2 - 2) as it:
                    for q in range(2):
                        i = it * 2 + 2 + q
                        ch.start(i - 2 + before)
                        step(i, q)
                ch.start(B - 4 + before)
                for i in range(B - 2, B + 2):
                    step(i, i % 2)

            @block.tensor
            def _(pe):
                def gates_of(b, q):
                    pe.wait_ge(normed, b + 1)
                    for t in range(2):
                        last = nc.tensor.transpose(bx[q][:, t * P:(t + 1) * P], xl[:, q, t, :], ident[:])
                    last.then_inc(x_full, 1)
                    pe.wait_ge(x_taken, b + 1)
                    if not (isinstance(b, int) and b < 2):
                        pe.wait_ge(scanned, b - 1)
                    nc.tensor.matmul(bk[q][:, 0:S], wz[:], xT[:, q, :], start=True, stop=True)
                    nc.tensor.matmul(bk[q][:, S:2 * S], wh[:], xT[:, q, :], start=True, stop=True).then_inc(k_full, 1)

                def back(b, q):
                    pe.wait_ge(scanned, b + 1)
                    if not (isinstance(b, int) and b < 2):
                        pe.wait_ge(done, b - 1)
                    for t in range(2):
                        last = nc.tensor.transpose(bh[q][:, t * P:(t + 1) * P], hs[:, q, t * P:(t + 1) * P], ident[:])
                    last.then_inc(h_full, 1)

                gates_of(0, 0)
                back(0, 0)
                gates_of(1, 1)
                with pe.Fori(0, B // 2 - 1) as it:
                    for q in range(2):
                        i = it * 2 + 2 + q
                        back(i - 1, 1 - q)
                        gates_of(i, q)
                back(B - 1, 1)

            @block.scalar
            def _(act):
                def chunk(b, q):
                    act.wait_ge(x_full, b + 1)
                    if not (isinstance(b, int) and b < 2):
                        act.wait_ge(scanned, b - 1)
                    nc.scalar.copy(xT[:, q, :], bx[q][:, 0:2 * P]).then_inc(x_taken, 1)
                    act.wait_ge(k_full, b + 1)
                    nc.scalar.activation(z[:, q, :], bk[q][:, 0:S], ACT.Sigmoid, bias=cols[:, 0:1])
                    nc.scalar.activation(keep[:, q, :], bk[q][:, 0:S], ACT.Sigmoid, bias=cols[:, 2:3], scale=-1.0)
                    nc.scalar.activation(sg[:, q, :], bk[q][:, S:2 * S], ACT.Sigmoid, bias=cols[:, 1:2]).then_inc(gates, 1)

                chunk(0, 0)
                chunk(1, 1)
                with act.Fori(1, B // 2) as it:
                    chunk(it * 2, 0)
                    chunk(it * 2 + 1, 1)


_INS = ["L0_attn_a_x", "L0_attn_a_rel_pos", "L0_attn_a_in_proj_w", "L0_attn_a_in_proj_b", "L0_attn_a_out_w",
        "L0_attn_a_out_b", "L0_attn_a_w1", "L0_attn_a_b1", "L0_attn_a_w2", "L0_attn_a_b2", "L0_attn_a_ln1_g",
        "L0_attn_a_ln1_b", "L0_attn_a_ln2_g", "L0_attn_a_ln2_b", "L0_attn_b_Wz", "L0_attn_b_bz", "L0_attn_b_Wh",
        "L0_attn_b_bh", "L0_attn_b_gamma", "L0_attn_b_beta", "L0_ffn_router_w", "L0_ffn_gate_w", "L0_ffn_gate_b",
        "L0_ffn_up_w", "L0_ffn_up_b", "L0_ffn_down_w", "L0_ffn_down_b"]


def kernel(**inputs):
    import numpy as _np
    import concourse.bacc as _bacc
    from concourse import mybir as _mybir
    from concourse.bass_utils import run_bass_kernel_spmd as _run

    nc = _bacc.Bacc("TRN2", target_bir_lowering=False, num_devices=1)
    arrays, args = {}, {}
    for name in _INS:
        a = _np.ascontiguousarray(inputs[name])
        arrays[f"in_{name}"] = a
        args[name] = nc.dram_tensor(f"in_{name}", a.shape, _mybir.dt.from_np(a.dtype), kind="ExternalInput").ap()
    shape = inputs["L0_attn_a_x"].shape
    out = nc.dram_tensor("out", shape, _mybir.dt.float32, kind="ExternalOutput").ap()
    build(nc, args, out)
    r = _run(nc, [arrays], core_ids=[0])
    return r.results[0]["out"]
```

```python
import concourse.bass as bass
from concourse import mybir
from contextlib import ExitStack, contextmanager

F32 = mybir.dt.float32
F32R = mybir.dt.float32r
BF16 = mybir.dt.bfloat16
F16 = mybir.dt.float16
I32 = mybir.dt.int32
ALU = mybir.AluOpType
ACT = mybir.ActivationFunctionType
AXX = mybir.AxisListType.X

P = 128
EPS = 1e-5
MASKED = -1.0e30


class Chain:

    def __init__(self, engine, semaphore):
        self.engine, self.semaphore, self.base, self.n = engine, semaphore, 0, 0

    def start(self, base):
        self.base, self.n = base, 0

    def mark(self, instruction):
        self.n += 1
        instruction.then_inc(self.semaphore, 1)
        return self.base + self.n

    def wait(self, value):
        self.engine.wait_ge(self.semaphore, value)

    def step(self, instruction):
        self.wait(self.mark(instruction))


def moments(nc, ch, stats, mom):
    ch.mark(nc.vector.tensor_tensor(mom[:, 0, :], stats[:, :, 1], stats[:, :, 4], ALU.add))
    ch.mark(nc.vector.tensor_tensor(mom[:, 1, :], stats[:, :, 1], stats[:, :, 4], ALU.subtract))
    ch.step(nc.vector.tensor_tensor(mom[:, 2, :], stats[:, :, 2], stats[:, :, 5], ALU.add))
    ch.mark(nc.vector.tensor_scalar(mom[:, 0, :], mom[:, 0, :], 0.5, None, ALU.mult))
    ch.step(nc.vector.tensor_tensor(mom[:, 1, :], mom[:, 1, :], mom[:, 1, :], ALU.mult))
    ch.step(nc.vector.scalar_tensor_tensor(mom[:, 3, :], mom[:, 2, :], 4.0 / P, mom[:, 1, :], ALU.mult, ALU.add))


@contextmanager
def phase(nc):
    made = []

    def sem(name):
        made.append(nc.alloc_semaphore(name=name))
        return made[-1]

    with ExitStack() as ctx:
        yield ctx, sem
    nc.all_engine_barrier()
    nc.clear_and_free_semaphores(made)
    nc.all_engine_barrier()


class Shapes:
    def __init__(self, x, rel_pos, w1, gate_w):
        self.B, self.S, self.E = x.shape
        self.H, self.ML = rel_pos.shape
        self.HD = self.E // self.H
        self.FF = w1.shape[0]
        self.NE, _, self.EF = gate_w.shape
        self.QT = self.S // P
        self.TILES = self.B * self.QT
        self.N = self.B * self.S
        self.BODY = 8
        self.SLOT_TILES = -(-(2 * self.TILES + self.NE - 1) // self.BODY) * self.BODY


def build(nc, ins, out):
    s = Shapes(ins["L0_attn_a_x"], ins["L0_attn_a_rel_pos"], ins["L0_attn_a_w1"], ins["L0_ffn_gate_w"])
    assert s.E == P and s.QT == 2 and s.H == 16 and s.HD == 8 and s.NE == 8
    with ExitStack() as kept:
        xres = kept.enter_context(nc.sbuf_tensor("xres", [P, s.TILES, s.E], F32))
        ident = kept.enter_context(nc.sbuf_tensor("ident", [P, P], F32))
        identb = kept.enter_context(nc.sbuf_tensor("identb", [P, P], BF16))
        with ExitStack() as mem:
            attention(nc, mem, s, ins, xres, ident, identb)
        with ExitStack() as mem:
            experts = expert_weights(nc, mem, s, ins, ident)
            normed_dram = nc.dram_tensor("normed_rows", (s.N, s.E), F32, kind="Internal").ap()
            slot_dram = nc.dram_tensor("slot_rows", (s.SLOT_TILES * P, s.E), F32, kind="Internal").ap()
            with ExitStack() as routes:
                share, slot = mixture(nc, routes, s, "first_", xres, ident, experts, normed_dram, slot_dram, None)
                recurrence(nc, s, ins, xres, ident, share, slot, slot_dram)
            with ExitStack() as routes:
                choice_dram = nc.dram_tensor("choice_rows", (2 * s.N + s.SLOT_TILES * P, s.E), F32, kind="Internal").ap()
                share, _ = mixture(nc, routes, s, "second_", xres, ident, experts, normed_dram, None, choice_dram)
                combine(nc, s, xres, share, choice_dram, out)


def attention(nc, ctx, s, ins, xres, ident, identb):
    H, HD, FF, B = s.H, s.HD, s.FF, s.B
    AUG = 64
    PAIRS = H // 2
    KROWS, XROWS = 6 * HD, 6 * HD + 2
    VW = 3 * (HD + 1)
    BK = 3 * P

    def sb(name, shape, dt=F32):
        return ctx.enter_context(nc.sbuf_tensor(name, shape, dt))

    def sem(name):
        return ctx.enter_context(nc.semaphore(name))

    wqkv = sb("wqkv", [P, 3 * s.E])
    bqkv = sb("bqkv", [P, 3 * s.E])
    wo = sb("wo", [P, s.E])
    outb = sb("outb", [P, s.E])
    w1 = sb("w1", [P, FF])
    b1 = sb("b1", [P, FF // P])
    w2 = sb("w2", [P, FF // P, s.E])
    b2 = sb("b2", [P, s.E])
    bias32 = sb("bias32", [P, H, BK])
    biasb = sb("biasb", [P, H, 2 * P], BF16)
    neghalf = sb("neghalf", [P, 4])
    unit = sb("unit", [P, 2, s.E])
    aug = sb("aug", [P, 2, 2, 2, H, AUG], BF16)
    vaug = sb("vaug", [P, 2, H, 3, HD + 1], BF16)

    x_dram = ins["L0_attn_a_x"].rearrange("b (t p) e -> p (b t) e", p=P)

    with ExitStack() as c2:
        def sb2(name, shape, dt=F32):
            return c2.enter_context(nc.sbuf_tensor(name, shape, dt))

        def sem2(name):
            return c2.enter_context(nc.semaphore(name))

        wrow = sb2("wrow", [P, 8, s.E])
        w2row = sb2("w2row", [P, FF])
        gcol = sb2("gcol", [P, 4])
        b1ld = sb2("b1ld", [P, FF // P])
        inb = sb2("inb", [P, 3 * s.E])
        ones = sb2("ones", [P, P])
        lnb1 = sb2("lnb1", [P, P])
        anti = sb2("anti", [P, P])
        relpad = sb2("relpad", [H, 3 * P])
        hank = sb2("hank", [P, H, 2 * P])
        pw = [c2.enter_context(nc.psum_tensor(f"pw{i}", [P, 512], F32)) for i in range(4)]
        scratch = nc.dram_tensor("rel_padded", (H, 3 * P), F32, kind="Internal").ap()
        hankel = bass.AP(tensor=scratch.tensor, offset=0, ap=[[1, P], [3 * P, H], [1, 2 * P]])

        loaded = sem2("weights_loaded")
        rel_in, rel_out, rel_tab = sem2("rel_loaded"), sem2("rel_stored"), sem2("hankel_loaded")
        x_in = sem2("x_loaded")
        filled, full, taken = sem2("filled"), sem2("pw_full"), sem2("pw_taken")
        padded = sem2("rel_padded_set")
        vchain = sem2("vector_steps")
        gchain = sem2("gpsimd_steps")
        NLOADS = 14

        def col(name):
            return ins[name].rearrange("(p a) -> p a", a=1)

        def row(name):
            t = ins[name]
            return bass.AP(tensor=t.tensor, offset=t.offset, ap=[[0, P], [1, t.shape[0]]])

        with nc.Block() as block:
            @block.sync
            def _(sp):
                sp.wait_ge(padded, 1)
                sp.dma_start(relpad[:, P - 1:P - 1 + s.S], ins["L0_attn_a_rel_pos"][:, 0:s.S]).then_inc(rel_in, 16)
                sp.wait_ge(rel_in, 16)
                sp.dma_start(scratch, relpad[:]).then_inc(rel_out, 16)
                sp.wait_ge(rel_out, 16)
                sp.dma_start(hank[:], hankel).then_inc(rel_tab, 16)
                sp.wait_ge(loaded, 16 * (NLOADS + 1))
                for q in range(4):
                    n = s.TILES // 4
                    sp.dma_start(xres[:, q * n:(q + 1) * n, :], x_dram[:, q * n:(q + 1) * n, :]).then_inc(x_in, 16)
                sp.wait_ge(x_in, 64)
                sp.wait_ge(rel_tab, 16)

            @block.scalar
            def _(act):
                loads = [
                    (wrow[:, 0:3, :], ins["L0_attn_a_in_proj_w"].rearrange("(c p) e -> p c e", p=P)),
                    (wrow[:, 3, :], ins["L0_attn_a_out_w"]),
                    (wrow[:, 4:8, :], ins["L0_attn_a_w1"].rearrange("(c p) e -> p c e", p=P)),
                    (w2row[:], ins["L0_attn_a_w2"]),
                    (gcol[:, 0:1], col("L0_attn_a_ln1_g")), (gcol[:, 1:2], col("L0_attn_a_ln1_b")),
                    (gcol[:, 2:3], col("L0_attn_a_ln2_g")), (gcol[:, 3:4], col("L0_attn_a_ln2_b")),
                    (inb[:], row("L0_attn_a_in_proj_b")), (outb[:], row("L0_attn_a_out_b")),
                    (b2[:], row("L0_attn_a_b2")),
                ] + [(b1ld[:, c:c + 1], ins["L0_attn_a_b1"][c * P:(c + 1) * P].rearrange("(p a) -> p a", a=1))
                     for c in range(FF // P)]
                for dst, src in loads:
                    act.dma_start(dst, src).then_inc(loaded, 16)
                act.wait_ge(loaded, 16 * len(loads))
                assert len(loads) == NLOADS + 1
                for j in range(PAIRS):
                    act.wait_ge(taken, 2 + j + 1)
                    nc.scalar.copy(biasb[:, 2 * j:2 * j + 2, :], bias32[:, 2 * j:2 * j + 2, 0:2 * P])
                    nc.scalar.copy(bias32[:, 2 * j:2 * j + 2, 2 * P:BK], bias32[:, 2 * j:2 * j + 2, 0:P])

            @block.gpsimd
            def _(pool):
                ch = Chain(pool, gchain)
                nc.gpsimd.memset(relpad[:], MASKED).then_inc(padded, 1)
                ch.step(nc.gpsimd.memset(ident[:], 0.0))
                ch.step(nc.gpsimd.affine_select(out=ident[:], in_=ident[:], compare_op=ALU.not_equal, fill=1.0,
                                                base=0, pattern=[[-1, P]], channel_multiplier=1))
                ch.step(nc.gpsimd.memset(anti[:], 0.0))
                nc.gpsimd.affine_select(out=anti[:], in_=anti[:], compare_op=ALU.not_equal, fill=1.0,
                                        base=-(P - 1), pattern=[[1, P]], channel_multiplier=1).then_inc(filled, 1)
                ch.step(nc.gpsimd.memset(aug[:], 0.0))
                for q in range(2):
                    for t in range(2):
                        ch.step(nc.gpsimd.memset(aug[:, q, 1, t, :, KROWS:XROWS], 1.0))
                ch.step(nc.gpsimd.memset(vaug[:], 0.0))
                for t in range(2):
                    ch.step(nc.gpsimd.memset(vaug[:, t, :, 0, HD:HD + 1], 1.0))
                ch.step(nc.gpsimd.memset(unit[:], 1.0))
                nc.gpsimd.memset(neghalf[:], -0.5).then_inc(filled, 1)

            @block.vector
            def _(dve):
                ch = Chain(dve, vchain)
                dve.wait_ge(filled, 1)
                ch.step(nc.vector.tensor_copy(identb[:], ident[:]))
                dve.wait_ge(loaded, 16 * (NLOADS + 1))
                ch.step(nc.vector.memset(ones[:], 1.0))
                nc.vector.tensor_scalar(lnb1[:], ones[:], gcol[:, 1:2], None, ALU.mult).then_inc(filled, 1)
                dve.wait_ge(full, 1)
                ch.step(nc.vector.tensor_copy(wqkv[:], pw[0][:, 0:3 * s.E]))
                nc.vector.tensor_copy(wo[:], pw[0][:, 3 * s.E:4 * s.E]).then_inc(taken, 1)
                dve.wait_ge(full, 2)
                ch.step(nc.vector.tensor_copy(w1[:], pw[1][:]))
                nc.vector.tensor_copy(w2[:].rearrange("p c e -> p (c e)"), pw[2][:]).then_inc(taken, 1)
                dve.wait_ge(full, 3)
                ch.step(nc.vector.tensor_tensor(bqkv[:], pw[3][:, 0:3 * s.E], inb[:], ALU.add))
                ch.step(nc.vector.tensor_scalar(bqkv[:, 0:s.E], bqkv[:, 0:s.E], HD ** -0.5, None, ALU.mult))
                ch.step(nc.vector.tensor_tensor(b1[:], pw[0][:, 0:FF // P], b1ld[:], ALU.add))
                ch.step(nc.vector.tensor_scalar(wqkv[:], wqkv[:], gcol[:, 0:1], None, ALU.mult))
                ch.step(nc.vector.tensor_scalar(wqkv[:, 0:s.E], wqkv[:, 0:s.E], HD ** -0.5, None, ALU.mult))
                ch.step(nc.vector.tensor_scalar(w1[:], w1[:], gcol[:, 2:3], None, ALU.mult))
                for j in range(PAIRS):
                    dve.wait_ge(full, 4 + j)
                    src = pw[1 + j % 2][:].rearrange("p (h q) -> p h q", h=2)
                    nc.vector.tensor_copy(bias32[:, 2 * j:2 * j + 2, 0:2 * P], src).then_inc(taken, 1)

            @block.tensor
            def _(pe):
                pe.wait_ge(loaded, 16 * (NLOADS + 1))
                pe.wait_ge(filled, 3)
                for c in range(4):
                    last = nc.tensor.transpose(pw[0][:, c * P:(c + 1) * P], wrow[:, c, :], ident[:])
                last.then_inc(full, 1)
                for c in range(4):
                    nc.tensor.transpose(pw[1][:, c * P:(c + 1) * P], wrow[:, 4 + c, :], ident[:])
                for c in range(4):
                    last = nc.tensor.transpose(pw[2][:, c * P:(c + 1) * P], w2row[:, c * P:(c + 1) * P], ident[:])
                last.then_inc(full, 1)
                pe.wait_ge(taken, 2)
                nc.tensor.matmul(pw[3][:, 0:3 * s.E], lnb1[:], wqkv[:], start=True, stop=True)
                for c in range(FF // P):
                    last = nc.tensor.matmul(pw[0][:, c:c + 1], w1[:, c * P:(c + 1) * P], gcol[:, 3:4],
                                            start=True, stop=True)
                last.then_inc(full, 1)
                pe.wait_ge(rel_tab, 16)
                for j in range(PAIRS):
                    if j >= 2:
                        pe.wait_ge(taken, 2 + j - 1)
                    nc.tensor.matmul(pw[1 + j % 2][:], anti[:],
                                     hank[:, 2 * j:2 * j + 2, :].rearrange("p h q -> p (h q)"),
                                     start=True, stop=True).then_inc(full, 1)

    xn = sb("xn", [P, 2, s.E])
    xnT = sb("xnT", [P, 2 * P])
    xlb = sb("xlb", [P, 2, 2, s.E])
    qkv = sb("qkv", [P, 2, 3, 2, s.E])
    rest = sb("rest", [P, 2, 2, s.E])
    vrest = sb("vrest", [P, 2, s.E])
    qT = sb("qT", [P, 2, PAIRS, 2 * P], BF16)
    kT = sb("kT", [P, 2, PAIRS, 2 * P], BF16)
    stats = sb("stats", [P, 2, 6])
    mv = sb("mv", [P, 2, 4, 2])
    arg = sb("arg", [P, 2, 2])
    rs = sb("rs", [P, 2, 2, 2])
    stats2 = sb("stats2", [P, 2, 6])
    mv2 = sb("mv2", [P, 4, 2])
    arg2 = sb("arg2", [P, 2])
    rs2 = sb("rs2", [P, 2])
    mx = sb("mx", [P, H, 3])
    mq = sb("mq", [P, 2, H])
    ebuf = sb("ebuf", [P, 2, 2, BK])
    p32 = sb("p32", [P, 2, 2, BK])
    phi = sb("phi", [P, 4, 2, BK], F16)
    plo = sb("plo", [P, 4, 2, BK], F16)
    osum = sb("osum", [P, 2, H, HD + 1])
    rden = sb("rden", [P, 2, H, 1])
    onrm = sb("onrm", [P, 2, s.E])
    oT = sb("oT", [P, 2 * P])
    y1 = sb("y1", [P, 2, s.E])
    xb2 = sb("xb2", [P, 2, s.E])
    ysum = sb("ysum", [P, 2, s.E])
    xm = sb("xm", [P, 2, s.E])
    xmT = sb("xmT", [P, 2 * P])
    hT = sb("hT", [P, FF // P, 2 * P])

    score_banks = ctx.enter_context(nc.psum_tensor("score_banks", [P, 2, 512], F32))
    max_banks = ctx.enter_context(nc.psum_tensor("max_banks", [P, 2, 512], F32))
    bankT = ctx.enter_context(nc.psum_tensor("bankT", [P, 512], F32))
    bankW = ctx.enter_context(nc.psum_tensor("bankW", [P, 512], F32))
    bankO = [ctx.enter_context(nc.psum_tensor(f"bankO{t}", [P, 512], F32)) for t in range(2)]

    T_full, T_free, W_full, W_free = sem("T_full"), sem("T_free"), sem("W_full"), sem("W_free")
    scores_full, maxed_full, maxed_free = sem("scores_full"), sem("maxed_full"), sem("maxed_free")
    kT_full, kT_taken, maxT_full, maxT_taken = sem("kT_full"), sem("kT_taken"), sem("maxT_full"), sem("maxT_taken")
    biased, exped, lowed, weighed = sem("scores_biased"), sem("exp_done"), sem("low_done"), sem("pv_done")
    O_free = sem("O_free")
    arg1_ready, rs1_ready, xn_ready, xlb_ready, xl_ready = (sem("arg1_ready"), sem("rs1_ready"), sem("xn_ready"),
                                                            sem("xlb_ready"), sem("xl_ready"))
    v_ready, vaug_ready = sem("v_ready"), sem("vaug_ready")
    aug_ready, aug_copied, rest_ready, max_ready = sem("aug_ready"), sem("aug_copied"), sem("rest_ready"), sem("max_ready")
    on_ready, y1_ready, arg2_ready, rs2_ready = sem("on_ready"), sem("y1_ready"), sem("arg2_ready"), sem("rs2_ready")
    xm_ready, ysum_ready, x_done = sem("xm_ready"), sem("ysum_ready"), sem("x_done")
    vchain, gchain = sem("attn_vector_steps"), sem("attn_gpsimd_steps")

    def attends(b):
        return not isinstance(b, int) or 0 <= b < B

    def outputs(b):
        return not isinstance(b, int) or 1 <= b

    def maximises(b):
        return not isinstance(b, int) or -1 <= b <= B - 2

    def prepares(b):
        return not isinstance(b, int) or -2 <= b <= B - 3

    T_USES = ("oT", "project", "xmT", "up", "q")
    W_USES = ("att", "norm", "project", "up", "down", "q")

    def uses_of(order, b):
        has = {"oT": outputs, "att": outputs, "xmT": outputs, "up": outputs, "down": outputs}
        return [u for u in order if has.get(u, prepares)(b)]

    def use(order, name, b):
        if isinstance(b, int):
            return sum(len(uses_of(order, c)) for c in range(-2, b)) + uses_of(order, b).index(name)
        return sum(len(uses_of(order, c)) for c in range(-2, 1)) + len(order) * (b - 1) + order.index(name)

    def useT(name, b):
        return use(T_USES, name, b)

    def useW(name, b):
        return use(W_USES, name, b)

    def some(n):
        return not isinstance(n, int) or n > 0

    FIRST, SECOND, THIRD = ((0, 1, 2), (0, 3, 5)), ((3, 4), (1, 4)), (5, 2)

    def slot(q, which, i):
        return aug[:, q, which, :, :, i * HD:(i + 1) * HD].rearrange("p t h d -> p (t h) d")

    def heads(t):
        return t.rearrange("p t (h d) -> p (t h) d", d=HD)

    def tiles(b):
        return xres[:, bass.ds(2 * b, 2), :]

    def tile(b, t):
        return xres[:, bass.ds(2 * b + t, 1), :].rearrange("p a e -> p (a e)")

    with nc.Block() as block:

        @block.tensor
        def _(pe):
            def takeT(name, b):
                n = useT(name, b)
                if some(n):
                    pe.wait_ge(T_free, n)

            def takeW(name, b):
                n = useW(name, b)
                if some(n):
                    pe.wait_ge(W_free, n)

            def norm_T(b):
                pe.wait_ge(xn_ready, b + 3)
                takeW("norm", b)
                for t in range(2):
                    last = nc.tensor.transpose(bankW[:, t * P:(t + 1) * P], xn[:, t, :], ident[:])
                last.then_inc(W_full, 1)

            def project_0(b):
                pe.wait_ge(W_free, useW("norm", b) + 1)
                takeT("project", b)
                nc.tensor.matmul(bankT[:, 0:3 * s.E], xnT[:, 0:P], wqkv[:], start=True, stop=True).then_inc(T_full, 1)

            def project_1(b):
                takeW("project", b)
                nc.tensor.matmul(bankW[:, 0:3 * s.E], xnT[:, P:2 * P], wqkv[:], start=True, stop=True).then_inc(W_full, 1)

            def aug_T(bank, q, which, t):
                dst = bank.bitcast(BF16).rearrange("p (g q) -> p g q", g=PAIRS)
                for g in range(PAIRS):
                    last = nc.tensor.transpose(dst[:, g, :], aug[:, q, which, t, 2 * g:2 * g + 2, :].rearrange("p h a -> p (h a)"),
                                               identb[:])
                return last

            def q_T(b, p):
                pe.wait_ge(aug_ready, 2 * b + 5)
                pe.wait_ge(aug_copied, 2 * b + 5)
                takeT("q", b)
                aug_T(bankT[:], p, 0, 0).then_inc(T_full, 1)
                takeW("q", b)
                aug_T(bankW[:], p, 0, 1).then_inc(W_full, 1)

            def k_T(b, p):
                pe.wait_ge(aug_ready, 2 * b + 6)
                pe.wait_ge(aug_copied, 2 * b + 6)
                if maximises(b):
                    pe.wait_ge(maxed_free, 8 * b + 16)
                for t in range(2):
                    aug_T(max_banks[:, t, :], p, 1, t).then_inc(kT_full, 1)

            def max_T(b, p):
                pe.wait_ge(max_ready, b + 2)
                if attends(b):
                    pe.wait_ge(biased, 8 * b + 9)
                for t in range(2):
                    aug_T(score_banks[:, t, :], 1 - p, 0, t).then_inc(maxT_full, 1)

            def scores_for_max(b, q, j):
                r = max_banks
                if j == 0:
                    pe.wait_ge(T_free, useT("q", b - 2) + 1)
                    pe.wait_ge(W_free, useW("q", b - 2) + 1)
                    pe.wait_ge(kT_taken, 2 * b + 2)
                if some(8 * b + j):
                    pe.wait_ge(maxed_free, 8 * b + j)
                for hh in range(2):
                    h = 2 * j + hh
                    nc.tensor.matmul(r[:, hh, 0:P], biasb[:, h, P:2 * P], identb[:], start=True, stop=False,
                                     skip_group_check=True)
                    nc.tensor.matmul(r[:, hh, P:2 * P], biasb[:, h, 0:P], identb[:], start=False, stop=False,
                                     skip_group_check=True)
                    nc.tensor.matmul(r[:, hh, 2 * P:BK], biasb[:, h, 0:P], identb[:], start=False, stop=False,
                                     skip_group_check=True)
                for hh in range(2):
                    rows = slice(AUG * hh, AUG * hh + KROWS)
                    nc.tensor.matmul(r[:, hh, 0:2 * P], qT[rows, q, j, P:2 * P], kT[rows, q, j, :],
                                     start=False, stop=True, skip_group_check=True)
                for hh in range(2):
                    rows = slice(AUG * hh, AUG * hh + KROWS)
                    last = nc.tensor.matmul(r[:, hh, 2 * P:BK], qT[rows, q, j, 0:P], kT[rows, q, j, 0:P],
                                            start=False, stop=True, skip_group_check=True)
                last.then_inc(maxed_full, 1)

            def scores(b, p, j):
                r = score_banks
                if j == 0:
                    pe.wait_ge(maxT_taken, 2 * b + 2)
                pe.wait_ge(biased, 8 * b + j + 1)
                for hh in range(2):
                    rows = slice(AUG * hh, AUG * hh + XROWS)
                    nc.tensor.matmul(r[:, hh, 0:2 * P], kT[rows, p, j, 0:P], qT[rows, p, j, :], start=True, stop=True)
                for hh in range(2):
                    rows = slice(AUG * hh, AUG * hh + XROWS)
                    last = nc.tensor.matmul(r[:, hh, 2 * P:BK], kT[rows, p, j, P:2 * P], qT[rows, p, j, P:2 * P],
                                            start=True, stop=True)
                last.then_inc(scores_full, 1)

            def weigh(b, j):
                if j == 0:
                    pe.wait_ge(vaug_ready, b + 1)
                    pe.wait_ge(O_free, b + 1)
                pe.wait_ge(lowed, 8 * b + j + 3)
                for hh in range(2):
                    h = 2 * j + hh
                    for t, blocks in ((0, ((0, 0),)), (1, ((P, 0), (2 * P, 1)))):
                        n = 2 * len(blocks)
                        i = 0
                        for part in (phi, plo):
                            for col, kt in blocks:
                                last = nc.tensor.matmul(bankO[t][:, h * VW:(h + 1) * VW], part[:, j % 4, hh, col:col + P],
                                                        vaug[:, kt, h, :, :].rearrange("p s d -> p (s d)"),
                                                        start=(i == 0), stop=(i == n - 1))
                                i += 1
                last.then_inc(weighed, 1)

            def out_T(b):
                pe.wait_ge(on_ready, b)
                takeT("oT", b)
                for t in range(2):
                    last = nc.tensor.transpose(bankT[:, t * P:(t + 1) * P], onrm[:, t, :], ident[:])
                last.then_inc(T_full, 1)

            def out_proj(b):
                pe.wait_ge(T_free, useT("oT", b) + 1)
                takeW("att", b)
                for t in range(2):
                    last = nc.tensor.matmul(bankW[:, t * P:(t + 1) * P], oT[:, t * P:(t + 1) * P], wo[:],
                                            start=True, stop=True)
                last.then_inc(W_full, 1)

            def mlp_T(b):
                pe.wait_ge(xm_ready, b)
                takeT("xmT", b)
                for t in range(2):
                    last = nc.tensor.transpose(bankT[:, t * P:(t + 1) * P], xm[:, t, :], ident[:])
                last.then_inc(T_full, 1)

            def mlp_up_0(b):
                pe.wait_ge(T_free, useT("xmT", b) + 1)
                takeW("up", b)
                for f in range(2):
                    last = nc.tensor.matmul(bankW[:, f * 2 * P:(f + 1) * 2 * P], w1[:, f * P:(f + 1) * P], xmT[:],
                                            start=True, stop=True)
                last.then_inc(W_full, 1)

            def mlp_up_1(b):
                takeT("up", b)
                for f in range(2):
                    last = nc.tensor.matmul(bankT[:, f * 2 * P:(f + 1) * 2 * P], w1[:, (2 + f) * P:(3 + f) * P], xmT[:],
                                            start=True, stop=True)
                last.then_inc(T_full, 1)

            def mlp_down(b):
                pe.wait_ge(T_free, useT("up", b) + 1)
                takeW("down", b)
                for t in range(2):
                    for f in range(FF // P):
                        last = nc.tensor.matmul(bankW[:, t * P:(t + 1) * P], hT[:, f, t * P:(t + 1) * P], w2[:, f, :],
                                                start=(f == 0), stop=(f == FF // P - 1))
                last.then_inc(W_full, 1)

            def body(b, p):
                if attends(b):
                    scores(b, p, 0)
                if maximises(b):
                    scores_for_max(b + 1, 1 - p, 0)
                if attends(b):
                    scores(b, p, 1)
                if maximises(b):
                    scores_for_max(b + 1, 1 - p, 1)
                if outputs(b):
                    out_T(b)
                if attends(b):
                    scores(b, p, 2)
                if maximises(b):
                    scores_for_max(b + 1, 1 - p, 2)
                if attends(b):
                    weigh(b, 0)
                if outputs(b):
                    out_proj(b)
                if attends(b):
                    scores(b, p, 3)
                if maximises(b):
                    scores_for_max(b + 1, 1 - p, 3)
                if attends(b):
                    weigh(b, 1)
                    scores(b, p, 4)
                if prepares(b):
                    norm_T(b)
                if maximises(b):
                    scores_for_max(b + 1, 1 - p, 4)
                if attends(b):
                    weigh(b, 2)
                if prepares(b):
                    project_0(b)
                if attends(b):
                    scores(b, p, 5)
                if maximises(b):
                    scores_for_max(b + 1, 1 - p, 5)
                if attends(b):
                    weigh(b, 3)
                if prepares(b):
                    project_1(b)
                if outputs(b):
                    mlp_T(b)
                if attends(b):
                    scores(b, p, 6)
                if maximises(b):
                    scores_for_max(b + 1, 1 - p, 6)
                if attends(b):
                    weigh(b, 4)
                if outputs(b):
                    mlp_up_0(b)
                    mlp_up_1(b)
                if attends(b):
                    scores(b, p, 7)
                if maximises(b):
                    scores_for_max(b + 1, 1 - p, 7)
                if attends(b):
                    weigh(b, 5)
                if outputs(b):
                    mlp_down(b)
                if prepares(b):
                    q_T(b, p)
                    k_T(b, p)
                if attends(b):
                    weigh(b, 6)
                if maximises(b):
                    max_T(b, p)
                if attends(b):
                    weigh(b, 7)

            for b in (-2, -1, 0):
                body(b, b % 2)
            with pe.Fori(0, (B - 4) // 2) as it:
                body(it * 2 + 1, 1)
                body(it * 2 + 2, 0)
            for b in (B - 3, B - 2, B - 1, B):
                body(b, b % 2)

        @block.vector
        def _(dve):
            ch = Chain(dve, vchain)

            def norm_stats(b, p):
                for t in range(2):
                    last = ch.mark(nc.vector.bn_stats(stats[:, t, :], tile(b + 2, t)))
                ch.wait(last)
                moments(nc, ch, stats, mv[:, p])
                nc.vector.tensor_scalar(arg[:, 0, :], mv[:, p, 3, :], 0.25, EPS, ALU.mult, ALU.add)
                nc.vector.tensor_scalar(arg[:, 1, :], mv[:, p, 3, :], 0.25 * (1.0 + EPS), EPS * EPS, ALU.mult, ALU.add).then_inc(arg1_ready, 1)

            def norm_apply(b, p):
                dve.wait_ge(rs1_ready, b + 3)
                for t in range(2):
                    last = nc.vector.tensor_scalar(xn[:, t, :], tile(b + 2, t), mv[:, p, 0, t:t + 1], rs[:, p, 1, t:t + 1],
                                                   ALU.subtract, ALU.mult)
                last.then_inc(xn_ready, 1)

            def normed_input(b, p):
                for t in range(2):
                    last = nc.vector.tensor_scalar(xlb[:, p, t, :], tile(b, t), mv[:, p, 0, t:t + 1], rs[:, p, 0, t:t + 1],
                                                   ALU.subtract, ALU.mult)
                last.then_inc(xl_ready, 1)

            def take_qkv_0(b, p):
                if some(b + 1):
                    dve.wait_ge(vaug_ready, b + 1)
                dve.wait_ge(T_full, useT("project", b) + 1)
                nc.vector.tensor_tensor(qkv[:, p, :, 0, :], bankT[:, 0:3 * s.E].rearrange("p (c e) -> p c e", c=3),
                                        bqkv[:].rearrange("p (c e) -> p c e", c=3), ALU.add).then_inc(T_free, 1)

            def take_qkv_1(b, p):
                dve.wait_ge(W_full, useW("project", b) + 1)
                nc.vector.tensor_tensor(qkv[:, p, :, 1, :], bankW[:, 0:3 * s.E].rearrange("p (c e) -> p c e", c=3),
                                        bqkv[:].rearrange("p (c e) -> p c e", c=3), ALU.add).then_inc(W_free, 1)
                dve.wait_ge(W_free, useW("project", b) + 1)
                dve.wait_ge(T_free, useT("project", b) + 1)
                dve.sem_inc(v_ready, 1)

            def split(b, p, which):
                x, r = heads(qkv[:, p, which, :, :]), heads(rest[:, which, :, :])
                first, second, third = FIRST[which][0], SECOND[which][0], THIRD[which]
                if some(b + 2):
                    dve.wait_ge(aug_copied, 2 * b + 3 + which)
                ch.step(nc.vector.tensor_copy(slot(p, which, first), x))
                ch.step(nc.vector.tensor_tensor(r, x, slot(p, which, first), ALU.subtract))
                dve.sem_inc(rest_ready, 1)
                ch.step(nc.vector.tensor_copy(slot(p, which, second), r))
                nc.vector.tensor_tensor(slot(p, which, third), r, slot(p, which, second), ALU.subtract).then_inc(aug_ready, 1)

            def take_q(b, p):
                dve.wait_ge(W_full, useW("q", b) + 1)
                nc.vector.tensor_copy(qT[:, p, :, P:2 * P],
                                      bankW[:].bitcast(BF16).rearrange("p (g q) -> p g q", g=PAIRS)).then_inc(W_free, 1)

            def take_k(b, p):
                dve.wait_ge(kT_full, 2 * b + 6)
                nc.vector.tensor_copy(kT[:, p, :, P:2 * P],
                                      max_banks[:, 1, :].bitcast(BF16).rearrange("p (g q) -> p g q", g=PAIRS)).then_inc(kT_taken, 1)

            def reduce_max(b, j):
                dve.wait_ge(maxed_full, 8 * b + j + 1)
                if j == 0 and some(b):
                    dve.wait_ge(max_ready, b)
                nc.vector.reduce_max(mx[:, 2 * j:2 * j + 2, :],
                                     max_banks[:, :, 0:BK].rearrange("p h (k c) -> p h k c", k=3), AXX).then_inc(maxed_free, 1)

            def take_max(b, q):
                dve.wait_ge(maxed_free, 8 * b + 8)
                nc.vector.tensor_tensor(mq[:, 1, :], mx[:, :, 0], mx[:, :, 1], ALU.max)
                ch.step(nc.vector.tensor_copy(mq[:, 0, :], mx[:, :, 2]))
                part = aug[:, q, 0, :, :, KROWS:XROWS]
                ch.step(nc.vector.tensor_scalar(part[:, :, :, 0], mq[:], -1.0, None, ALU.mult))
                nc.vector.scalar_tensor_tensor(part[:, :, :, 1], mq[:], -1.0, part[:, :, :, 0],
                                               ALU.mult, ALU.subtract).then_inc(max_ready, 1)

            def take_max_T(b, p):
                dve.wait_ge(maxT_full, 2 * b + 4)
                nc.vector.tensor_copy(qT[:, 1 - p, :, P:2 * P],
                                      score_banks[:, 1, :].bitcast(BF16).rearrange("p (g q) -> p g q", g=PAIRS)).then_inc(maxT_taken, 1)

            def add_mask(b, j):
                dve.wait_ge(scores_full, 8 * b + j + 1)
                if j >= 2:
                    dve.wait_ge(exped, 8 * b + j - 1)
                nc.vector.tensor_tensor(ebuf[:, j % 2, :, :], score_banks[:, :, 0:BK], bias32[:, 2 * j:2 * j + 2, :],
                                        ALU.add).then_inc(biased, 1)

            def normalise(b):
                dve.wait_ge(weighed, 8 * b + 8)
                for t in range(2):
                    last = nc.vector.reduce_sum(osum[:, t, :, :], bankO[t][:, 0:H * VW].rearrange(
                        "p (h s d) -> p h d s", h=H, s=3), AXX)
                last.then_inc(O_free, 1)
                dve.wait_ge(O_free, b + 2)
                ch.step(nc.vector.reciprocal(rden[:].rearrange("p t h a -> p (t h a)"),
                                             osum[:, :, :, HD].rearrange("p t h -> p (t h)")))
                nc.vector.tensor_tensor(heads(onrm[:]), osum[:, :, :, 0:HD].rearrange("p t h d -> p (t h) d"),
                                        rden[:].rearrange("p t h a -> p (t h) a").broadcast_to([P, 2 * H, HD]),
                                        ALU.mult).then_inc(on_ready, 1)

            def second_norm(b, p):
                dve.wait_ge(W_full, useW("att", b) + 1)
                dve.wait_ge(xlb_ready, b)
                ch.step(nc.vector.tensor_tensor(y1[:].rearrange("p t e -> p (t e)"), bankW[:, 0:2 * P],
                                                xlb[:, 1 - p, :, :].rearrange("p t e -> p (t e)"), ALU.add))
                dve.sem_inc(W_free, 1)
                dve.sem_inc(y1_ready, 1)
                for t in range(2):
                    last = ch.mark(nc.vector.bn_stats(stats2[:, t, :], y1[:, t, :]))
                ch.wait(last)
                moments(nc, ch, stats2, mv2)
                nc.vector.tensor_scalar(arg2[:], mv2[:, 3, :], 0.25, EPS, ALU.mult, ALU.add).then_inc(arg2_ready, 1)

            def second_apply(b):
                dve.wait_ge(rs2_ready, b)
                for t in range(2):
                    last = nc.vector.tensor_scalar(xm[:, t, :], y1[:, t, :], mv2[:, 0, t:t + 1], rs2[:, t:t + 1],
                                                   ALU.subtract, ALU.mult)
                last.then_inc(xm_ready, 1)

            def finish(b):
                dve.wait_ge(W_full, useW("down", b) + 1)
                dve.wait_ge(ysum_ready, b)
                nc.vector.tensor_tensor(tiles(b - 1).rearrange("p t e -> p (t e)"), bankW[:, 0:2 * P],
                                        ysum[:].rearrange("p t e -> p (t e)"), ALU.add).then_inc(x_done, 1)
                dve.wait_ge(x_done, b)
                dve.sem_inc(W_free, 1)

            def body(b, p):
                for j in range(PAIRS):
                    if prepares(b) and j == 5:
                        take_qkv_0(b, p)
                    if attends(b):
                        add_mask(b, j)
                    if maximises(b):
                        reduce_max(b + 1, j)
                    if outputs(b):
                        if j == 0:
                            normalise(b - 1)
                        if j == 3:
                            second_norm(b, p)
                        if j == 4:
                            second_apply(b)
                    if prepares(b):
                        if j == 1:
                            norm_stats(b, p)
                        if j == 2:
                            norm_apply(b, p)
                        if j == 5:
                            take_qkv_1(b, p)
                        if j == 5:
                            split(b, p, 0)
                        if j == 6:
                            split(b, p, 1)
                if maximises(b):
                    take_max(b + 1, 1 - p)
                if outputs(b):
                    finish(b)
                if prepares(b):
                    take_q(b, p)
                if attends(b + 1):
                    normed_input(b + 1, 1 - p)
                if prepares(b):
                    take_k(b, p)
                if maximises(b):
                    take_max_T(b, p)

            dve.sem_inc(O_free, 1)
            dve.sem_inc(biased, 1)
            for b in (-2, -1, 0):
                body(b, b % 2)
            before = ch.base + ch.n
            with dve.Fori(0, (B - 4) // 2) as it:
                for u in range(2):
                    b = it * 2 + 1 + u
                    per = 26
                    ch.start((b - 1) * per + before)
                    body(b, 1 - u)
                    assert ch.n == per, ch.n
            ch.start((B - 4) * per + before)
            for b in (B - 3, B - 2, B - 1, B):
                body(b, b % 2)

        @block.scalar
        def _(act):
            def take_norm(b):
                act.wait_ge(W_full, useW("norm", b) + 1)
                nc.scalar.copy(xnT[:], bankW[:, 0:2 * P]).then_inc(W_free, 1)

            def take_q(b, p):
                act.wait_ge(T_full, useT("q", b) + 1)
                nc.scalar.copy(qT[:, p, :, 0:P],
                               bankT[:].bitcast(BF16).rearrange("p (g q) -> p g q", g=PAIRS)).then_inc(T_free, 1)

            def take_k(b, p):
                act.wait_ge(kT_full, 2 * b + 5)
                nc.scalar.copy(kT[:, p, :, 0:P],
                               max_banks[:, 0, :].bitcast(BF16).rearrange("p (g q) -> p g q", g=PAIRS)).then_inc(kT_taken, 1)

            def take_max_T(b, p):
                act.wait_ge(maxT_full, 2 * b + 3)
                nc.scalar.copy(qT[:, 1 - p, :, 0:P],
                               score_banks[:, 0, :].bitcast(BF16).rearrange("p (g q) -> p g q", g=PAIRS)).then_inc(maxT_taken, 1)

            def repeat_parts(b, p, which):
                act.wait_ge(v_ready, b + 3)
                for i in FIRST[which][1:]:
                    nc.scalar.copy(slot(p, which, i), heads(qkv[:, p, which, :, :]))
                act.wait_ge(rest_ready, 2 * b + 5 + which)
                nc.scalar.copy(slot(p, which, SECOND[which][1]), heads(rest[:, which, :, :])).then_inc(aug_copied, 1)

            def exponentials(b, j):
                use = 8 * b + j
                act.wait_ge(biased, use + 2)
                act.wait_ge(lowed, use + 1)
                nc.scalar.activation(p32[:, j % 2, :, :], ebuf[:, j % 2, :, :], ACT.Exp)
                if j >= 4:
                    act.wait_ge(weighed, use - 3)
                nc.scalar.activation(phi[:, j % 4, :, :], ebuf[:, j % 2, :, :], ACT.Exp).then_inc(exped, 1)

            def body(b, p):
                for j in range(PAIRS):
                    if attends(b):
                        exponentials(b, j)
                    if outputs(b):
                        if j == 1:
                            act.wait_ge(T_full, useT("oT", b) + 1)
                            nc.scalar.copy(oT[:], bankT[:, 0:2 * P]).then_inc(T_free, 1)
                        if j == 5:
                            act.wait_ge(T_full, useT("xmT", b) + 1)
                            nc.scalar.copy(xmT[:], bankT[:, 0:2 * P]).then_inc(T_free, 1)
                        if j == 6:
                            act.wait_ge(W_full, useW("up", b) + 1)
                            for f in range(2):
                                last = nc.scalar.activation(hT[:, f, :], bankW[:, f * 2 * P:(f + 1) * 2 * P], ACT.Relu,
                                                            bias=b1[:, f:f + 1])
                            last.then_inc(W_free, 1)
                            act.wait_ge(T_full, useT("up", b) + 1)
                            for f in range(2):
                                last = nc.scalar.activation(hT[:, 2 + f, :], bankT[:, f * 2 * P:(f + 1) * 2 * P], ACT.Relu,
                                                            bias=b1[:, 2 + f:3 + f])
                            last.then_inc(T_free, 1)
                    if prepares(b) and j == 3:
                        take_norm(b)
                    if prepares(b) and j == 5:
                        repeat_parts(b, p, 0)
                    if prepares(b) and j == 6:
                        repeat_parts(b, p, 1)
                if prepares(b):
                    take_q(b, p)
                    take_k(b, p)
                if maximises(b):
                    take_max_T(b, p)

            for b in (-2, -1, 0):
                body(b, b % 2)
            with act.Fori(0, (B - 4) // 2) as it:
                body(it * 2 + 1, 1)
                body(it * 2 + 2, 0)
            for b in (B - 3, B - 2, B - 1, B):
                body(b, b % 2)

        @block.gpsimd
        def _(pool):
            ch = Chain(pool, gchain)

            def low_part(b, j):
                use = 8 * b + j
                pool.wait_ge(exped, use + 1)
                if j >= 4:
                    pool.wait_ge(weighed, use - 3)
                nc.gpsimd.tensor_tensor(plo[:, j % 4, :, :], p32[:, j % 2, :, :], phi[:, j % 4, :, :],
                                        ALU.subtract).then_inc(lowed, 1)

            def split_v(b, p):
                pool.wait_ge(v_ready, b + 1)
                if some(b):
                    pool.wait_ge(weighed, 8 * b)
                v = heads(qkv[:, p, 2, :, :])

                def part(i):
                    return vaug[:, :, :, i, 0:HD].rearrange("p t h d -> p (t h) d")

                ch.step(nc.gpsimd.tensor_tensor(part(0), v, heads(unit[:]), ALU.mult))
                ch.step(nc.gpsimd.tensor_tensor(heads(vrest[:]), v, part(0), ALU.subtract))
                ch.step(nc.gpsimd.tensor_tensor(part(1), heads(vrest[:]), heads(unit[:]), ALU.mult))
                nc.gpsimd.tensor_tensor(part(2), heads(vrest[:]), part(1), ALU.subtract).then_inc(vaug_ready, 1)

            def roots(b, p):
                pool.wait_ge(arg1_ready, b + 3)
                nc.gpsimd.tensor_tensor(rs[:, p].rearrange("p a t -> p (a t)"), arg[:].rearrange("p a t -> p (a t)"),
                                        neghalf[:], ALU.pow).then_inc(rs1_ready, 1)

            def normed(b, p):
                pool.wait_ge(xl_ready, b + 1)
                for t in range(2):
                    last = nc.gpsimd.tensor_tensor(xlb[:, p, t, :], xlb[:, p, t, :], outb[:], ALU.add)
                last.then_inc(xlb_ready, 1)

            def second_root(b):
                pool.wait_ge(arg2_ready, b)
                nc.gpsimd.tensor_tensor(rs2[:], arg2[:], neghalf[:, 0:2], ALU.pow).then_inc(rs2_ready, 1)

            def biased_input(b):
                if some(b - 1):
                    pool.wait_ge(ysum_ready, b - 1)
                for t in range(2):
                    last = ch.mark(nc.gpsimd.tensor_tensor(xb2[:, t, :], tile(b - 1, t), b2[:], ALU.add))
                ch.wait(last)

            def residuals(b):
                pool.wait_ge(y1_ready, b)
                nc.gpsimd.tensor_tensor(ysum[:].rearrange("p t e -> p (t e)"), y1[:].rearrange("p t e -> p (t e)"),
                                        xb2[:].rearrange("p t e -> p (t e)"), ALU.add).then_inc(ysum_ready, 1)

            def body(b, p):
                if attends(b):
                    split_v(b, p)
                for j in range(PAIRS):
                    if prepares(b) and j == 2:
                        roots(b, p)
                    if outputs(b) and j == 4:
                        second_root(b)
                    if attends(b):
                        low_part(b, j)
                    if attends(b) and j == 2:
                        normed(b, p)
                    if outputs(b) and j == 3:
                        biased_input(b)
                    if outputs(b) and j == 5:
                        residuals(b)

            pool.sem_inc(lowed, 2)
            for b in (-2, -1, 0):
                body(b, b % 2)
            before = ch.base + ch.n
            with pool.Fori(0, (B - 4) // 2) as it:
                for u in range(2):
                    b = it * 2 + 1 + u
                    per = 5
                    ch.start((b - 1) * per + before)
                    body(b, 1 - u)
                    assert ch.n == per, ch.n
            ch.start((B - 4) * per + before)
            for b in (B - 3, B - 2, B - 1, B):
                body(b, b % 2)


CH = 4


def expert_weights(nc, ctx, s, ins, ident):
    NE, EF, E = s.NE, s.EF, s.E
    NF = EF // P

    def sb(name, shape, dt=F32):
        return ctx.enter_context(nc.sbuf_tensor(name, shape, dt))

    w = {
        "hi": sb("gate_up_hi", [P, NE, 2 * EF], F32R), "lo": sb("gate_up_lo", [P, NE, 2 * EF], F32R),
        "bias": sb("gate_up_bias", [P, NE, 2 * EF], BF16), "ones": sb("bias_rows_on", [P, P], BF16),
        "down": sb("down_w", [P, NE, NF, E]), "downb": sb("down_b", [P, NE, E]),
        "router": sb("router", [P, NE]), "iota": sb("iota", [P, NE]),
        "before": sb("before", [P, P]), "all": sb("all_ones", [P, P]),
        "slots": sb("iota_slots", [P, P], BF16), "ids": sb("token_ids", [P, s.TILES]),
        "tiles": sb("iota_tiles", [P, s.SLOT_TILES], BF16), "bits": sb("expert_bits", [1, 4]), "spare": sb("spare_rows", [P, s.SLOT_TILES]), "tilesf": sb("iota_tiles_f", [P, s.SLOT_TILES]),
    }
    with ExitStack() as c2:
        def sb2(name, shape, dt=F32):
            return c2.enter_context(nc.sbuf_tensor(name, shape, dt))

        def sem2(name):
            return c2.enter_context(nc.semaphore(name))

        rrow = sb2("router_rows", [NE, E])
        raw = sb2("gate_up_raw", [P, NE, 2 * EF])
        braw = sb2("bias_raw", [NE, 2 * EF])
        brest = sb2("bias_rest", [NE, 2 * EF])
        bpart = sb2("bias_part", [NE, 3, 2 * EF], BF16)
        bank = c2.enter_context(nc.psum_tensor("setup_bank", [P, 512], F32))
        small, loaded, full, counted, parts, placed, zeroed = (
            sem2("router_loaded"), sem2("experts_loaded"), sem2("experts_bank_full"), sem2("experts_iotas"),
            sem2("bias_parts_ready"), sem2("bias_placed"), sem2("bias_zeroed"))
        chain, gchain = sem2("experts_vector_steps"), sem2("experts_gpsimd_steps")
        downb = ins["L0_ffn_down_b"]
        with nc.Block() as block:
            @block.sync
            def _(sp):
                sp.dma_start(rrow[:], ins["L0_ffn_router_w"]).then_inc(small, 16)
                sp.dma_start(braw[:, 0:EF], ins["L0_ffn_gate_b"]).then_inc(small, 16)
                sp.dma_start(braw[:, EF:2 * EF], ins["L0_ffn_up_b"]).then_inc(small, 16)
                sp.dma_start(raw[:, :, 0:EF], ins["L0_ffn_gate_w"].rearrange("e d f -> d e f")).then_inc(loaded, 16)
                sp.dma_start(raw[:, :, EF:2 * EF], ins["L0_ffn_up_w"].rearrange("e d f -> d e f")).then_inc(loaded, 16)
                sp.dma_start(w["downb"][:], bass.AP(tensor=downb.tensor, offset=downb.offset,
                                                    ap=[[0, P], [E, NE], [1, E]])).then_inc(loaded, 16)
                sp.dma_start(w["down"][:], ins["L0_ffn_down_w"].rearrange("e (c p) d -> p e c d", p=P)).then_inc(loaded, 16)
                sp.wait_ge(small, 48)
                sp.wait_ge(loaded, 64)
                sp.wait_ge(parts, 1)
                sp.wait_ge(zeroed, 1)
                for j in range(3):
                    sp.dma_start(w["bias"][j:j + 1, :, :], bpart[:, j, :]).then_inc(placed, 16)
                sp.wait_ge(placed, 48)

            @block.gpsimd
            def _(pool):
                ch = Chain(pool, gchain)
                nc.gpsimd.iota(w["iota"][:], pattern=[[1, NE]], base=0, channel_multiplier=0,
                               allow_small_or_imprecise_dtypes=True)
                for half, base in enumerate((-s.N // 2, 1)):
                    nc.gpsimd.iota(w["ids"][:, half * s.TILES // 2:(half + 1) * s.TILES // 2], pattern=[[P, s.TILES // 2]],
                                   base=base, channel_multiplier=1, allow_small_or_imprecise_dtypes=True)
                nc.gpsimd.iota(w["spare"][:], pattern=[[P, s.SLOT_TILES]], base=2 * s.N - s.N // 2, channel_multiplier=1,
                               allow_small_or_imprecise_dtypes=True)
                nc.gpsimd.iota(w["slots"][:], pattern=[[1, P]], base=0, channel_multiplier=0,
                               allow_small_or_imprecise_dtypes=True)
                nc.gpsimd.iota(w["tiles"][:], pattern=[[1, s.SLOT_TILES]], base=0, channel_multiplier=0,
                               allow_small_or_imprecise_dtypes=True)
                nc.gpsimd.iota(w["tilesf"][:], pattern=[[1, s.SLOT_TILES]], base=0, channel_multiplier=0,
                               allow_small_or_imprecise_dtypes=True).then_inc(counted, 1)
                for u in range(4):
                    nc.gpsimd.memset(w["bits"][:, u:u + 1], float(NE ** u))
                ch.step(nc.gpsimd.memset(w["all"][:], 1.0))
                ch.step(nc.gpsimd.affine_select(out=w["before"][:], in_=w["all"][:], compare_op=ALU.is_gt, fill=0.0,
                                                base=0, pattern=[[1, P]], channel_multiplier=-1))
                ch.step(nc.gpsimd.affine_select(out=w["ones"][:], in_=w["all"][:], compare_op=ALU.is_gt, fill=0.0,
                                                base=3, pattern=[[0, P]], channel_multiplier=-1))

            @block.tensor
            def _(pe):
                pe.wait_ge(small, 48)
                nc.tensor.transpose(bank[:, 0:NE], rrow[:], ident[0:NE, 0:NE]).then_inc(full, 1)

            @block.vector
            def _(dve):
                ch = Chain(dve, chain)
                nc.vector.memset(w["bias"][:].rearrange("p e f -> p (e f)").bitcast(F32), 0.0).then_inc(zeroed, 1)
                dve.wait_ge(small, 48)
                ch.step(nc.vector.tensor_copy(bpart[:, 0, :], braw[:]))
                ch.step(nc.vector.tensor_tensor(brest[:], braw[:], bpart[:, 0, :], ALU.subtract))
                ch.step(nc.vector.tensor_copy(bpart[:, 1, :], brest[:]))
                nc.vector.tensor_tensor(bpart[:, 2, :], brest[:], bpart[:, 1, :], ALU.subtract).then_inc(parts, 1)
                dve.wait_ge(full, 1)
                nc.vector.tensor_copy(w["router"][:], bank[:, 0:NE])
                dve.wait_ge(loaded, 64)
                for e in range(NE):
                    ch.step(nc.vector.tensor_copy(w["hi"][:, e, :], raw[:, e, :]))
                    last = ch.mark(nc.vector.tensor_tensor(w["lo"][:, e, :], raw[:, e, :], w["hi"][:, e, :].bitcast(F32),
                                                           ALU.subtract))
                ch.wait(last)
    return w


def mixture(nc, kept, s, tag, xres, ident, w, normed_dram, slot_dram, choice_dram):
    share = kept.enter_context(nc.sbuf_tensor(tag + "share", [P, 2, s.TILES], F32))
    slot = kept.enter_context(nc.sbuf_tensor(tag + "slot", [P, 2, s.TILES], I32))
    with ExitStack() as ctx:
        def sb(name, shape, dt=F32):
            return ctx.enter_context(nc.sbuf_tensor(tag + name, shape, dt))

        token = sb("token", [P, s.SLOT_TILES], I32)
        expert = sb("expert", [1, s.SLOT_TILES // 4], I32)
        choice_row = sb("choice_row", [P, s.SLOT_TILES], I32) if choice_dram is not None else None
        route(nc, s, tag, xres, ident, w, share, slot, token, choice_row, expert, normed_dram)
        run_experts(nc, s, tag, ident, w, token, choice_row, expert, normed_dram, slot_dram, choice_dram)
    return share, slot


def run_experts(nc, s, tag, ident, w, token, choice_row, expert, normed_dram, slot_dram, choice_dram):
    NE, EF, E, ST = s.NE, s.EF, s.E, s.SLOT_TILES
    NF = EF // P
    U = s.BODY
    G = 4
    assert ST % U == 0 and NE == 8
    with phase(nc) as (ctx, new_sem):
        def sb(name, shape, dt=F32):
            return ctx.enter_context(nc.sbuf_tensor(tag + name, shape, dt))

        def sem(name):
            return new_sem(tag + name)

        def pb(name):
            return [ctx.enter_context(nc.psum_tensor(f"{tag}{name}{i}", [P, 512], F32)) for i in range(2)]

        index = sb("index", [P, 2, G], I32)
        xg = sb("xg", [P, G, E])
        xhi, xlo = sb("xhi", [P, 2, P], F32R), sb("xlo", [P, 2, P], F32R)
        act_ = sb("silu", [P, 2, EF])
        hid = sb("hid", [P, 4, EF])
        hT = sb("hT", [P, 2, NF, P])
        yo = sb("yo", [P, 4, E])
        out_index = sb("out_index", [P, 2, G], I32)
        bx, bgu, bh, by = pb("bx"), pb("bgu"), pb("bh"), pb("by")
        arrived = [sem(f"rows_arrived{i}") for i in range(G)]
        stored = [sem(f"rows_stored{i}") for i in range(4)]
        xT_full, hi_done, lo_done, gu_full, silu_done, hid_done, hT_full, hT_done, y_full, y_done = (
            sem("xT_full"), sem("hi_done"), sem("lo_done"), sem("gu_full"), sem("silu_done"), sem("hid_done"),
            sem("hT_full"), sem("hT_done"), sem("y_full"), sem("y_done"))
        picked, turns, placed = sem("index_picked"), sem("gather_turns"), sem("places_picked")

        def experts_from(engine, word):
            packed = engine.value_load(expert[0:1, bass.ds(word, 1)], min_val=0, max_val=NE ** U - 1)
            return lambda k: (packed >> (3 * k)) & (NE - 1)

        with nc.Block() as block:
            @block.gpsimd
            def _(pool):
                def gather(i, u, it=0):
                    if u % G == 0:
                        if not isinstance(i, int):
                            pool.wait_ge(xT_full, i - G)
                        nc.gpsimd.tensor_copy(index[:, (u // G) % 2, :], token[:, bass.ds(i, G)]).then_inc(picked, 1)
                        if isinstance(i, int):
                            pool.wait_ge(picked, i // G + 1)
                        else:
                            pool.wait_ge(picked, it * (U // G) + u // G + 1)
                    if not isinstance(i, int) or i >= G:
                        pool.wait_ge(xT_full, i - G + 1)
                    pool.sem_inc(turns, 1)
                    pool.indirect_dma_start(
                        xg[:, u % G, :], None, normed_dram,
                        bass.IndirectOffsetOnAxis(ap=index[:, (u // G) % 2, u % G:u % G + 1], axis=0),
                    ).then_inc(arrived[u % G], 16)

                def scatter(i, u, it):
                    if u % G == 0:
                        if not isinstance(i, int) or i >= 2 * G:
                            pool.wait_ge(y_done, i)
                            pool.sem_inc(turns, 1)
                        nc.gpsimd.tensor_copy(out_index[:, (u // G) % 2, :], choice_row[:, bass.ds(i, G)]).then_inc(placed, 1)
                        pool.wait_ge(placed, it * (U // G) + u // G + 1)
                    pool.wait_ge(y_done, i + 1)
                    pool.sem_inc(turns, 1)
                    pool.indirect_dma_start(
                        choice_dram, bass.IndirectOffsetOnAxis(ap=out_index[:, (u // G) % 2, u % G:u % G + 1], axis=0),
                        yo[:, u % 4, :], None,
                    ).then_inc(stored[u % 4], 16)

                for u in range(U):
                    gather(u, u)
                with pool.Fori(1, ST // U) as it:
                    for u in range(U):
                        gather(it * U + u, u, it)
                        if choice_dram is not None:
                            scatter(it * U - U + u, u, it - 1)
                if choice_dram is not None:
                    for u in range(U):
                        scatter(ST - U + u, u, ST // U - 1)
                    for q in range(4):
                        pool.wait_ge(stored[q], 16 * ST // 4)

            @block.tensor
            def _(pe):
                def transpose_x(i, u, n):
                    pe.wait_ge(arrived[u % G], n)
                    if not isinstance(i, int) or i >= 2:
                        pe.wait_ge(lo_done, i - 1)
                    nc.tensor.transpose(bx[u % 2][:, 0:P], xg[:, u % G, :], ident[:]).then_inc(xT_full, 1)

                def gate_up(i, u, e):
                    if not isinstance(i, int) or i >= 2:
                        pe.wait_ge(hid_done, i - 1)
                    wh = w["hi"][:, bass.ds(e, 1), :].rearrange("p a f -> p (a f)")
                    wl = w["lo"][:, bass.ds(e, 1), :].rearrange("p a f -> p (a f)")
                    bias = w["bias"][:, bass.ds(e, 1), :].rearrange("p a f -> p (a f)")
                    dst = bgu[u % 2][:]
                    nc.tensor.matmul(dst, w["ones"][:], bias, start=True, stop=False)
                    pe.wait_ge(lo_done, i + 1)
                    nc.tensor.matmul(dst, xhi[:, u % 2, :], wh, start=False, stop=False)
                    nc.tensor.matmul(dst, xhi[:, u % 2, :], wl, start=False, stop=False)
                    nc.tensor.matmul(dst, xlo[:, u % 2, :], wh, start=False, stop=True).then_inc(gu_full, 1)

                def transpose_h(i, u):
                    pe.wait_ge(hid_done, i + 1)
                    if not isinstance(i, int) or i >= 2:
                        pe.wait_ge(hT_done, i - 1)
                    for f in range(NF):
                        last = nc.tensor.transpose(bh[u % 2][:, f * P:(f + 1) * P], hid[:, u % 4, f * P:(f + 1) * P], ident[:])
                    last.then_inc(hT_full, 1)

                def down(i, u, e):
                    pe.wait_ge(hT_done, i + 1)
                    if not isinstance(i, int) or i >= 2:
                        pe.wait_ge(y_done, i - 1)
                    for f in range(NF):
                        last = nc.tensor.matmul(by[u % 2][:, 0:E], hT[:, u % 2, f, :],
                                                w["down"][:, bass.ds(e, 1), f, :].rearrange("p a d -> p (a d)"),
                                                start=(f == 0), stop=(f == NF - 1))
                    last.then_inc(y_full, 1)

                def steps(i, u, n, e, first):
                    early = i if isinstance(i, int) else ST
                    if early >= 3:
                        transpose_h(i - 3, (u - 3) % U)
                    if n is not None:
                        transpose_x(i, u, n)
                    if early >= 4:
                        down(i - 4, (u - 4) % U, e(u - 4 + first))
                    if early >= 1:
                        gate_up(i - 1, (u - 1) % U, e(u - 1 + first))

                now = experts_from(pe, 0)
                for u in range(U):
                    steps(u, u, 16 * (u // G + 1), now, 0)
                with pe.Fori(1, ST // U) as it:
                    for u in range(U):
                        if u % 4 == 0:
                            now = experts_from(pe, it * 2 + u // 4 - 1)
                        steps(it * U + u, u, it * (16 * U // G) + 16 * (u // G + 1), now, 4 - u // 4 * 4)
                now = experts_from(pe, ST // 4 - 1)
                steps(ST, 0, None, now, 4)
                for i in range(ST - 2, ST):
                    transpose_h(i, i % U)
                    down(i - 1, (i - 1) % U, now(i - 1 - ST + 4))
                down(ST - 1, U - 1, now(3))

            @block.scalar
            def _(act):
                def high(i, u):
                    act.wait_ge(xT_full, i + 1)
                    if not isinstance(i, int) or i >= 2:
                        act.wait_ge(gu_full, i - 1)
                    nc.scalar.copy(xhi[:, u % 2, :], bx[u % 2][:, 0:P]).then_inc(hi_done, 1)

                def silu(i, u):
                    act.wait_ge(gu_full, i + 1)
                    if not isinstance(i, int) or i >= 2:
                        act.wait_ge(hid_done, i - 1)
                    nc.scalar.activation(act_[:, u % 2, :], bgu[u % 2][:, 0:EF], ACT.Silu).then_inc(silu_done, 1)

                def take_h(i, u):
                    act.wait_ge(hT_full, i + 1)
                    if not isinstance(i, int) or i >= 2:
                        act.wait_ge(y_full, i - 1)
                    nc.scalar.copy(hT[:, u % 2, :, :], bh[u % 2][:, 0:EF].rearrange("p (f q) -> p f q", f=NF)).then_inc(hT_done, 1)

                def steps(i, u):
                    if not isinstance(i, int) or i >= 3:
                        take_h(i - 3, (u - 3) % U)
                    high(i, u)
                    if not isinstance(i, int) or i >= 1:
                        silu(i - 1, (u - 1) % U)

                for u in range(U):
                    steps(u, u)
                with act.Fori(1, ST // U) as it:
                    for u in range(U):
                        steps(it * U + u, u)
                take_h(ST - 3, U - 3)
                silu(ST - 1, U - 1)
                take_h(ST - 2, U - 2)
                take_h(ST - 1, U - 1)

            @block.vector
            def _(dve):
                def low(i, u):
                    dve.wait_ge(hi_done, i + 1)
                    if not isinstance(i, int) or i >= 2:
                        dve.wait_ge(gu_full, i - 1)
                    nc.vector.tensor_tensor(xlo[:, u % 2, :], bx[u % 2][:, 0:P], xhi[:, u % 2, :].bitcast(F32),
                                            ALU.subtract).then_inc(lo_done, 1)

                def hidden(i, u):
                    dve.wait_ge(silu_done, i + 1)
                    if not isinstance(i, int) or i >= 4:
                        dve.wait_ge(hT_full, i - 3)
                    nc.vector.tensor_tensor(hid[:, u % 4, :], bgu[u % 2][:, EF:2 * EF], act_[:, u % 2, :], ALU.mult).then_inc(hid_done, 1)

                def take_y(i, u, n, e):
                    dve.wait_ge(y_full, i + 1)
                    if n is not None:
                        dve.wait_ge(stored[u % 4], n)
                    nc.vector.tensor_tensor(yo[:, u % 4, :], by[u % 2][:, 0:E],
                                            w["downb"][:, bass.ds(e, 1), :].rearrange("p a d -> p (a d)"), ALU.add).then_inc(y_done, 1)

                def steps(i, u, it, e, first):
                    low(i, u)
                    if not isinstance(i, int) or i >= 4:
                        k = (i - 4) if isinstance(i, int) else u - 4
                        n = 16 * (k // 4)
                        take_y(i - 4, (u - 4) % U, (n or None) if isinstance(i, int) else it * (16 * U // 4) + n, e(u - 4 + first))
                    if not isinstance(i, int) or i >= 1:
                        hidden(i - 1, (u - 1) % U)

                now = experts_from(dve, 0)
                for u in range(U):
                    steps(u, u, None, now, 0)
                with dve.Fori(1, ST // U) as it:
                    now = experts_from(dve, it * 2 - 1)
                    for u in range(U):
                        steps(it * U + u, u, it, now, 4)
                now = experts_from(dve, ST // 4 - 1)
                for i in range(ST - 4, ST):
                    take_y(i, i % U, 16 * (i // 4), now(i - ST + 4))
                    if i == ST - 4:
                        hidden(ST - 1, U - 1)

            @block.sync
            def _(sp):
                def store(i, u):
                    sp.wait_ge(y_done, i + 1)
                    sp.dma_start(slot_dram[bass.ds(i * P, P), :], yo[:, u % 4, :]).then_inc(stored[u % 4], 16)

                if slot_dram is not None:
                    with sp.Fori(0, ST // U) as it:
                        for u in range(U):
                            store(it * U + u, u)
                for i in range(4):
                    sp.wait_ge(stored[i], 16 * ST // 4)


def combine(nc, s, xres, share, choice_dram, out):
    E, TILES, N = s.E, s.TILES, s.N
    C, U = 4, 4
    CHUNKS = TILES // C
    with phase(nc) as (ctx, sem):
        rows = ctx.enter_context(nc.sbuf_tensor("c_rows", [P, U, 2, C, E], F32))
        loaded = [sem(f"c_loaded{i}") for i in range(U)]
        half, added, sent = sem("c_half"), sem("c_added"), sem("c_sent")
        out_tiles = out.rearrange("b (t p) e -> p (b t) e", p=P)

        def rows_of(k, c):
            return choice_dram[k * N:(k + 1) * N, :].rearrange("(t p) e -> p t e", p=P)[:, bass.ds(c * C, C), :]

        with nc.Block() as block:
            @block.sync
            def _(sp):
                def load(c, q):
                    for k in range(2):
                        sp.dma_start(rows[:, q, k, :, :], rows_of(k, c)).then_inc(loaded[q], 16)

                for q in range(U):
                    load(q, q)
                with sp.Fori(1, CHUNKS // U) as it:
                    for q in range(U):
                        sp.wait_ge(added, it * U + q - U + 1)
                        load(it * U + q, q)

            @block.vector
            def _(dve):
                with dve.Fori(0, CHUNKS // U) as it:
                    for q in range(U):
                        c = it * U + q
                        dve.wait_ge(loaded[q], it * 32 + 32)
                        for k in range(2):
                            if k == 1:
                                dve.wait_ge(half, c + 1)
                            for t in range(C):
                                x = xres[:, bass.ds(c * C + t, 1), :].rearrange("p a e -> p (a e)")
                                last = nc.vector.scalar_tensor_tensor(x, rows[:, q, k, t, :], share[:, k, bass.ds(c * C + t, 1)], x,
                                                                      ALU.mult, ALU.add)
                            last.then_inc((half, added)[k], 1)

            @block.scalar
            def _(act):
                with act.Fori(0, CHUNKS) as c:
                    act.wait_ge(added, c + 1)
                    act.dma_start(out_tiles[:, bass.ds(c * C, C), :], xres[:, bass.ds(c * C, C), :]).then_inc(sent, 16)
                act.wait_ge(sent, 16 * CHUNKS)


def route(nc, s, tag, xres, ident, w, share, slot, token, choice_row, expert, normed_dram):
    NE, E, TILES, ST = s.NE, s.E, s.TILES, s.SLOT_TILES
    CHUNKS = TILES // CH
    with phase(nc) as (ctx, new_sem):
        def sb(name, shape, dt=F32):
            return ctx.enter_context(nc.sbuf_tensor(tag + name, shape, dt))

        def sem(name):
            return new_sem(tag + name)

        def pb(name, n=1):
            return [ctx.enter_context(nc.psum_tensor(f"{tag}{name}{i}", [P, 512], F32)) for i in range(n)]

        stats = sb("r_stats", [P, 2, CH, 6])
        mv = sb("r_mv", [P, 2, 4, CH])
        arg = sb("r_arg", [P, 2, CH])
        minus_mean, shift = sb("r_minus_mean", [P, 2, CH]), sb("r_shift", [P, 2, CH])
        rs = sb("r_rs", [P, 2, CH])
        half = sb("r_half", [P, CH])
        xl = sb("r_xl", [P, 2, CH, E])
        xT = sb("r_xT", [P, 2, CH * P])
        logits = sb("logits", [P, TILES, NE])
        prob = sb("prob", [P, TILES, NE])
        tmp = sb("r_tmp", [P, TILES, NE])
        tmp2 = sb("r_tmp2", [P, TILES, NE])
        hot = [sb(f"hot{k}", [P, TILES, NE]) for k in range(2)]
        top = [sb(f"top{k}", [P, TILES]) for k in range(2)]
        first = sb("first", [P, TILES])
        den = sb("den", [P, TILES])
        member = sb("member", [P, NE, TILES])
        seen = sb("seen", [P, NE, TILES])
        unit = sb("r_unit", [P, NE * TILES])
        count = sb("count", [P, NE])
        place = sb("place", [P, NE])
        ends = sb("ends", [P, NE])
        tiles_i = sb("tiles_i", [P, NE], I32)
        tiles_f = sb("tiles_f", [P, NE])
        slot_f = sb("slot_f", [P, 2, TILES])
        part_i = sb("part_i", [P, 2, 2, TILES], I32)
        part_f = sb("part_f", [P, 2, 2, TILES])
        minus_row = sb("minus_row", [P, 2, TILES])
        away = sb("away", [P, 4, P])
        ge = sb("ge", [1, ST, NE])
        ex_f = sb("ex_f", [1, ST])
        held, sums, above, spare, second = (sb(n, [P, ST]) for n in ("held", "sums", "above", "spare", "second"))
        tokf = sb("token_f", [P, ST])
        ex_w, ex_h = sb("ex_w", [1, ST // 4]), sb("ex_h", [1, ST // 4])
        in_tile = sb("in_tile", [P, 8, P], F32R)
        in_row = sb("in_row", [P, 8, 2 * P], F32R)
        bx, (bl,) = pb("r_bx", 2), pb("r_logits")
        bc, = pb("r_bc")
        bt = pb("r_bt", 2)
        ready, rooted, normed, x_full, x_taken, l_full, half_set = (
            sem("r_arg_ready"), sem("r_rooted"), sem("r_normed"), sem("r_xT_full"), sem("r_xT_taken"),
            sem("r_logits_full"), sem("r_half_set"))
        shifted, exped, chain = sem("r_shifted"), sem("r_exped"), sem("r_vector_steps")
        row_out = [sem(f"r_rows_out{i}") for i in range(2)]
        counted, summed, hot_ready, hot_used, table_full = (sem("r_counted"), sem("r_summed"), sem("r_hot_ready"),
                                                            sem("r_hot_used"), sem("r_table_full"))
        powered = sem("r_powered")
        rows_known, squared, tile_ready = sem("r_rows_known"), sem("r_squared"), sem("r_tile_ready")
        assert 2 * P >= ST and TILES * NE <= 512

        with nc.Block() as block:
            @block.vector
            def _(dve):
                ch = Chain(dve, chain)
                nc.vector.memset(half[:], -0.5).then_inc(half_set, 1)
                PER = CH + 6

                def head(c, q):
                    for t in range(CH):
                        last = ch.mark(nc.vector.bn_stats(stats[:, q, t, :], xres[:, bass.ds(c * CH + t, 1), :].rearrange("p a e -> p (a e)")))
                    ch.wait(last)
                    moments(nc, ch, stats[:, q], mv[:, q])
                    if not isinstance(c, int) or c >= 2:
                        dve.wait_ge(rooted, c - 1)
                    nc.vector.tensor_scalar(minus_mean[:, q, :], mv[:, q, 0, :], -1.0, None, ALU.mult)
                    nc.vector.tensor_scalar(arg[:, q, :], mv[:, q, 3, :], 0.25, EPS, ALU.mult, ALU.add).then_inc(ready, 1)

                head(0, 0)
                head(1, 1)
                with dve.Fori(1, CHUNKS // 2) as it:
                    ch.start(it * (2 * PER))
                    head(it * 2, 0)
                    head(it * 2 + 1, 1)
                ch.start(CHUNKS * PER)
                dve.wait_ge(l_full, CHUNKS)

                V = nc.vector

                def over(x):
                    return x.rearrange("p (t a) -> p t a", a=1).broadcast_to([P, TILES, NE])

                iota = w["iota"][:].rearrange("p (a e) -> p a e", a=1).broadcast_to([P, TILES, NE])
                raw = bl[:].rearrange("p (t e) -> p t e", e=NE)
                ch.step(V.reduce_max(den[:], raw, AXX))
                V.tensor_tensor(logits[:], raw, over(den[:]), ALU.subtract).then_inc(shifted, 1)
                dve.wait_ge(exped, 1)
                ch.step(V.reduce_sum(den[:], prob[:], AXX))
                ch.step(V.reciprocal(den[:], den[:]))
                ch.step(V.tensor_tensor(prob[:], prob[:], over(den[:]), ALU.mult))
                left = prob
                for k in range(2):
                    ch.step(V.reduce_max(top[k][:], left[:], AXX))
                    ch.step(V.tensor_tensor(tmp[:], left[:], over(top[k][:]), ALU.is_equal))
                    ch.step(V.scalar_tensor_tensor(tmp[:], tmp[:], -float(NE), iota, ALU.mult, ALU.add))
                    ch.step(V.tensor_reduce(first[:], tmp[:], AXX, ALU.min))
                    ch.step(V.tensor_scalar(first[:], first[:], float(NE), None, ALU.add))
                    ch.step(V.tensor_tensor(hot[k][:], over(first[:]), iota, ALU.is_equal))
                    if k == 0:
                        ch.step(V.scalar_tensor_tensor(tmp2[:], hot[0][:], -2.0, left[:], ALU.mult, ALU.add))
                        left = tmp2
                ch.step(V.scalar_tensor_tensor(den[:], top[0][:], 1e-9, top[1][:], ALU.add, ALU.add))
                ch.step(V.reciprocal(den[:], den[:]))
                for k in range(2):
                    ch.step(V.tensor_tensor(share[:, k, :], top[k][:], den[:], ALU.mult))

                ch.step(V.memset(unit[:], 1.0))
                ch.step(V.tensor_tensor(member[:].rearrange("p e t -> p t e"), hot[0][:], hot[1][:], ALU.add))
                ch.step(V.tensor_tensor_scan(seen[:].rearrange("p e t -> p (e t)"), unit[:],
                                             member[:].rearrange("p e t -> p (e t)"), 0.0, ALU.mult, ALU.add))
                ch.step(V.memset(ends[:], 0.0))
                ch.step(V.tensor_copy(ends[:, 1:NE], seen[:, 0:NE - 1, TILES - 1]))
                V.tensor_tensor(count[:], seen[:, :, TILES - 1], ends[:], ALU.subtract).then_inc(counted, 1)
                dve.wait_ge(summed, 1)
                ch.step(V.tensor_scalar(tiles_i[:], bc[:, NE:2 * NE], float(P - 1), None, ALU.add))
                ch.step(V.tensor_scalar(tiles_i[:], tiles_i[:], 7, None, ALU.arith_shift_right))
                ch.step(V.tensor_copy(tiles_f[:], tiles_i[:]))
                ch.step(V.tensor_tensor_scan(place[:], unit[:, 0:NE], tiles_f[:], 0.0, ALU.mult, ALU.add))
                ch.step(V.tensor_tensor(ge[:], w["tilesf"][0:1, :].rearrange("p (t a) -> p t a", a=1).broadcast_to([1, ST, NE]),
                                        place[0:1, :].rearrange("p (a e) -> p a e", a=1).broadcast_to([1, ST, NE]), ALU.is_ge))
                ch.step(V.reduce_sum(ex_f[:], ge[:], AXX))
                ch.step(V.tensor_scalar(ex_f[:], ex_f[:], float(NE - 1), None, ALU.min))
                fours = ex_f[:].rearrange("p (b u) -> p b u", u=4)
                ch.step(V.tensor_tensor(fours, fours, w["bits"][0:1, :].rearrange("p (a u) -> p a u", a=1).broadcast_to([1, ST // 4, 4]),
                                        ALU.mult))
                ch.step(V.reduce_sum(ex_w[:], fours, AXX))
                ch.step(V.tensor_copy(ex_h[:], ex_w[:]))
                ch.step(V.scalar_tensor_tensor(ex_w[:, 0:ST // 4 - 1], ex_h[:, 1:ST // 4], float(NE ** 4), ex_h[:, 0:ST // 4 - 1],
                                               ALU.mult, ALU.add))
                ch.step(V.tensor_copy(expert[:], ex_w[:]))
                ch.step(V.tensor_tensor(place[:], place[:], tiles_f[:], ALU.subtract))
                ch.step(V.scalar_tensor_tensor(place[:], place[:], float(P), ends[:], ALU.mult, ALU.subtract))
                ch.step(V.tensor_tensor(place[:], place[:], bc[:, 0:NE], ALU.add))
                ch.step(V.tensor_tensor(seen[:], seen[:], member[:], ALU.subtract))
                ch.step(V.tensor_tensor(seen[:], seen[:], place[:].rearrange("p (e a) -> p e a", a=1).broadcast_to([P, NE, TILES]),
                                        ALU.add))
                for k in range(2):
                    ch.step(V.tensor_tensor(tmp[:], seen[:].rearrange("p e t -> p t e"), hot[k][:], ALU.mult))
                    ch.step(V.reduce_sum(slot_f[:, k, :], tmp[:], AXX))
                ch.step(V.tensor_copy(slot[:], slot_f[:]))
                ch.step(V.tensor_scalar(part_i[:, 0], slot[:], 7, None, ALU.arith_shift_right))
                ch.step(V.tensor_scalar(part_i[:, 1], slot[:], P - 1, None, ALU.bitwise_and))
                ch.step(V.tensor_copy(part_f[:].rearrange("p a k t -> p (a k t)"), part_i[:].rearrange("p a k t -> p (a k t)")))
                V.tensor_scalar(minus_row[:], part_f[:, 1], -1.0, None, ALU.mult).then_inc(rows_known, 1)
                for q in range(8):
                    last = ch.mark(V.memset(in_row[:, q, ST:2 * P].bitcast(F32), 0.0))
                ch.wait(last)
                dve.sem_inc(hot_used, 2)
                with dve.Fori(0, TILES // 4) as it:
                    for u in range(4):
                        for k in range(2):
                            n = 2 * u + k
                            if n % 4 == 0:
                                dve.wait_ge(hot_used, it * 2 + n // 4 + 1)
                            if k == 0:
                                V.tensor_scalar(in_tile[:, n, :], w["slots"][:], part_f[:, 1, k, bass.ds(it * 4 + u, 1)],
                                                None, ALU.is_equal)
                            last = V.tensor_scalar(in_row[:, n, 0:ST], w["tiles"][:], part_f[:, 0, k, bass.ds(it * 4 + u, 1)],
                                                   w["ids"][:, bass.ds(it * 4 + u, 1)], ALU.is_equal, ALU.mult)
                        if u % 2 == 1:
                            last.then_inc(hot_ready, 1)
                dve.wait_ge(table_full, 1)
                ch.step(V.tensor_copy(held[:], bt[0][:, 0:ST]))
                ch.step(V.tensor_tensor(sums[:], held[:], bt[1][:, 0:ST], ALU.add))
                ch.step(V.tensor_scalar(above[:], sums[:], 0.0, None, ALU.is_gt))
                ch.step(V.scalar_tensor_tensor(tokf[:], sums[:], float(s.N // 2), above[:], ALU.add, ALU.subtract))
                ch.step(V.tensor_copy(token[:], tokf[:]))
                if choice_row is not None:
                    ch.step(V.tensor_scalar(second[:], bt[1][:, 0:ST], 0.0, float(s.N), ALU.not_equal, ALU.mult))
                    ch.step(V.scalar_tensor_tensor(spare[:], sums[:], 0.0, w["spare"][:], ALU.is_equal, ALU.mult))
                    ch.step(V.tensor_tensor(tokf[:], tokf[:], second[:], ALU.add))
                    ch.step(V.tensor_tensor(choice_row[:], tokf[:], spare[:], ALU.add))

            @block.gpsimd
            def _(pool):
                pool.wait_ge(half_set, 1)

                def root(c, q):
                    pool.wait_ge(ready, c + 1)
                    if not isinstance(c, int):
                        pool.wait_ge(normed, c - 1)
                    nc.gpsimd.tensor_tensor(rs[:, q, :], arg[:, q, :], half[:], ALU.pow).then_inc(powered, 1)
                    pool.wait_ge(powered, c + 1)
                    nc.gpsimd.tensor_tensor(shift[:, q, :], minus_mean[:, q, :], rs[:, q, :], ALU.mult).then_inc(rooted, 1)

                root(0, 0)
                root(1, 1)
                with pool.Fori(1, CHUNKS // 2) as it:
                    root(it * 2, 0)
                    root(it * 2 + 1, 1)

            @block.sync
            def _(sp):
                def store(c, q):
                    sp.wait_ge(normed, c + 1)
                    sp.dma_start(normed_dram.rearrange("(t p) e -> p t e", p=P)[:, bass.ds(c * CH, CH), :], xl[:, q, :, :]
                                 ).then_inc(row_out[q], 16)

                with sp.Fori(0, CHUNKS // 2) as it:
                    store(it * 2, 0)
                    store(it * 2 + 1, 1)
                for q in range(2):
                    sp.wait_ge(row_out[q], 8 * CHUNKS)

            @block.tensor
            def _(pe):
                def transposes(c, q):
                    pe.wait_ge(normed, c + 1)
                    if not isinstance(c, int) or c >= 2:
                        pe.wait_ge(x_taken, c - 1)
                    for t in range(CH):
                        last = nc.tensor.transpose(bx[q][:, t * P:(t + 1) * P], xl[:, q, t, :], ident[:])
                    last.then_inc(x_full, 1)

                def router(c, q):
                    pe.wait_ge(x_taken, c + 1)
                    for t in range(CH):
                        last = nc.tensor.matmul(bl[:, bass.ds(c * (CH * NE) + t * NE, NE)], xT[:, q, t * P:(t + 1) * P],
                                                w["router"][:], start=True, stop=True)
                    last.then_inc(l_full, 1)

                transposes(0, 0)
                transposes(1, 1)
                router(0, 0)
                transposes(2, 0)
                router(1, 1)
                transposes(3, 1)
                with pe.Fori(2, CHUNKS // 2) as it:
                    router(it * 2 - 2, 0)
                    transposes(it * 2, 0)
                    router(it * 2 - 1, 1)
                    transposes(it * 2 + 1, 1)
                router(CHUNKS - 2, 0)
                router(CHUNKS - 1, 1)
                pe.wait_ge(counted, 1)
                nc.tensor.matmul(bc[:, 0:NE], w["before"][:], count[:], start=True, stop=True)
                nc.tensor.matmul(bc[:, NE:2 * NE], w["all"][:], count[:], start=True, stop=True).then_inc(summed, 1)

                def place_four(n, first, final):
                    for q in range(4):
                        last = nc.tensor.matmul(bt[q % 2][:, 0:2 * P], in_tile[:, 4 * n + q, :], in_row[:, 4 * n + q, :],
                                                start=(first and q < 2), stop=(final and q >= 2), skip_group_check=True)
                    return last

                pe.wait_ge(hot_ready, 1)
                pe.wait_ge(tile_ready, 1)
                place_four(0, True, False).then_inc(hot_used, 1)
                pe.wait_ge(hot_ready, 2)
                pe.wait_ge(tile_ready, 2)
                place_four(1, False, False).then_inc(hot_used, 1)
                with pe.Fori(1, TILES // 4 - 1) as it:
                    for n in range(2):
                        pe.wait_ge(hot_ready, it * 2 + n + 1)
                        pe.wait_ge(tile_ready, it * 2 + n + 1)
                        place_four(n, False, False).then_inc(hot_used, 1)
                pe.wait_ge(hot_ready, TILES // 2 - 1)
                pe.wait_ge(tile_ready, TILES // 2 - 1)
                place_four(0, False, False).then_inc(hot_used, 1)
                pe.wait_ge(hot_ready, TILES // 2)
                pe.wait_ge(tile_ready, TILES // 2)
                place_four(1, False, True).then_inc(table_full, 1)

            @block.scalar
            def _(act):
                def apply(c, q, n):
                    act.wait_ge(rooted, c + 1)
                    if n is not None:
                        act.wait_ge(row_out[q], n)
                    for t in range(CH):
                        last = nc.scalar.activation(xl[:, q, t, :], xres[:, bass.ds(c * CH + t, 1), :].rearrange("p a e -> p (a e)"),
                                                    ACT.Identity, bias=shift[:, q, t:t + 1], scale=rs[:, q, t:t + 1])
                    last.then_inc(normed, 1)

                def take(c, q):
                    act.wait_ge(x_full, c + 1)
                    if not isinstance(c, int) or c >= 2:
                        act.wait_ge(l_full, c - 1)
                    nc.scalar.copy(xT[:, q, :], bx[q][:]).then_inc(x_taken, 1)

                apply(0, 0, None)
                apply(1, 1, None)
                take(0, 0)
                with act.Fori(1, CHUNKS // 2) as it:
                    apply(it * 2, 0, it * 16)
                    take(it * 2 - 1, 1)
                    apply(it * 2 + 1, 1, it * 16)
                    take(it * 2, 0)
                take(CHUNKS - 1, 1)
                act.wait_ge(shifted, 1)
                nc.scalar.activation(prob[:], logits[:], ACT.Exp).then_inc(exped, 1)
                act.wait_ge(rows_known, 1)
                with act.Fori(0, TILES // 4) as it:
                    for u in range(4):
                        if u % 2 == 0:
                            act.wait_ge(hot_used, it * 2 + u // 2 + 1)
                        last = nc.scalar.activation(away[:, u, :], w["slots"][:], ACT.Square,
                                                    bias=minus_row[:, 1, bass.ds(it * 4 + u, 1)])
                        if u % 2 == 1:
                            last.then_inc(squared, 1)
                            act.wait_ge(squared, it * 2 + u // 2 + 1)
                            nc.scalar.activation(in_tile[:].rearrange("p (u k) r -> p u k r", k=2)[:, u - 1:u + 1, 1, :],
                                                 away[:, u - 1:u + 1, :], ACT.Relu,
                                                 bias=w["all"][:, 0:1], scale=-4.0).then_inc(tile_ready, 1)


def recurrence(nc, s, ins, xres, ident, share, slot, slot_dram):
    E, B, S = s.E, s.B, s.S
    with phase(nc) as (ctx, sem):
        def sb(name, shape, dt=F32):
            return ctx.enter_context(nc.sbuf_tensor(name, shape, dt))

        index = sb("z_index", [P, 2, 2, 2], I32)
        rows = sb("z_rows", [P, 2, 2, 2, E])
        arrived = [sem(f"z_arrived{i}") for i in range(8)]
        picked, turns, first_added, added, combined = (sem("z_picked"), sem("z_turns"), sem("z_first_added"),
                                                       sem("z_added"), sem("z_combined"))
        wz, wh = sb("wz", [P, E]), sb("wh", [P, E])
        cols = sb("z_cols", [P, 3])
        gamma, beta = sb("gamma", [P, 2, E]), sb("beta", [P, 2, E])
        half = sb("z_half", [P, 4])
        stats, mv = sb("z_stats", [P, 2, 4, 6]), sb("z_mv", [P, 2, 4, 4])
        arg, rs = sb("z_arg", [P, 2, 4]), sb("z_rs", [P, 2, 4])
        xl = sb("z_xl", [P, 2, 2, E])
        xT = sb("z_xT", [P, 2, 2 * P])
        keep, z, sg = sb("z_keep", [P, 2, S]), sb("z_gate", [P, 2, S]), sb("z_sig", [P, 2, S])
        relu, val, hs = sb("z_relu", [P, S]), sb("z_val", [P, S]), sb("z_h", [P, 2, S])
        nh = sb("z_nh", [P, 2, E])
        bx = [ctx.enter_context(nc.psum_tensor(f"zx{i}", [P, 512], F32)) for i in range(2)]
        bk = [ctx.enter_context(nc.psum_tensor(f"zk{i}", [P, 512], F32)) for i in range(2)]
        bh = [ctx.enter_context(nc.psum_tensor(f"zh{i}", [P, 512], F32)) for i in range(2)]
        loaded, setup = sem("z_loaded"), sem("z_setup")
        ready, rooted, normed, x_full, x_taken, k_full = (sem("z_arg_ready"), sem("z_rooted"), sem("z_normed"),
                                                          sem("z_xT_full"), sem("z_xT_taken"), sem("z_k_full"))
        gates, scanned, h_full, based, done = (sem("z_gates"), sem("z_scanned"), sem("z_h_full"), sem("z_based"),
                                               sem("z_done"))
        chain, gchain = sem("z_vector_steps"), sem("z_gpsimd_steps")

        def col(name):
            return ins[name].rearrange("(p a) -> p a", a=1)

        def row(name):
            t = ins[name]
            return bass.AP(tensor=t.tensor, offset=t.offset, ap=[[0, P], [1, E]])

        with nc.Block() as block:
            @block.sync
            def _(sp):
                for dst, src in ((wz[:], ins["L0_attn_b_Wz"]), (wh[:], ins["L0_attn_b_Wh"]), (cols[:, 0:1], col("L0_attn_b_bz")),
                                 (cols[:, 1:2], col("L0_attn_b_bh")), (gamma[:, 0, :], row("L0_attn_b_gamma")),
                                 (gamma[:, 1, :], row("L0_attn_b_gamma")), (beta[:, 0, :], row("L0_attn_b_beta")),
                                 (beta[:, 1, :], row("L0_attn_b_beta"))):
                    sp.dma_start(dst, src).then_inc(loaded, 16)
                sp.wait_ge(loaded, 128)

            @block.vector
            def _(dve):
                dve.wait_ge(loaded, 128)
                nc.vector.tensor_scalar(cols[:, 2:3], cols[:, 0:1], -1.0, None, ALU.mult).then_inc(setup, 1)
                nc.vector.memset(stats[:], 0.0).then_inc(setup, 1)
                nc.vector.memset(half[:], -0.5).then_inc(setup, 1)

        def tile(b, t):
            return xres[:, bass.ds(2 * b + t, 1), :].rearrange("p a e -> p (a e)")

        def tiles(b):
            return xres[:, bass.ds(2 * b, 2), :].rearrange("p t e -> p (t e)")

        def flat(t):
            return t.rearrange("p t e -> p (t e)")

        def enters(i):
            return not isinstance(i, int) or i < B

        def scans(i):
            return not isinstance(i, int) or 1 <= i <= B

        def ends(i):
            return not isinstance(i, int) or i >= 2

        with nc.Block() as block:
            @block.vector
            def _(dve):
                ch = Chain(dve, chain)

                def combine_rows(b, q):
                    for k in range(2):
                        for t in range(2):
                            dve.wait_ge(arrived[4 * q + 2 * t + k], (b - q) * 8 + 16)
                            if k == 1:
                                dve.wait_ge(first_added, b * 2 + t + 1)
                            nc.vector.scalar_tensor_tensor(
                                tile(b, t), rows[:, q, t, k, :], share[:, k, bass.ds(b * 2 + t, 1)], tile(b, t), ALU.mult, ALU.add
                            ).then_inc((first_added, added)[k], 1)
                    dve.wait_ge(added, b * 2 + 2)
                    dve.sem_inc(combined, 1)

                def statistics(i, q):
                    last = None
                    if ends(i):
                        dve.wait_ge(h_full, i - 1)
                        for t in range(2):
                            last = ch.mark(nc.vector.bn_stats(stats[:, q, 2 + t, :], bh[q][:, t * P:(t + 1) * P]))
                    if enters(i):
                        combine_rows(i, q)
                        for t in range(2):
                            last = ch.mark(nc.vector.bn_stats(stats[:, q, t, :], tile(i, t)))
                    ch.wait(last)
                    moments(nc, ch, stats[:, q], mv[:, q])
                    nc.vector.tensor_scalar(arg[:, q, :], mv[:, q, 3, :], 0.25, EPS, ALU.mult, ALU.add).then_inc(ready, 1)

                def normalise(i, q):
                    if not isinstance(i, int) or i >= 2:
                        dve.wait_ge(based, i - 1)
                    for t in range(2):
                        last = nc.vector.tensor_scalar(xl[:, q, t, :], tile(i, t), mv[:, q, 0, t:t + 1], rs[:, q, t:t + 1],
                                                       ALU.subtract, ALU.mult)
                    last.then_inc(normed, 1)

                def scan(b, q):
                    dve.wait_ge(gates, b + 1)
                    ch.step(nc.vector.tensor_scalar(relu[:], bk[q][:, S:2 * S], cols[:, 1:2], 0.0, ALU.add, ALU.max))
                    ch.step(nc.vector.scalar_tensor_tensor(relu[:], sg[:, q, :], 0.5, relu[:], ALU.min, ALU.add))
                    ch.step(nc.vector.tensor_tensor(val[:], z[:, q, :], relu[:], ALU.mult))
                    nc.vector.tensor_tensor_scan(hs[:, q, :], keep[:, q, :], val[:], 0.0, ALU.mult, ALU.add).then_inc(scanned, 1)

                def finish(b, q):
                    for t in range(2):
                        last = ch.mark(nc.vector.scalar_tensor_tensor(nh[:, t, :], bh[q][:, t * P:(t + 1) * P], mv[:, q, 0, 2 + t:3 + t],
                                                                      gamma[:, t, :], ALU.subtract, ALU.mult))
                    ch.wait(last)
                    dve.wait_ge(based, b + 1)
                    for t in range(2):
                        last = nc.vector.scalar_tensor_tensor(tile(b, t), nh[:, t, :], rs[:, q, 2 + t:3 + t], tile(b, t),
                                                              ALU.mult, ALU.add)
                    last.then_inc(done, 1)

                def step(i, q):
                    statistics(i, q)
                    if scans(i):
                        scan(i - 1, 1 - q)
                    dve.wait_ge(rooted, i + 1)
                    if enters(i):
                        normalise(i, q)
                    if ends(i):
                        finish(i - 2, q)

                step(0, 0)
                step(1, 1)
                before = ch.base + ch.n
                with dve.Fori(0, B // 2 - 1) as it:
                    for q in range(2):
                        i = it * 2 + 2 + q
                        per = 15
                        ch.start((i - 2) * per + before)
                        step(i, q)
                        assert ch.n == per, ch.n
                ch.start((B - 2) * per + before)
                step(B, 0)
                step(B + 1, 1)
                dve.wait_ge(done, B)

            @block.gpsimd
            def _(pool):
                ch = Chain(pool, gchain)

                def pick(b, q):
                    if not isinstance(b, int) or b >= 2:
                        pool.wait_ge(added, b * 2 - 2)
                    pool.sem_inc(turns, 1)
                    nc.gpsimd.tensor_copy(index[:, q, :, :], slot[:, :, bass.ds(b * 2, 2)]).then_inc(picked, 1)
                    pool.wait_ge(picked, b + 1)
                    pool.sem_inc(turns, 1)

                def gather(q, t, k):
                    pool.indirect_dma_start(rows[:, q, t, k, :], None, slot_dram,
                                            bass.IndirectOffsetOnAxis(ap=index[:, q, k, t:t + 1], axis=0)
                                            ).then_inc(arrived[4 * q + 2 * t + k], 16)

                def add_to_tiles(b, q):
                    pool.wait_ge(normed, b + 1)
                    pool.sem_inc(turns, 1)
                    ch.step(nc.gpsimd.tensor_tensor(tiles(b), flat(xl[:, q, :, :]), tiles(b), ALU.add))
                    pool.wait_ge(x_full, b + 1)
                    pool.sem_inc(turns, 1)
                    nc.gpsimd.tensor_tensor(tiles(b), tiles(b), flat(beta[:]), ALU.add).then_inc(based, 1)

                def step(i, q):
                    more = not isinstance(i, int) or i + 1 < B
                    if more:
                        pick(i + 1, 1 - q)
                        gather(1 - q, 0, 0)
                        gather(1 - q, 1, 0)
                        gather(1 - q, 0, 1)
                    pool.wait_ge(ready, i + 1)
                    nc.gpsimd.tensor_tensor(rs[:, q, :], arg[:, q, :], half[:], ALU.pow).then_inc(rooted, 1)
                    if more:
                        gather(1 - q, 1, 1)
                    if enters(i):
                        add_to_tiles(i, q)

                pick(0, 0)
                for t in range(2):
                    for k in range(2):
                        gather(0, t, k)
                step(0, 0)
                step(1, 1)
                before = ch.base + ch.n
                with pool.Fori(0, B // 2 - 2) as it:
                    for q in range(2):
                        i = it * 2 + 2 + q
                        ch.start(i - 2 + before)
                        step(i, q)
                ch.start(B - 4 + before)
                for i in range(B - 2, B + 2):
                    step(i, i % 2)

            @block.tensor
            def _(pe):
                def gates_of(b, q):
                    pe.wait_ge(normed, b + 1)
                    for t in range(2):
                        last = nc.tensor.transpose(bx[q][:, t * P:(t + 1) * P], xl[:, q, t, :], ident[:])
                    last.then_inc(x_full, 1)
                    pe.wait_ge(x_taken, b + 1)
                    if not (isinstance(b, int) and b < 2):
                        pe.wait_ge(scanned, b - 1)
                    nc.tensor.matmul(bk[q][:, 0:S], wz[:], xT[:, q, :], start=True, stop=True)
                    nc.tensor.matmul(bk[q][:, S:2 * S], wh[:], xT[:, q, :], start=True, stop=True).then_inc(k_full, 1)

                def back(b, q):
                    pe.wait_ge(scanned, b + 1)
                    if not (isinstance(b, int) and b < 2):
                        pe.wait_ge(done, b - 1)
                    for t in range(2):
                        last = nc.tensor.transpose(bh[q][:, t * P:(t + 1) * P], hs[:, q, t * P:(t + 1) * P], ident[:])
                    last.then_inc(h_full, 1)

                gates_of(0, 0)
                back(0, 0)
                gates_of(1, 1)
                with pe.Fori(0, B // 2 - 1) as it:
                    for q in range(2):
                        i = it * 2 + 2 + q
                        back(i - 1, 1 - q)
                        gates_of(i, q)
                back(B - 1, 1)

            @block.scalar
            def _(act):
                def chunk(b, q):
                    act.wait_ge(x_full, b + 1)
                    if not (isinstance(b, int) and b < 2):
                        act.wait_ge(scanned, b - 1)
                    nc.scalar.copy(xT[:, q, :], bx[q][:, 0:2 * P]).then_inc(x_taken, 1)
                    act.wait_ge(k_full, b + 1)
                    nc.scalar.activation(z[:, q, :], bk[q][:, 0:S], ACT.Sigmoid, bias=cols[:, 0:1])
                    nc.scalar.activation(keep[:, q, :], bk[q][:, 0:S], ACT.Sigmoid, bias=cols[:, 2:3], scale=-1.0)
                    nc.scalar.activation(sg[:, q, :], bk[q][:, S:2 * S], ACT.Sigmoid, bias=cols[:, 1:2]).then_inc(gates, 1)

                chunk(0, 0)
                chunk(1, 1)
                with act.Fori(1, B // 2) as it:
                    chunk(it * 2, 0)
                    chunk(it * 2 + 1, 1)


_INS = ["L0_attn_a_x", "L0_attn_a_rel_pos", "L0_attn_a_in_proj_w", "L0_attn_a_in_proj_b", "L0_attn_a_out_w",
        "L0_attn_a_out_b", "L0_attn_a_w1", "L0_attn_a_b1", "L0_attn_a_w2", "L0_attn_a_b2", "L0_attn_a_ln1_g",
        "L0_attn_a_ln1_b", "L0_attn_a_ln2_g", "L0_attn_a_ln2_b", "L0_attn_b_Wz", "L0_attn_b_bz", "L0_attn_b_Wh",
        "L0_attn_b_bh", "L0_attn_b_gamma", "L0_attn_b_beta", "L0_ffn_router_w", "L0_ffn_gate_w", "L0_ffn_gate_b",
        "L0_ffn_up_w", "L0_ffn_up_b", "L0_ffn_down_w", "L0_ffn_down_b"]


def kernel(**inputs):
    import numpy as _np
    import concourse.bacc as _bacc
    from concourse import mybir as _mybir
    from concourse.bass_utils import run_bass_kernel_spmd as _run

    nc = _bacc.Bacc("TRN2", target_bir_lowering=False, num_devices=1)
    arrays, args = {}, {}
    for name in _INS:
        a = _np.ascontiguousarray(inputs[name])
        arrays[f"in_{name}"] = a
        args[name] = nc.dram_tensor(f"in_{name}", a.shape, _mybir.dt.from_np(a.dtype), kind="ExternalInput").ap()
    shape = inputs["L0_attn_a_x"].shape
    out = nc.dram_tensor("out", shape, _mybir.dt.float32, kind="ExternalOutput").ap()
    build(nc, args, out)
    r = _run(nc, [arrays], core_ids=[0])
    return r.results[0]["out"]
```
